# Optimizing a Trainium2 kernel written in Bass

```python
import numpy as np
import jax
import jax.numpy as jnp

def _softmax(x, axis=-1):
    return jax.nn.softmax(x, axis=axis)

def _gelu(x):
    return jax.nn.gelu(x, approximate=True)

def _silu(x):
    return jax.nn.silu(x)

def _sigmoid(x):
    return jax.nn.sigmoid(x)

def _layernorm(x, axis=-1, eps=1e-05):
    m = jnp.mean(x, axis=axis, keepdims=True)
    v = jnp.var(x, axis=axis, keepdims=True)
    return (x - m) / jnp.sqrt(v + eps)

def _scatter_add(tgt, idx, src, axis=0):
    return tgt.at[idx].add(src)

def _segment_sum(src, seg, n):
    return jax.ops.segment_sum(src, seg, n)
kernel_name = 'mk_conv_attn_hybrid_d4_conv_nchw512_r4_b388df'

def setup_inputs(seed: int=0):
    np.random.seed(seed)
    _w = jnp.asarray

    def _rec_inputs():
        import jax
        import jax.numpy as jnp
        _gk = jax.random.key(seed)
        x = -0.000125 + 0.9999 * jax.random.normal(jax.random.fold_in(_gk, 1), (16, 128, 16, 16), jnp.float32)
        return x
    x = _rec_inputs()

    def _L0_conv_setup():
        import jax, jax.numpy as jnp
        import numpy as np
        C_IN = 128
        C2 = C_IN // 2
        key = jax.random.key(seed)
        k = jax.random.split(key, 6)
        B, C, H, W = (16, C_IN, 16, 16)
        s = 1.0 / np.sqrt(C)
        s2 = 1.0 / np.sqrt(C2)
        return {'x': jax.random.normal(k[0], (B, C, H, W), dtype=jnp.float32), 'wq_r': jax.random.normal(k[1], (C,), dtype=jnp.float32) * s, 'wv_r': jax.random.normal(k[2], (C2, C), dtype=jnp.float32) * s, 'w_up': jax.random.normal(k[3], (C, C2), dtype=jnp.float32) * s2, 'wq_l': jax.random.normal(k[4], (C2, C), dtype=jnp.float32) * s, 'wv_l': jax.random.normal(k[5], (C2, C), dtype=jnp.float32) * s}
    _L0_conv_all = _L0_conv_setup()
    _L0_conv_in = {k: v for k, v in _L0_conv_all.items() if k in ('wq_r', 'wv_r', 'w_up', 'wq_l', 'wv_l')}
    del _L0_conv_all

    def _L1_conv_setup():
        import jax, jax.numpy as jnp
        import numpy as np
        HEADS = 8
        D = 16
        key = jax.random.key(seed)
        ks = jax.random.split(key, 5)
        bs, cin, h, w = (8, 128, 32, 32)
        x = jax.random.normal(ks[0], (bs, cin, h, w), dtype=jnp.float32)
        W_fc = jax.random.normal(ks[1], (HEADS * D * 3, cin), dtype=jnp.float32) * cin ** (-0.5)
        b_fc = jax.random.normal(ks[2], (HEADS * D * 3,), dtype=jnp.float32) * 0.01
        W_last = jax.random.normal(ks[3], (cin, HEADS * D), dtype=jnp.float32) * (HEADS * D) ** (-0.5)
        b_last = jax.random.normal(ks[4], (cin,), dtype=jnp.float32) * 0.01
        return {'x': x, 'W_fc': W_fc, 'b_fc': b_fc, 'W_last': W_last, 'b_last': b_last}
    _L1_conv_all = _L1_conv_setup()
    _L1_conv_in = {k: v for k, v in _L1_conv_all.items() if k in ('W_fc', 'b_fc', 'W_last', 'b_last')}
    del _L1_conv_all

    def _L2_attn_setup():
        import jax, jax.numpy as jnp
        import numpy as np
        NHEAD = 8
        WINDOW = 64

        def _sliding_window_attention(q, k, v, w):
            B, H, S, D = q.shape
            assert S % w == 0
            nb = S // w
            qb = q.reshape(B, H, nb, w, D)
            kb = k.reshape(B, H, nb, w, D)
            vb = v.reshape(B, H, nb, w, D)
            k_prev = jnp.pad(kb, ((0, 0), (0, 0), (1, 0), (0, 0), (0, 0)))[:, :, :nb]
            v_prev = jnp.pad(vb, ((0, 0), (0, 0), (1, 0), (0, 0), (0, 0)))[:, :, :nb]
            k2 = jnp.concatenate([k_prev, kb], axis=3)
            v2 = jnp.concatenate([v_prev, vb], axis=3)
            scores = jnp.einsum('bhnqd,bhnkd->bhnqk', qb, k2) / jnp.sqrt(jnp.asarray(D, q.dtype))
            qi = jnp.arange(w)[:, None]
            ki = jnp.arange(2 * w)[None, :]
            valid = (ki >= qi + 1) & (ki <= qi + w)
            n_idx = jnp.arange(nb)[:, None, None]
            valid = valid[None] & ((n_idx > 0) | (ki[None] >= w))
            neg = jnp.asarray(-1e+30, scores.dtype)
            scores = jnp.where(valid[None, None], scores, neg)
            attn = jax.nn.softmax(scores, axis=-1)
            out = jnp.einsum('bhnqk,bhnkd->bhnqd', attn, v2)
            return out.reshape(B, H, S, D)
        key = jax.random.key(seed)
        ks = jax.random.split(key, 5)
        B, S, Dm = (2, 2048, 128)
        x = jax.random.normal(ks[0], (B, S, Dm), jnp.float32)
        w_scale = 0.02
        Wq = jax.random.normal(ks[1], (Dm, Dm), jnp.float32) * w_scale
        Wk = jax.random.normal(ks[2], (Dm, Dm), jnp.float32) * w_scale
        Wv = jax.random.normal(ks[3], (Dm, Dm), jnp.float32) * w_scale
        Wo = jax.random.normal(ks[4], (Dm, Dm), jnp.float32) * w_scale
        return {'x': x, 'Wq': Wq, 'Wk': Wk, 'Wv': Wv, 'Wo': Wo}
    _L2_attn_all = _L2_attn_setup()
    _L2_attn_in = {k: v for k, v in _L2_attn_all.items() if k in ('Wq', 'Wk', 'Wv', 'Wo')}
    del _L2_attn_all

    def _L2_ffn_setup():
        import jax, jax.numpy as jnp
        import numpy as np
        TOP_K = 2
        key = jax.random.key(seed)
        k1, k2, k3, k4 = jax.random.split(key, 4)
        B, S, D, F, E = (4, 128, 128, 512, 16)
        hidden_states = jax.random.normal(k1, (B, S, D), dtype=jnp.float32)
        gate_weight = jax.random.normal(k2, (E, D), dtype=jnp.float32) * 0.02
        w1 = jax.random.normal(k3, (E, F, D), dtype=jnp.float32) * 0.02
        w2 = jax.random.normal(k4, (E, D, F), dtype=jnp.float32) * 0.02
        return {'hidden_states': hidden_states, 'gate_weight': gate_weight, 'w1': w1, 'w2': w2}
    _L2_ffn_all = _L2_ffn_setup()
    _L2_ffn_in = {k: v for k, v in _L2_ffn_all.items() if k in ('gate_weight', 'w1', 'w2')}
    del _L2_ffn_all

    def _L3_attn_setup():
        import jax, jax.numpy as jnp
        import numpy as np
        B, N, DIM, H, DH = (2, 512, 128, 8, 16)
        EPS = 0.001

        def causal_linear_attn(q, k, v, eps=EPS):
            q = jax.nn.relu(q) + eps
            k = jax.nn.relu(k) + eps
            k_cum = jnp.cumsum(k, axis=2)
            ctx = jnp.cumsum(k[..., :, None] * v[..., None, :], axis=2)
            d_inv = 1.0 / jnp.einsum('bhnd,bhnd->bhn', q, k_cum)
            return jnp.einsum('bhnd,bhnde,bhn->bhne', q, ctx, d_inv)
        key = jax.random.key(seed)
        k0, k1, k2, k3, k4 = jax.random.split(key, 5)
        s_in = 1.0 / np.sqrt(DIM)
        s_out = 1.0 / np.sqrt(H * DH)
        return {'x': jax.random.normal(k0, (B, N, DIM), jnp.float32), 'Wq': jax.random.normal(k1, (DIM, H * DH), jnp.float32) * s_in, 'Wk': jax.random.normal(k2, (DIM, H * DH), jnp.float32) * s_in, 'Wv': jax.random.normal(k3, (DIM, H * DH), jnp.float32) * s_in, 'Wo': jax.random.normal(k4, (H * DH, DIM), jnp.float32) * s_out, 'bo': jnp.zeros((DIM,), jnp.float32)}
    _L3_attn_all = _L3_attn_setup()
    _L3_attn_in = {k: v for k, v in _L3_attn_all.items() if k in ('Wq', 'Wk', 'Wv', 'Wo', 'bo')}
    del _L3_attn_all

    def _L3_ffn_setup():
        import jax, jax.numpy as jnp
        import numpy as np
        B, S, D, F, E = (4, 512, 128, 512, 8)
        key = jax.random.key(seed)
        k = jax.random.split(key, 5)
        x = jax.random.normal(k[0], (B, S, D), dtype=jnp.float32)
        Ws = jax.random.normal(k[1], (D, E), dtype=jnp.float32) * 0.02
        bs = jnp.zeros((E,), dtype=jnp.float32)
        W1 = jax.random.normal(k[2], (E, D, F), dtype=jnp.float32) * 0.02
        b1 = jnp.zeros((E, F), dtype=jnp.float32)
        W2 = jax.random.normal(k[3], (E, F, D), dtype=jnp.float32) * 0.02
        b2 = jnp.zeros((E, D), dtype=jnp.float32)
        return {'x': x, 'Ws': Ws, 'bs': bs, 'W1': W1, 'b1': b1, 'W2': W2, 'b2': b2}
    _L3_ffn_all = _L3_ffn_setup()
    _L3_ffn_in = {k: v for k, v in _L3_ffn_all.items() if k in ('Ws', 'bs', 'W1', 'b1', 'W2', 'b2')}
    del _L3_ffn_all
    return {'x': x, 'L0_conv_wq_r': _L0_conv_in['wq_r'], 'L0_conv_wv_r': _L0_conv_in['wv_r'], 'L0_conv_w_up': _L0_conv_in['w_up'], 'L0_conv_wq_l': _L0_conv_in['wq_l'], 'L0_conv_wv_l': _L0_conv_in['wv_l'], 'L1_conv_W_fc': _L1_conv_in['W_fc'], 'L1_conv_b_fc': _L1_conv_in['b_fc'], 'L1_conv_W_last': _L1_conv_in['W_last'], 'L1_conv_b_last': _L1_conv_in['b_last'], 'L2_attn_Wq': _L2_attn_in['Wq'], 'L2_attn_Wk': _L2_attn_in['Wk'], 'L2_attn_Wv': _L2_attn_in['Wv'], 'L2_attn_Wo': _L2_attn_in['Wo'], 'L2_ffn_gate_weight': _L2_ffn_in['gate_weight'], 'L2_ffn_w1': _L2_ffn_in['w1'], 'L2_ffn_w2': _L2_ffn_in['w2'], 'L3_attn_Wq': _L3_attn_in['Wq'], 'L3_attn_Wk': _L3_attn_in['Wk'], 'L3_attn_Wv': _L3_attn_in['Wv'], 'L3_attn_Wo': _L3_attn_in['Wo'], 'L3_attn_bo': _L3_attn_in['bo'], 'L3_ffn_Ws': _L3_ffn_in['Ws'], 'L3_ffn_bs': _L3_ffn_in['bs'], 'L3_ffn_W1': _L3_ffn_in['W1'], 'L3_ffn_b1': _L3_ffn_in['b1'], 'L3_ffn_W2': _L3_ffn_in['W2'], 'L3_ffn_b2': _L3_ffn_in['b2']}

def reference(x, L0_conv_wq_r, L0_conv_wv_r, L0_conv_w_up, L0_conv_wq_l, L0_conv_wv_l, L1_conv_W_fc, L1_conv_b_fc, L1_conv_W_last, L1_conv_b_last, L2_attn_Wq, L2_attn_Wk, L2_attn_Wv, L2_attn_Wo, L2_ffn_gate_weight, L2_ffn_w1, L2_ffn_w2, L3_attn_Wq, L3_attn_Wk, L3_attn_Wv, L3_attn_Wo, L3_attn_bo, L3_ffn_Ws, L3_ffn_bs, L3_ffn_W1, L3_ffn_b1, L3_ffn_W2, L3_ffn_b2):
    import jax
    import jax.numpy as jnp

    def _L0_conv_ref(x, wq_r, wv_r, w_up, wq_l, wv_l):
        import jax, jax.numpy as jnp
        import numpy as np
        C_IN = 128
        C2 = C_IN // 2
        B, C, H, W = x.shape
        HW = H * W
        xf = x.reshape(B, C, HW)
        ch_wv = jnp.einsum('kc,bcn->bkn', wv_r, xf)
        ch_wq = jnp.einsum('c,bcn->bn', wq_r, xf)
        p = jax.nn.softmax(ch_wq, axis=-1)
        ch_wz = jnp.einsum('bkn,bn->bk', ch_wv, p)
        ch_weight = jax.nn.sigmoid(jnp.einsum('ck,bk->bc', w_up, ch_wz))
        ch_out = xf * ch_weight[:, :, None]
        sp_wv = jnp.einsum('kc,bcn->bkn', wv_l, ch_out)
        sp_wq = jnp.einsum('kc,bcn->bk', wq_l, ch_out) / HW
        q = jax.nn.softmax(sp_wq, axis=-1)
        wz_hw = jnp.einsum('bk,bkn->bn', q, sp_wv)
        out = ch_out * jax.nn.sigmoid(wz_hw)[:, None, :]
        return out.reshape(B, C, H, W)

    def _L1_conv_ref(x, W_fc, b_fc, W_last, b_last):
        import jax, jax.numpy as jnp
        import numpy as np
        HEADS = 8
        D = 16
        bs, cin, h, w = x.shape
        n = h * w
        scale = D ** (-0.5)
        xt = x.reshape(bs, cin, n).transpose(0, 2, 1)
        qkv = (xt @ W_fc.T + b_fc).reshape(bs, n, HEADS, 3 * D)
        q, k, v = jnp.split(qkv, 3, axis=-1)
        attn = jnp.einsum('bihd,bjhd->bijh', q, k) * scale
        attn = jax.nn.softmax(attn, axis=2)
        out = jnp.einsum('bijh,bjhd->bihd', attn, v).reshape(bs, n, HEADS * D)
        out = out @ W_last.T + b_last + xt
        return out.transpose(0, 2, 1).reshape(bs, cin, h, w)

    def _L2_attn_ref(x, Wq, Wk, Wv, Wo):
        import jax, jax.numpy as jnp
        import numpy as np
        NHEAD = 8
        WINDOW = 64

        def _sliding_window_attention(q, k, v, w):
            B, H, S, D = q.shape
            assert S % w == 0
            nb = S // w
            qb = q.reshape(B, H, nb, w, D)
            kb = k.reshape(B, H, nb, w, D)
            vb = v.reshape(B, H, nb, w, D)
            k_prev = jnp.pad(kb, ((0, 0), (0, 0), (1, 0), (0, 0), (0, 0)))[:, :, :nb]
            v_prev = jnp.pad(vb, ((0, 0), (0, 0), (1, 0), (0, 0), (0, 0)))[:, :, :nb]
            k2 = jnp.concatenate([k_prev, kb], axis=3)
            v2 = jnp.concatenate([v_prev, vb], axis=3)
            scores = jnp.einsum('bhnqd,bhnkd->bhnqk', qb, k2) / jnp.sqrt(jnp.asarray(D, q.dtype))
            qi = jnp.arange(w)[:, None]
            ki = jnp.arange(2 * w)[None, :]
            valid = (ki >= qi + 1) & (ki <= qi + w)
            n_idx = jnp.arange(nb)[:, None, None]
            valid = valid[None] & ((n_idx > 0) | (ki[None] >= w))
            neg = jnp.asarray(-1e+30, scores.dtype)
            scores = jnp.where(valid[None, None], scores, neg)
            attn = jax.nn.softmax(scores, axis=-1)
            out = jnp.einsum('bhnqk,bhnkd->bhnqd', attn, v2)
            return out.reshape(B, H, S, D)
        B, S, Dm = x.shape
        hd = Dm // NHEAD
        q = (x @ Wq.T).reshape(B, S, NHEAD, hd).transpose(0, 2, 1, 3)
        k = (x @ Wk.T).reshape(B, S, NHEAD, hd).transpose(0, 2, 1, 3)
        v = (x @ Wv.T).reshape(B, S, NHEAD, hd).transpose(0, 2, 1, 3)
        attn = _sliding_window_attention(q, k, v, WINDOW)
        attn = attn.transpose(0, 2, 1, 3).reshape(B, S, Dm)
        return attn @ Wo.T

    def _L2_ffn_ref(hidden_states, gate_weight, w1, w2):
        import jax, jax.numpy as jnp
        import numpy as np
        TOP_K = 2
        B, S, D = hidden_states.shape
        E = gate_weight.shape[0]
        x = hidden_states.reshape(-1, D)
        gate_logits = x @ gate_weight.T
        top_vals, top_idx = jax.lax.top_k(gate_logits, TOP_K)
        routing_w = jax.nn.softmax(top_vals, axis=-1)
        mask = jnp.any(top_idx[:, :, None] == jnp.arange(E)[None, None, :], axis=1)
        h = jax.nn.silu(jnp.einsum('td,efd->tef', x, w1))
        counts = jnp.sum(mask, axis=0)
        h_sum = jnp.einsum('tef,te->ef', h, mask.astype(h.dtype))
        h_mean = h_sum / jnp.maximum(counts, 1)[:, None].astype(h.dtype)
        y_mean = jnp.einsum('ef,edf->ed', h_mean, w2)
        y_mean = jnp.where((counts > 0)[:, None], y_mean, 0.0)
        out = jnp.einsum('tk,tkd->td', routing_w, y_mean[top_idx])
        return out.reshape(B, S, D)

    def _L3_attn_ref(x, Wq, Wk, Wv, Wo, bo):
        import jax, jax.numpy as jnp
        import numpy as np
        B, N, DIM, H, DH = (2, 512, 128, 8, 16)
        EPS = 0.001

        def causal_linear_attn(q, k, v, eps=EPS):
            q = jax.nn.relu(q) + eps
            k = jax.nn.relu(k) + eps
            k_cum = jnp.cumsum(k, axis=2)
            ctx = jnp.cumsum(k[..., :, None] * v[..., None, :], axis=2)
            d_inv = 1.0 / jnp.einsum('bhnd,bhnd->bhn', q, k_cum)
            return jnp.einsum('bhnd,bhnde,bhn->bhne', q, ctx, d_inv)
        b, n, _ = x.shape
        split = lambda t: t.reshape(b, n, H, DH).transpose(0, 2, 1, 3)
        q = split(x @ Wq)
        k = split(x @ Wk)
        v = split(x @ Wv)
        out = causal_linear_attn(q, k, v)
        out = out.transpose(0, 2, 1, 3).reshape(b, n, H * DH)
        return out @ Wo + bo

    def _L3_ffn_ref(x, Ws, bs, W1, b1, W2, b2):
        import jax, jax.numpy as jnp
        import numpy as np
        B, S, D, F, E = (4, 512, 128, 512, 8)
        Bb, Ss, Dd = x.shape
        xt = x.reshape(-1, Dd)
        logits = xt @ Ws + bs
        probs = jax.nn.softmax(logits, axis=-1)
        prob_max = jnp.max(probs, axis=-1)
        routes = jnp.argmax(probs, axis=-1)
        onehot = jax.nn.one_hot(routes, W1.shape[0], dtype=xt.dtype)

        def expert_ffn(w1, bb1, w2, bb2):
            h = jax.nn.gelu(xt @ w1 + bb1, approximate=False)
            return h @ w2 + bb2
        y = jax.vmap(expert_ffn)(W1, b1, W2, b2)
        out = jnp.einsum('te,etd->td', onehot, y)
        out = out * prob_max[:, None]
        return out.reshape(Bb, Ss, Dd)

    def _gn(v, G=32, eps=1e-05):
        B_, C_, H_, W_ = v.shape
        g = v.reshape(B_, G, C_ // G, H_, W_)
        m = jnp.mean(g, axis=(2, 3, 4), keepdims=True)
        s = jnp.var(g, axis=(2, 3, 4), keepdims=True)
        return ((g - m) / jnp.sqrt(s + eps)).reshape(v.shape)

    def _ln_c(v, eps=1e-06):
        m = jnp.mean(v, axis=1, keepdims=True)
        s = jnp.var(v, axis=1, keepdims=True)
        return (v - m) / jnp.sqrt(s + eps)

    def _ln_t(v, eps=1e-05):
        m = jnp.mean(v, axis=-1, keepdims=True)
        s = jnp.var(v, axis=-1, keepdims=True)
        return (v - m) / jnp.sqrt(s + eps)

    def _to_tokens(v):
        B_, C_, H_, W_ = v.shape
        return v.reshape(B_, C_, H_ * W_).transpose(0, 2, 1)

    def _from_tokens(t, like):
        B_, C_, H_, W_ = like.shape
        return t.transpose(0, 2, 1).reshape(B_, C_, H_, W_)
    x = x + _L0_conv_ref(_gn(x), L0_conv_wq_r, L0_conv_wv_r, L0_conv_w_up, L0_conv_wq_l, L0_conv_wv_l)
    x = _L1_conv_ref(x, L1_conv_W_fc, L1_conv_b_fc, L1_conv_W_last, L1_conv_b_last)
    t = _to_tokens(x)
    t = t + _L2_attn_ref(_ln_t(t), L2_attn_Wq, L2_attn_Wk, L2_attn_Wv, L2_attn_Wo)
    t = t + _L2_ffn_ref(_ln_t(t), L2_ffn_gate_weight, L2_ffn_w1, L2_ffn_w2)
    t = t + _L3_attn_ref(_ln_t(t), L3_attn_Wq, L3_attn_Wk, L3_attn_Wv, L3_attn_Wo, L3_attn_bo)
    t = t + _L3_ffn_ref(_ln_t(t), L3_ffn_Ws, L3_ffn_bs, L3_ffn_W1, L3_ffn_b1, L3_ffn_W2, L3_ffn_b2)
    x = _from_tokens(t, x)
    return x

_drawn_inputs = setup_inputs


def setup_inputs(seed=0):
    import zlib

    import numpy as np

    out = dict(_drawn_inputs(seed))
    spreads = {'L3_attn_bo': (0.0, 0.1),
     'L3_ffn_bs': (0.0, 0.627),
     'L3_ffn_b1': (0.0, 0.8),
     'L3_ffn_b2': (0.0, 0.582)}
    factors = {'L0_conv_wq_r': 4.687,
     'L0_conv_wv_r': 3.778,
     'L0_conv_w_up': 3.858,
     'L0_conv_wq_l': 8.0,
     'L0_conv_wv_l': 6.056,
     'L1_conv_b_fc': 4.236,
     'L1_conv_b_last': 5.141,
     'L2_attn_Wq': 8.0,
     'L2_attn_Wk': 8.0,
     'L2_attn_Wv': 5.613,
     'L2_attn_Wo': 5.649,
     'L2_ffn_gate_weight': 8.0,
     'L2_ffn_w1': 8.0,
     'L2_ffn_w2': 8.0,
     'L3_ffn_Ws': 3.823,
     'L3_ffn_W1': 7.556,
     'L3_ffn_W2': 6.833}
    for name, (base, spread) in spreads.items():
        noise = np.random.default_rng([zlib.crc32(name.encode()), seed]).standard_normal(out[name].shape)
        drawn = base * np.exp(spread * noise) if base else spread * noise
        out[name] = jnp.asarray(drawn.astype(out[name].dtype))
    for name, factor in factors.items():
        out[name] = (out[name] * factor).astype(out[name].dtype)
    return out
```

```python
import concourse.bass as bass
from concourse import mybir
from contextlib import ExitStack, contextmanager

FP32 = mybir.dt.float32
FP32R = mybir.dt.float32r
BF16 = mybir.dt.bfloat16
INT32 = mybir.dt.int32
UINT32 = mybir.dt.uint32
ALU = mybir.AluOpType
ACT = mybir.ActivationFunctionType
AX = mybir.AxisListType

C = 128
IMAGES, N = 16, 256
TOKENS = IMAGES * N
TILES = TOKENS // 128
H, D = 8, 16
WINDOW = 64
GROUP = 4
C2 = C // 2
F = 512
FC = F // 128
E2, K2 = 16, 2
E3, K3 = 8, 1
GN_EPS, LN_EPS, LINEAR_EPS = 1e-5, 1e-5, 0.001
MASKED = -1e30


def slot_tiles(experts, taken):
    most = (TOKENS * taken + experts * 127) // 128
    return most + most % 2


S2, S3 = slot_tiles(E2, K2), slot_tiles(E3, K3)


@contextmanager
def stage(nc, name):
    taken = []
    with ExitStack() as ctx:
        def sb(n, shape, dt=FP32):
            return ctx.enter_context(nc.sbuf_tensor(f"{name}_{n}", shape, dt))

        def sem(n):
            taken.append(ctx.enter_context(nc.semaphore(f"{name}_{n}")))
            return taken[-1]

        yield sb, sem
        with nc.Block() as block:
            @block.gpsimd
            def _(pool):
                for s in taken:
                    pool.sem_clear(s)


def link_on(engine, sem):
    count = [0]

    def link(instruction):
        count[0] += 1
        instruction.then_inc(sem, 1)
        engine.wait_ge(sem, count[0])
    return link


def spatial_gate(nc, x_dram, w, xf, tokens, consts, ps):
    with stage(nc, "gate") as (sb, sem):

        x = sb("x", [128, IMAGES, N])
        xn = sb("xn", [128, IMAGES, N])
        stats = sb("stats", [128, IMAGES, 6])
        small = sb("small", [128, 12, IMAGES])
        mean, dev, square, spread, rstd, peak, total, pooled, gate, summed, vw, halves = (
            small[:, i, :] for i in range(12))
        group_mean = sb("group_mean", [128, IMAGES])
        prob = sb("prob", [128, 2, 2, N])
        weighted = sb("weighted", [128, 2, 2, N])
        wq_wide = sb("wq_wide", [128, 128])
        v_wide = sb("v_wide", [128, 4, 128])
        turned = sb("turned", [128, 3, 128])
        squeezed = sb("squeezed", [C2, IMAGES])
        q_small = sb("q_small", [IMAGES, C2])
        q_exp = sb("q_exp", [IMAGES, C2])
        q_one = sb("q_one", [IMAGES, 3])
        qT = sb("qT", [C2, IMAGES])
        place = sb("place", [128, 2, 2, N])
        gated = sb("gated", [128, 2, 2, N])
        out = sb("out", [128, 2, 2 * N])

        x_in = [sem(f"x_in{i}") for i in range(4)]
        weights_turned = sem("weights_turned")
        weights_ready = sem("weights_ready")
        stats_ready = sem("stats_ready")
        mean_ready = sem("mean_ready")
        grouped = sem("grouped")
        spread_ready = sem("spread_ready")
        var_ready = sem("var_ready")
        std_ready = sem("std_ready")
        xn_ready = sem("xn_ready")
        logits_ready = sem("logits_ready")
        peak_ready = sem("peak_ready")
        prob_ready = sem("prob_ready")
        weighted_ready = sem("weighted_ready")
        pooled_part = sem("pooled_part")
        pooled_ready = sem("pooled_ready")
        small_on_pe = sem("small_on_pe")
        small_on_dve = sem("small_on_dve")
        small_on_act = sem("small_on_act")
        wide_ready = sem("wide_ready")
        place_on_pe = sem("place_on_pe")
        place_ready = sem("place_ready")
        gated_ready = sem("gated_ready")
        out_ready = sem("out_ready")
        xf_ready = sem("xf_ready")
        out_turned = sem("out_turned")
        tokens_ready = sem("tokens_ready")
        chained = sem("chained")

        with nc.Block() as block:
            @block.sync
            def _(sp):
                for i in range(4):
                    sp.dma_start(x[:, 4 * i:4 * i + 4, :],
                                 x_dram[4 * i:4 * i + 4].rearrange("b c h w -> c b (h w)")).then_inc(x_in[i], 16)

            @block.tensor
            def _(pe):
                for i, name in enumerate(("wv_r", "w_up", "wq_l")):
                    rows, cols = w[name].shape
                    mm = nc.tensor.transpose(ps[0:cols, 7, i * 128:i * 128 + rows], w[name][:, :],
                                             consts["ident"][0:rows, 0:rows])
                mm.then_inc(weights_turned, 1)
                pe.wait_ge(mean_ready, 1)
                nc.tensor.matmul(ps[:, 0, 0:IMAGES], consts["group"][:], mean, start=True,
                                 stop=True).then_inc(grouped, 1)
                pe.wait_ge(spread_ready, 1)
                nc.tensor.matmul(ps[:, 0, 0:IMAGES], consts["group"][:], spread, start=True,
                                 stop=True).then_inc(grouped, 1)
                pe.wait_ge(weights_ready, 2)
                for m in range(IMAGES // 2):
                    pe.wait_ge(xn_ready, 2 * m + 2)
                    if m >= 2:
                        pe.wait_ge(prob_ready, m - 1)
                    nc.tensor.matmul(ps[:, 1 + m % 2, :], wq_wide[:],
                                     xn[:, 2 * m:2 * m + 2, :].rearrange("p b n -> p (b n)"),
                                     start=True, stop=True).then_inc(logits_ready, 1)
                pe.wait_ge(pooled_ready, 1)
                nc.tensor.matmul(ps[0:C2, 0, 0:IMAGES], turned[:, 0, 0:C2], pooled, start=True,
                                 stop=True).then_inc(small_on_pe, 1)
                pe.wait_ge(small_on_dve, 1)
                nc.tensor.matmul(ps[:, 0, 32:32 + IMAGES], turned[0:C2, 1, :], squeezed[:], start=True,
                                 stop=True).then_inc(small_on_pe, 1)
                pe.wait_ge(small_on_dve, 2)
                nc.tensor.matmul(ps[0:IMAGES, 3, 0:C2], summed, turned[:, 2, 0:C2], start=True,
                                 stop=True).then_inc(small_on_pe, 1)
                pe.wait_ge(small_on_dve, 4)
                nc.tensor.transpose(ps[0:C2, 4, 0:IMAGES], q_small[:], consts["ident"][0:IMAGES, 0:IMAGES])\
                    .then_inc(small_on_pe, 1)
                pe.wait_ge(small_on_dve, 5)
                nc.tensor.matmul(ps[:, 3, 0:IMAGES], w["wv_l"][:, :], qT[:], start=True,
                                 stop=True).then_inc(small_on_pe, 1)

                def turn_out(m):
                    pe.wait_ge(out_ready, m + 1)
                    if m >= 2:
                        pe.wait_ge(tokens_ready, m - 1)
                    for a in range(4):
                        mm = nc.tensor.transpose(ps[:, 5 + m % 2, a * 128:(a + 1) * 128],
                                                 out[:, m % 2, a * 128:(a + 1) * 128], consts["ident"][:])
                    mm.then_inc(out_turned, 1)

                for m in range(IMAGES // 2):
                    pe.wait_ge(wide_ready, 2 * m + 2)
                    if m >= 2:
                        pe.wait_ge(place_ready, m - 1)
                    for a in range(2):
                        b = 2 * m + a
                        mm = nc.tensor.matmul(ps[:, 1 + m % 2, a * N:(a + 1) * N], v_wide[:, b % 4, :], xn[:, b, :],
                                              start=True, stop=True)
                    mm.then_inc(place_on_pe, 1)
                    if m >= 1:
                        turn_out(m - 1)
                turn_out(IMAGES // 2 - 1)

            @block.scalar
            def _(act):
                act.wait_ge(var_ready, 1)
                nc.scalar.activation(square, dev, ACT.Sqrt).then_inc(std_ready, 1)
                for m in range(IMAGES // 2):
                    act.wait_ge(peak_ready, m + 1)
                    if m >= 2:
                        act.wait_ge(weighted_ready, m - 1)
                    for a in range(2):
                        b = 2 * m + a
                        last = nc.scalar.activation(prob[:, m % 2, a, :], ps[:, 1 + m % 2, a * N:(a + 1) * N], ACT.Exp,
                                                    bias=peak[:, b:b + 1], accum_out=total[:, b:b + 1])
                    last.then_inc(prob_ready, 1)
                act.wait_ge(small_on_pe, 2)
                nc.scalar.activation(gate, ps[:, 0, 32:32 + IMAGES], ACT.Sigmoid).then_inc(small_on_act, 1)
                act.wait_ge(small_on_dve, 3)
                nc.scalar.activation(q_exp[:], ps[0:IMAGES, 3, 0:C2], ACT.Exp, bias=q_one[:, 0:1],
                                     accum_out=q_one[:, 1:2]).then_inc(small_on_act, 1)
                for m in range(IMAGES // 2):
                    act.wait_ge(place_on_pe, m + 1)
                    if m >= 2:
                        act.wait_ge(gated_ready, m - 1)
                    nc.scalar.activation(place[:, m % 2].rearrange("p a n -> p (a n)"), ps[:, 1 + m % 2, :],
                                         ACT.Sigmoid).then_inc(place_ready, 1)
                    act.wait_ge(out_ready, m + 1)
                    nc.scalar.activation(xf[:, 2 * m * N:(2 * m + 2) * N], out[:, m % 2, :],
                                         ACT.Copy).then_inc(xf_ready, 1)
                    if m >= 1:
                        act.wait_ge(out_turned, m)
                        nc.scalar.activation(tokens[:, 4 * m - 4:4 * m, :].rearrange("p a c -> p (a c)"),
                                             ps[:, 5 + (m - 1) % 2, :], ACT.Copy).then_inc(tokens_ready, 1)
                m = IMAGES // 2
                act.wait_ge(out_turned, m)
                nc.scalar.activation(tokens[:, 4 * m - 4:4 * m, :].rearrange("p a c -> p (a c)"),
                                     ps[:, 5 + (m - 1) % 2, :], ACT.Copy).then_inc(tokens_ready, 1)

            @block.gpsimd
            def _(pool):
                for m in range(IMAGES // 2):
                    pool.wait_ge(prob_ready, m + 1)
                    if m >= 2:
                        pool.wait_ge(pooled_part, m - 1)
                    nc.gpsimd.tensor_tensor(weighted[:, m % 2], prob[:, m % 2], xn[:, 2 * m:2 * m + 2, :],
                                            ALU.mult).then_inc(weighted_ready, 1)
                for m in range(IMAGES // 2):
                    pool.wait_ge(gated_ready, m + 1)
                    if m >= 2:
                        pool.wait_ge(xf_ready, m - 1)
                        pool.wait_ge(out_turned, m - 1)
                    nc.gpsimd.tensor_tensor(out[:, m % 2, :], gated[:, m % 2].rearrange("p a n -> p (a n)"),
                                            x[:, 2 * m:2 * m + 2, :].rearrange("p b n -> p (b n)"),
                                            ALU.add).then_inc(out_ready, 1)

            @block.vector
            def _(dve):
                link = link_on(dve, chained)
                dve.wait_ge(weights_turned, 1)
                nc.vector.tensor_copy(turned[:, 0, 0:C2], ps[:, 7, 0:C2])
                nc.vector.tensor_copy(turned[0:C2, 1, :], ps[0:C2, 7, 128:256])
                nc.vector.tensor_copy(turned[:, 2, 0:C2], ps[:, 7, 256:256 + C2]).then_inc(weights_ready, 1)
                nc.vector.tensor_copy(wq_wide[:], w["wq_r"][:, 0:1].to_broadcast([128, 128])).then_inc(weights_ready, 1)
                for b in range(IMAGES):
                    if b % 4 == 0:
                        dve.wait_ge(x_in[b // 4], 16)
                    last = nc.vector.bn_stats(stats[:, b, :], x[:, b, :])
                last.then_inc(stats_ready, 1)
                dve.wait_ge(stats_ready, 1)
                even, odd = stats[:, :, 1], stats[:, :, 4]
                link(nc.vector.tensor_tensor(mean, even, odd, ALU.add))
                link(nc.vector.tensor_scalar(mean, mean, 0.5, None, ALU.mult))
                last = nc.vector.tensor_tensor(dev, even, odd, ALU.subtract)
                last.then_inc(mean_ready, 1)
                dve.wait_ge(mean_ready, 1)
                link(nc.vector.tensor_tensor(square, dev, dev, ALU.mult))
                link(nc.vector.tensor_scalar(square, square, N / 4.0, None, ALU.mult))
                link(nc.vector.tensor_tensor(square, square, stats[:, :, 2], ALU.add))
                link(nc.vector.tensor_tensor(square, square, stats[:, :, 5], ALU.add))
                dve.wait_ge(grouped, 1)
                link(nc.vector.tensor_copy(group_mean[:], ps[:, 0, 0:IMAGES]))
                link(nc.vector.tensor_tensor(halves, mean, group_mean[:], ALU.subtract))
                link(nc.vector.tensor_tensor(spread, halves, halves, ALU.mult))
                link(nc.vector.tensor_scalar(spread, spread, float(N), None, ALU.mult))
                nc.vector.tensor_tensor(spread, spread, square, ALU.add).then_inc(spread_ready, 1)
                dve.wait_ge(grouped, 2)
                nc.vector.tensor_scalar(dev, ps[:, 0, 0:IMAGES], 1.0 / N, GN_EPS, ALU.mult,
                                        ALU.add).then_inc(var_ready, 1)
                dve.wait_ge(std_ready, 1)
                link(nc.vector.reciprocal(rstd, square))
                for b in range(IMAGES):
                    nc.vector.tensor_scalar(xn[:, b, :], x[:, b, :], group_mean[:, b:b + 1], rstd[:, b:b + 1],
                                            ALU.subtract, ALU.mult).then_inc(xn_ready, 1)
                for m in range(IMAGES // 2 + 2):
                    if m < IMAGES // 2:
                        dve.wait_ge(logits_ready, m + 1)
                        nc.vector.tensor_reduce(out=peak[:, 2 * m:2 * m + 2],
                                                in_=ps[:, 1 + m % 2, :].rearrange("p (b n) -> p b n", b=2),
                                                axis=AX.X, op=ALU.max, negate=True).then_inc(peak_ready, 1)
                    if m >= 2:
                        dve.wait_ge(weighted_ready, m - 1)
                        nc.vector.tensor_reduce(out=pooled[:, 2 * m - 4:2 * m - 2], in_=weighted[:, (m - 2) % 2],
                                                axis=AX.X, op=ALU.add).then_inc(pooled_part, 1)
                dve.wait_ge(prob_ready, IMAGES // 2)
                dve.wait_ge(pooled_part, IMAGES // 2)
                link(nc.vector.reciprocal(peak, total))
                nc.vector.tensor_tensor(pooled, pooled, peak, ALU.mult).then_inc(pooled_ready, 1)
                dve.wait_ge(small_on_pe, 1)
                nc.vector.tensor_copy(squeezed[:], ps[0:C2, 0, 0:IMAGES]).then_inc(small_on_dve, 1)
                dve.wait_ge(small_on_act, 1)
                link(nc.vector.tensor_tensor(summed, halves, rstd, ALU.mult))
                nc.vector.tensor_tensor(summed, summed, gate, ALU.mult).then_inc(small_on_dve, 1)
                dve.wait_ge(small_on_pe, 3)
                nc.vector.tensor_reduce(out=q_one[:, 0:1], in_=ps[0:IMAGES, 3, 0:C2], axis=AX.X, op=ALU.max,
                                        negate=True).then_inc(small_on_dve, 1)
                dve.wait_ge(small_on_act, 2)
                link(nc.vector.reciprocal(q_one[:, 2:3], q_one[:, 1:2]))
                nc.vector.tensor_scalar(q_small[:], q_exp[:], q_one[:, 2:3], None, ALU.mult).then_inc(small_on_dve, 1)
                dve.wait_ge(small_on_pe, 4)
                nc.vector.tensor_copy(qT[:], ps[0:C2, 4, 0:IMAGES]).then_inc(small_on_dve, 1)
                dve.wait_ge(small_on_pe, 5)
                link(nc.vector.tensor_tensor(vw, ps[:, 3, 0:IMAGES], gate, ALU.mult))

                def widen(b):
                    if b >= 4:
                        dve.wait_ge(place_on_pe, (b - 4) // 2 + 1)
                    nc.vector.tensor_copy(v_wide[:, b % 4, :], vw[:, b:b + 1].to_broadcast([128, 128]))\
                        .then_inc(wide_ready, 1)

                for b in range(4):
                    widen(b)
                for m in range(IMAGES // 2):
                    dve.wait_ge(place_ready, m + 1)
                    if m >= 2:
                        dve.wait_ge(out_ready, m - 1)
                    for a in range(2):
                        b = 2 * m + a
                        last = nc.vector.scalar_tensor_tensor(out=gated[:, m % 2, a, :], in0=xn[:, b, :],
                                                              scalar=gate[:, b:b + 1], in1=place[:, m % 2, a, :],
                                                              op0=ALU.mult, op1=ALU.mult)
                    last.then_inc(gated_ready, 1)
                    for b in (2 * m + 4, 2 * m + 5):
                        if b < IMAGES:
                            widen(b)


def attention(nc, mode, src, tokens, wqk, wv, wo, ident, q_bias, v_bias, o_bias, lo_rows, ones_row, mask, ps):
    softmax = mode != "linear"
    with stage(nc, mode) as (sb, sem):

        xs = sb("xs", [128, 2, N])
        full = sb("full", [128, 2, 2, N])
        high = sb("high", [128, 2, 2, N], FP32R)
        stack = sb("stack", [128, 2, 8, N], FP32R)
        vaug = sb("vaug", [128, 2, 2, H, 32])
        negmax = sb("negmax", [128, 2, 2])
        prob = sb("prob", [128, 2, 2, N])
        probT = sb("probT", [128, 2, 2, N])
        heads = sb("heads", [128, 2, 2, 128])
        recip = sb("recip", [128, 2, 2, 4])
        normed = sb("normed", [128, 2, 2, 4, 16])
        normedT = sb("normedT", [128, 2, 128])

        xs_ready = [sem(f"xs_ready{u}") for u in range(2)]
        qk_projected = sem("qk_projected")
        full_ready = sem("full_ready")
        high_ready = sem("high_ready")
        stack_ready = sem("stack_ready")
        v_projected = sem("v_projected")
        vaug_ready = sem("vaug_ready")
        vaug_set = sem("vaug_set")
        scored = sem("scored")
        max_ready = sem("max_ready")
        exp_ready = sem("exp_ready")
        transposed = sem("transposed")
        even_copied = sem("even_copied")
        odd_copied = sem("odd_copied")
        weighted = sem("weighted")
        heads_ready = sem("heads_ready")
        heads_turned = sem("heads_turned")
        recip_ready = sem("recip_ready")
        normed_ready = sem("normed_ready")
        normed_turned = sem("normed_turned")
        normedT_ready = sem("normedT_ready")
        out_projected = sem("out_projected")
        tokens_ready = sem("tokens_ready")

        PROJ, SCORE, TURN, HEADS, MISC = 0, 2, 4, 6, 7

        def images(step):
            def run(engine):
                step(0, 0, True, False)
                with engine.Fori(0, (IMAGES - 2) // 2) as i:
                    step(2 * i + 1, 1, False, False)
                    step(2 * i + 2, 0, False, False)
                step(IMAGES - 1, 1, False, True)
            return run

        with nc.Block() as block:
            @block.gpsimd
            def _(pool):
                nc.gpsimd.memset(vaug[:], 0.0).then_inc(vaug_set, 1)
                pool.wait_ge(vaug_set, 1)
                nc.gpsimd.memset(vaug[:, :, :, :, 16:17], 1.0).then_inc(vaug_set, 1)

            @block.sync
            def _(sp):
                def load(n, u, fresh):
                    at = n * N if fresh else sp.snap(n * N)
                    if not fresh:
                        sp.wait_ge(qk_projected, 4 * n - 4)
                    sp.dma_start(xs[:, u, :], src[:, bass.ds(at, N)]).then_inc(xs_ready[u], 16)

                load(0, 0, True)
                load(1, 1, True)

                def step(n, u, first, last):
                    if not first and not last:
                        load(n + 1, 1 - u, False)

                images(step)(sp)

            @block.tensor
            def _(pe):
                def project(n, u, fresh, j):
                    pe.wait_ge(xs_ready[u], 8 * n + 16 - 8 * u)
                    if not (fresh and j < 2):
                        pe.wait_ge(full_ready, 4 * n + j - 1)
                    for g in range(2):
                        mm = nc.tensor.matmul(ps[:, PROJ + j % 2, g * N:(g + 1) * N], wqk[:, 2 * j + g, :],
                                              xs[:, u, :], start=True, stop=True)
                    mm.then_inc(qk_projected, 1)

                def project_v(n, u, fresh):
                    pe.wait_ge(xs_ready[u], 8 * n + 16 - 8 * u)
                    if not fresh:
                        pe.wait_ge(vaug_ready, n)
                        pe.wait_ge(tokens_ready, n - 1)
                    elif n:
                        pe.wait_ge(vaug_ready, n)
                    for a in range(2):
                        mm = nc.tensor.matmul(ps[:, MISC, a * 128:(a + 1) * 128], xs[:, u, a * 128:(a + 1) * 128],
                                              wv[:], start=True, stop=True)
                    mm.then_inc(v_projected, 1)

                def score(n, u, fresh, k):
                    if k == 0:
                        pe.wait_ge(stack_ready, 4 * n + 4)
                    if not (fresh and k < 2):
                        if softmax:
                            pe.wait_ge(exp_ready, 8 * n + k - 1)
                        else:
                            pe.wait_ge(even_copied, 8 * n + k - 1)
                    rows = slice(64 * (k % 2), 64 * (k % 2) + 64)
                    q, key = stack[rows, u, k // 2, :], stack[rows, u, 4 + k // 2, :]
                    one, other = (q, key) if softmax else (key, q)
                    for a in range(2):
                        if mode == "window":
                            nc.tensor.matmul(ps[:, SCORE + k % 2, a * N:(a + 1) * N], mask["ident"][:],
                                             mask["rows"][:, a * N:(a + 1) * N], start=True, stop=False)
                        mm = nc.tensor.matmul(ps[:, SCORE + k % 2, a * N:(a + 1) * N],
                                              one[:, a * 128:(a + 1) * 128], other,
                                              start=mode != "window", stop=True)
                    mm.then_inc(scored, 1)

                def turn(n, fresh, k):
                    pe.wait_ge(exp_ready, 8 * n + k + 1)
                    if not (fresh and k < 2):
                        pe.wait_ge(odd_copied if k % 2 else even_copied, 4 * n + k // 2)
                    for b in range(2):
                        for a in range(2):
                            mm = nc.tensor.transpose(ps[:, TURN + k % 2, (2 * b + a) * 128:(2 * b + a + 1) * 128],
                                                     prob[:, k % 2, a, b * 128:(b + 1) * 128], ident[:])
                    mm.then_inc(transposed, 1)

                def weigh(n, u, fresh, k):
                    if k == 0:
                        pe.wait_ge(vaug_ready, n + 1)
                        if not fresh:
                            pe.wait_ge(heads_ready, n)
                    if softmax:
                        pe.wait_ge(odd_copied if k % 2 else even_copied, 4 * n + k // 2 + 1)
                        keys = probT
                    else:
                        pe.wait_ge(even_copied, 8 * n + k + 1)
                        keys = prob
                    r, c = 32 * (k % 4), (k // 4) * N
                    for b in range(2):
                        mm = nc.tensor.matmul(ps[r:r + 32, HEADS, c:c + N], vaug[:, u, b, k, :],
                                              keys[:, k % 2, b, :], start=b == 0, stop=b == 1)
                    mm.then_inc(weighted, 1)

                def turn_heads(n, last):
                    pe.wait_ge(heads_ready, n + 1)
                    pe.wait_ge(vaug_ready, IMAGES if last else n + 2)
                    if last:
                        pe.wait_ge(tokens_ready, n)
                    for g in range(2):
                        for a in range(2):
                            mm = nc.tensor.transpose(ps[:, MISC, (2 * g + a) * 128:(2 * g + a + 1) * 128],
                                                     heads[:, g, a, :], ident[:])
                    mm.then_inc(heads_turned, 1)

                def turn_normed(n):
                    pe.wait_ge(normed_ready, 2 * n + 2)
                    for a in range(2):
                        mm = nc.tensor.transpose(ps[:, MISC, a * 128:(a + 1) * 128],
                                                 normed[:, a].rearrange("p g h d -> p (g h d)"), ident[:])
                    mm.then_inc(normed_turned, 1)

                def project_out(n):
                    pe.wait_ge(normedT_ready, n + 1)
                    for a in range(2):
                        mm = nc.tensor.matmul(ps[:, MISC, a * 128:(a + 1) * 128], normedT[:, a, :], wo[:],
                                              start=True, stop=o_bias is None)
                        if o_bias is not None:
                            mm = nc.tensor.matmul(ps[:, MISC, a * 128:(a + 1) * 128], ones_row[0:1, 0:128],
                                                  o_bias[0:1, :], start=False, stop=True)
                    mm.then_inc(out_projected, 1)

                for j in range(3):
                    project(0, 0, True, j)
                project_v(0, 0, True)
                project(0, 0, True, 3)

                def step(n, u, first, last):
                    for k in range(8):
                        score(n, u, first, k)
                        if not first:
                            if k == 0:
                                turn_heads(n - 1, False)
                            if k == 2:
                                turn_normed(n - 1)
                            if k == 4:
                                project_out(n - 1)
                        if not last:
                            if k in (1, 3, 5, 7):
                                project(n + 1, 1 - u, False, k // 2)
                            if k == 6:
                                project_v(n + 1, 1 - u, first)
                        if softmax and k >= 1:
                            turn(n, first, k - 1)
                        if k >= 2:
                            weigh(n, u, first, k - 2)
                    if softmax:
                        turn(n, first, 7)
                    weigh(n, u, first, 6)
                    weigh(n, u, first, 7)

                images(step)(pe)
                turn_heads(IMAGES - 1, True)
                turn_normed(IMAGES - 1)
                project_out(IMAGES - 1)

            @block.scalar
            def _(act):
                def evacuate(n, fresh, j):
                    act.wait_ge(qk_projected, 4 * n + j + 1)
                    if not (fresh and j < 2):
                        act.wait_ge(stack_ready, 4 * n + j - 1)
                    if q_bias is None:
                        nc.scalar.activation(full[:, j % 2].rearrange("p g n -> p (g n)"), ps[:, PROJ + j % 2, :],
                                             ACT.Copy).then_inc(full_ready, 1)
                    else:
                        for g in range(2):
                            last = nc.scalar.activation(full[:, j % 2, g, :], ps[:, PROJ + j % 2, g * N:(g + 1) * N],
                                                        ACT.Identity, bias=q_bias[:, 2 * j + g:2 * j + g + 1])
                        last.then_inc(full_ready, 1)

                def round_high(n, fresh, j):
                    act.wait_ge(full_ready, 4 * n + j + 1)
                    if not (fresh and j < 2):
                        act.wait_ge(stack_ready, 4 * n + j - 1)
                    nc.scalar.activation(high[:, j % 2], full[:, j % 2], ACT.Copy).then_inc(high_ready, 1)

                def exponential(n, fresh, k):
                    act.wait_ge(max_ready, 8 * n + k + 1)
                    if not (fresh and k < 2):
                        act.wait_ge(transposed, 8 * n + k - 1)
                    for g in range(2):
                        last = nc.scalar.activation(prob[:, k % 2, g, :], ps[:, SCORE + k % 2, g * N:(g + 1) * N],
                                                    ACT.Exp, bias=negmax[:, k % 2, g:g + 1])
                    last.then_inc(exp_ready, 1)

                def copy_odd(n, fresh, k):
                    act.wait_ge(transposed, 8 * n + k + 1)
                    if not (fresh and k < 2):
                        act.wait_ge(weighted, 8 * n + k - 1)
                    nc.scalar.activation(probT[:, 1].rearrange("p b n -> p (b n)"), ps[:, TURN + 1, :],
                                         ACT.Copy).then_inc(odd_copied, 1)

                def take_heads(n, fresh):
                    act.wait_ge(weighted, 8 * n + 8)
                    if not fresh:
                        act.wait_ge(heads_turned, n)
                    nc.scalar.activation(heads[:].rearrange("p g a n -> p (g a n)"), ps[:, HEADS, :],
                                         ACT.Copy).then_inc(heads_ready, 1)

                def take_normed(n, fresh):
                    act.wait_ge(normed_turned, n + 1)
                    if not fresh:
                        act.wait_ge(out_projected, n)
                    nc.scalar.activation(normedT[:].rearrange("p a n -> p (a n)"), ps[:, MISC, 0:N],
                                         ACT.Copy).then_inc(normedT_ready, 1)

                for j in range(4):
                    if softmax:
                        evacuate(0, True, j)
                    else:
                        round_high(0, True, j)

                def step(n, u, first, last):
                    for k in range(8):
                        if softmax:
                            exponential(n, first, k)
                        if not first and k == 3:
                            take_normed(n - 1, False)
                        if not last and k in (1, 3, 5, 7):
                            if softmax:
                                evacuate(n + 1, False, k // 2)
                            else:
                                round_high(n + 1, False, k // 2)
                        if softmax and k in (2, 4, 6):
                            copy_odd(n, first, k - 1)
                    if softmax:
                        copy_odd(n, first, 7)
                    take_heads(n, first)

                images(step)(act)
                take_normed(IMAGES - 1, False)

            @block.vector
            def _(dve):
                def evacuate(n, fresh, j):
                    dve.wait_ge(qk_projected, 4 * n + j + 1)
                    if not (fresh and j < 2):
                        dve.wait_ge(stack_ready, 4 * n + j - 1)
                    nc.vector.tensor_scalar(full[:, j % 2].rearrange("p g n -> p (g n)"), ps[:, PROJ + j % 2, :],
                                            0.0, LINEAR_EPS, ALU.max, ALU.add).then_inc(full_ready, 1)

                def round_high(n, j):
                    dve.wait_ge(full_ready, 4 * n + j + 1)
                    nc.vector.tensor_copy(high[:, j % 2], full[:, j % 2]).then_inc(high_ready, 1)

                def split(n, u, fresh, j):
                    dve.wait_ge(high_ready, 4 * n + j + 1)
                    if not fresh and j == 0:
                        dve.wait_ge(scored, 8 * n - 8)
                    nc.vector.scalar_tensor_tensor(
                        out=stack[:, u, 2 * j:2 * j + 2, :], in0=high[:, j % 2].bitcast(FP32),
                        scalar=lo_rows[:, j // 2:j // 2 + 1], in1=full[:, j % 2], op0=ALU.mult,
                        op1=ALU.add).then_inc(stack_ready, 1)

                def take_values(n, u, fresh):
                    dve.wait_ge(v_projected, n + 1)
                    if fresh and n == 0:
                        dve.wait_ge(vaug_set, 2)
                    if not fresh:
                        dve.wait_ge(weighted, 8 * n - 8)
                    for a in range(2):
                        out = vaug[:, u, a, :, 0:16]
                        got = ps[:, MISC, a * 128:(a + 1) * 128].rearrange("p (h d) -> p h d", d=D)
                        if v_bias is None:
                            last = nc.vector.tensor_copy(out, got)
                        else:
                            last = nc.vector.tensor_tensor(out, got, v_bias[:].rearrange("p (h d) -> p h d", d=D),
                                                           ALU.add)
                    last.then_inc(vaug_ready, 1)

                def maximum(n, fresh, k):
                    dve.wait_ge(scored, 8 * n + k + 1)
                    if not (fresh and k < 2):
                        dve.wait_ge(exp_ready, 8 * n + k - 1)
                    nc.vector.tensor_reduce(out=negmax[:, k % 2, :],
                                            in_=ps[:, SCORE + k % 2, :].rearrange("p (g n) -> p g n", n=N),
                                            axis=AX.X, op=ALU.max, negate=True).then_inc(max_ready, 1)

                def copy_even(n, fresh, k):
                    dve.wait_ge(transposed, 8 * n + k + 1)
                    if not (fresh and k < 2):
                        dve.wait_ge(weighted, 8 * n + k - 1)
                    nc.vector.tensor_copy(probT[:, 0].rearrange("p b n -> p (b n)"),
                                          ps[:, TURN, :]).then_inc(even_copied, 1)

                def causal(n, fresh, k):
                    dve.wait_ge(scored, 8 * n + k + 1)
                    if not (fresh and k < 2):
                        dve.wait_ge(weighted, 8 * n + k - 1)
                    nc.vector.tensor_tensor(prob[:, k % 2].rearrange("p g n -> p (g n)"), ps[:, SCORE + k % 2, :],
                                            mask["keep"][:], ALU.mult).then_inc(even_copied, 1)

                def normalise(n, fresh):
                    dve.wait_ge(heads_turned, n + 1)
                    turned = ps[:, MISC, :].rearrange("p (g a h d) -> p g a h d", g=2, a=2, h=4)
                    for g in range(2):
                        nc.vector.reciprocal(recip[:, g], turned[:, g, :, :, 16]).then_inc(recip_ready, 1)
                    dve.wait_ge(recip_ready, 2 * n + 2)
                    if not fresh:
                        dve.wait_ge(normed_turned, n)
                    for a in range(2):
                        nc.vector.tensor_tensor(
                            normed[:, a], turned[:, :, a, :, 0:16],
                            recip[:, :, a, :, None].to_broadcast([128, 2, 4, 16]), ALU.mult).then_inc(normed_ready, 1)

                def add_out(n):
                    dve.wait_ge(out_projected, n + 1)
                    at = tokens[:, bass.ds(2 * n, 2), :]
                    nc.vector.tensor_tensor(at, at, ps[:, MISC, 0:N].rearrange("p (a c) -> p a c", a=2),
                                            ALU.add).then_inc(tokens_ready, 1)

                for j in range(4):
                    if not softmax:
                        evacuate(0, True, j)
                    else:
                        round_high(0, j)
                    split(0, 0, True, j)
                take_values(0, 0, True)

                def step(n, u, first, last):
                    for k in range(8):
                        if softmax:
                            maximum(n, first, k)
                        else:
                            causal(n, first, k)
                        if not first:
                            if k == 1:
                                normalise(n - 1, False)
                            if k == 5:
                                add_out(n - 1)
                        if not last:
                            if k in (1, 3, 5, 7) and not softmax:
                                evacuate(n + 1, False, k // 2)
                            if k in (3, 5, 7):
                                split(n + 1, 1 - u, first, k // 2 - 1)
                            if k in (2, 4, 6) and softmax:
                                round_high(n + 1, k // 2 - 1)
                            if k == 7:
                                take_values(n + 1, 1 - u, first)
                        if softmax and k in (1, 3, 5, 7):
                            copy_even(n, first, k - 1)
                    if not last:
                        if softmax:
                            round_high(n + 1, 3)
                        split(n + 1, 1 - u, first, 3)

                images(step)(dve)
                normalise(IMAGES - 1, False)
                add_out(IMAGES - 1)


def layer_norm(nc, name, tokens, normed, xf, ident, ps, gate=None):
    CHUNK = 8
    CHUNKS = TILES // CHUNK
    with stage(nc, name) as (sb, sem):

        squares = sb("squares", [128, 2, CHUNK, C])
        stat = sb("stat", [128, 4, TILES])
        mean, var, std, rstd = (stat[:, i, :] for i in range(4))
        turned_sb = sb("turned", [128, 2, CHUNK * 128]) if gate is not None else None

        mean_ready, centred, squared, var_ready, std_ready, rstd_ready, normed_ready, turned, taken, logits_ready = (
            sem(n) for n in ("mean_ready", "centred", "squared", "var_ready", "std_ready", "rstd_ready",
                             "normed_ready", "turned", "taken", "logits_ready"))
        chained = sem("chained")

        def part(c):
            return slice(c * CHUNK, (c + 1) * CHUNK)

        with nc.Block() as block:
            @block.vector
            def _(dve):
                link = link_on(dve, chained)

                def centre(c):
                    link(nc.vector.tensor_reduce(out=mean[:, part(c)], in_=tokens[:, part(c), :], axis=AX.X,
                                                 op=ALU.add))
                    link(nc.vector.tensor_scalar(mean[:, part(c)], mean[:, part(c)], 1.0 / C, None, ALU.mult))
                    nc.vector.tensor_tensor(normed[:, part(c), :], tokens[:, part(c), :],
                                            mean[:, part(c), None].to_broadcast([128, CHUNK, C]),
                                            ALU.subtract).then_inc(centred, 1)

                def variance(c):
                    dve.wait_ge(squared, c + 1)
                    link(nc.vector.tensor_reduce(out=var[:, part(c)], in_=squares[:, c % 2], axis=AX.X, op=ALU.add))
                    nc.vector.tensor_scalar(var[:, part(c)], var[:, part(c)], 1.0 / C, LN_EPS, ALU.mult,
                                            ALU.add).then_inc(var_ready, 1)

                def scale(c):
                    dve.wait_ge(std_ready, c + 1)
                    link(nc.vector.reciprocal(rstd[:, part(c)], std[:, part(c)]))
                    nc.vector.tensor_tensor(normed[:, part(c), :], normed[:, part(c), :],
                                            rstd[:, part(c), None].to_broadcast([128, CHUNK, C]),
                                            ALU.mult).then_inc(normed_ready, 1)

                for c in range(CHUNKS + 2):
                    if c < CHUNKS:
                        centre(c)
                    if 1 <= c <= CHUNKS:
                        variance(c - 1)
                    if c >= 2:
                        scale(c - 2)

            @block.scalar
            def _(act):
                def take(c):
                    act.wait_ge(turned, c + 1)
                    if xf is not None:
                        out = xf[:, c * CHUNK * 128:(c + 1) * CHUNK * 128]
                    else:
                        if c >= 2:
                            act.wait_ge(logits_ready, c - 1)
                        out = turned_sb[:, c % 2, :]
                    nc.scalar.activation(out, ps[:, 2 * (c % 2):2 * (c % 2) + 2, :].rearrange("p a n -> p (a n)"),
                                         ACT.Copy).then_inc(taken, 1)

                for c in range(CHUNKS + 3):
                    if c < CHUNKS:
                        act.wait_ge(centred, c + 1)
                        if c >= 2:
                            act.wait_ge(var_ready, c - 1)
                        nc.scalar.activation(squares[:, c % 2], normed[:, part(c), :], ACT.Square).then_inc(squared, 1)
                    if 1 <= c <= CHUNKS:
                        act.wait_ge(var_ready, c)
                        nc.scalar.activation(std[:, part(c - 1)], var[:, part(c - 1)], ACT.Sqrt).then_inc(std_ready, 1)
                    if c >= 3:
                        take(c - 3)

            @block.tensor
            def _(pe):
                def logits(c):
                    pe.wait_ge(taken, c + 1)
                    experts = gate.shape[1]
                    for a in range(CHUNK):
                        at = (c * CHUNK + a) * experts
                        mm = nc.tensor.matmul(ps[:, 7, at:at + experts], turned_sb[:, c % 2, a * 128:(a + 1) * 128],
                                              gate[:, :], start=True, stop=True)
                    mm.then_inc(logits_ready, 1)

                for c in range(CHUNKS):
                    pe.wait_ge(normed_ready, c + 1)
                    if c >= 2:
                        pe.wait_ge(taken, c - 1)
                    for a in range(CHUNK):
                        mm = nc.tensor.transpose(ps[:, 2 * (c % 2) + a // 4, a % 4 * 128:(a % 4 + 1) * 128],
                                                 normed[:, c * CHUNK + a, :], ident[:])
                    mm.then_inc(turned, 1)
                    if gate is not None and c >= 1:
                        logits(c - 1)
                if gate is not None:
                    logits(CHUNKS - 1)


def route(nc, name, experts, taken, tiles, bias, consts, normed, slots, position, tile_expert, weight, counts, ps):
    with stage(nc, name) as (sb, sem):

        wide = [128, TILES, experts]
        logits = sb("logits", wide)
        chosen = [sb(f"chosen{k}", wide) for k in range(taken)]
        scratch = sb("scratch", wide)
        select = sb("select", wide) if taken > 1 else chosen[0]
        running = [sb(f"running{i}", wide) for i in range(2)]
        top = sb("top", [128, taken, TILES])
        first = sb("first", [128, TILES])
        ends = sb("ends", [128, 6, experts])
        ends_int = sb("ends_int", [128, experts], INT32)
        slot_of = sb("slot_of", [128, TILES])
        past = sb("past", [128, tiles, experts])
        expert_of = sb("expert_of", [128, tiles])
        zero = sb("zero", [128, 4, C])

        chosen_ready = sem("chosen_ready")
        counted = sem("counted")
        gap_ready = sem("gap_ready")
        exp_ready = sem("exp_ready")
        zero_set = sem("zero_set")
        cleared = sem("cleared")
        placed = sem("placed")
        scattered = sem("scattered")
        chained = sem("chained")

        def over(ap, shape=None):
            return ap.to_broadcast(shape or wide)

        with nc.Block() as block:
            @block.tensor
            def _(pe):
                pe.wait_ge(chosen_ready, 1)
                flat = select[:].rearrange("p t e -> p (t e)")
                nc.tensor.matmul(ps[:, 0, 0:TILES * experts], consts["before"][:], flat, start=True,
                                 stop=True).then_inc(counted, 1)
                nc.tensor.matmul(ps[:, 1, 0:TILES * experts], consts["ones"][:], flat, start=True,
                                 stop=True).then_inc(counted, 1)

            @block.scalar
            def _(act):
                act.wait_ge(gap_ready, 1)
                if taken == 2:
                    nc.scalar.activation(first[:], first[:], ACT.Exp).then_inc(exp_ready, 1)
                else:
                    nc.scalar.activation(scratch[:].rearrange("p t e -> p (t e)"),
                                         scratch[:].rearrange("p t e -> p (t e)"), ACT.Exp).then_inc(exp_ready, 1)

            @block.sync
            def _(sp):
                sp.wait_ge(zero_set, 1)
                for i in range(tiles // 4):
                    sp.dma_start(slots[512 * i:512 * i + 512, :].rearrange("(a p) c -> p a c", p=128), zero[:])\
                        .then_inc(cleared, 16)
                sp.wait_ge(cleared, tiles // 4 * 16)

            @block.gpsimd
            def _(pool):
                nc.gpsimd.memset(zero[:], 0.0).then_inc(zero_set, 1)
                pool.wait_ge(cleared, tiles // 4 * 16)
                for k in range(taken):
                    pool.wait_ge(placed, k + 1)
                    for t in range(TILES):
                        nc.gpsimd.indirect_dma_start(
                            out=slots[:, :], out_offset=bass.IndirectOffsetOnAxis(ap=position[:, k, t:t + 1], axis=0),
                            in_=normed[:, t, :], in_offset=None, bounds_check=tiles * 128 - 1).then_inc(scattered, 16)
                pool.wait_ge(scattered, 16 * taken * TILES)

            @block.vector
            def _(dve):
                link = link_on(dve, chained)
                got = ps[:, 7, 0:TILES * experts].rearrange("p (t e) -> p t e", e=experts)
                if bias is None:
                    link(nc.vector.tensor_copy(logits[:], got))
                else:
                    link(nc.vector.tensor_tensor(logits[:], got, over(bias[:, None, :]), ALU.add))
                index = over(consts["index"][:, None, 0:experts])
                work = logits
                for k in range(taken):
                    link(nc.vector.tensor_reduce(out=top[:, k, :], in_=work[:], axis=AX.X, op=ALU.max))
                    link(nc.vector.tensor_tensor(scratch[:], work[:], over(top[:, k, :, None]), ALU.is_equal))
                    link(nc.vector.tensor_tensor(scratch[:], scratch[:], index, ALU.mult))
                    link(nc.vector.tensor_reduce(out=first[:], in_=scratch[:], axis=AX.X, op=ALU.min))
                    picked = nc.vector.tensor_tensor(chosen[k][:], index, over(first[:, :, None]), ALU.is_equal)
                    if taken == 1:
                        picked.then_inc(chosen_ready, 1)
                        dve.wait_ge(chosen_ready, 1)
                    else:
                        link(picked)
                    if k + 1 < taken:
                        link(nc.vector.scalar_tensor_tensor(
                            out=running[0][:].rearrange("p t e -> p (t e)"),
                            in0=chosen[k][:].rearrange("p t e -> p (t e)"), scalar=MASKED,
                            in1=work[:].rearrange("p t e -> p (t e)"), op0=ALU.mult, op1=ALU.add))
                        work = running[0]
                if taken == 2:
                    nc.vector.tensor_tensor(select[:], chosen[0][:], chosen[1][:], ALU.add).then_inc(chosen_ready, 1)
                    nc.vector.tensor_tensor(first[:], top[:, 1, :], top[:, 0, :], ALU.subtract).then_inc(gap_ready, 1)
                else:
                    nc.vector.tensor_tensor(scratch[:], logits[:], over(top[:, 0, :, None]), ALU.subtract)\
                        .then_inc(gap_ready, 1)
                dve.wait_ge(counted, 2)
                link(nc.vector.tensor_copy(running[0][:].rearrange("p t e -> p (t e)"), ps[:, 1, 0:TILES * experts]))
                a, b, step = running[0], running[1], 1
                while step < TILES:
                    nc.vector.tensor_copy(b[:, 0:step, :], a[:, 0:step, :])
                    link(nc.vector.tensor_tensor(b[:, step:, :], a[:, step:, :], a[:, 0:TILES - step, :], ALU.add))
                    a, b, step = b, a, 2 * step
                total, padded, one, other, start = (ends[:, i, :] for i in range(5))
                link(nc.vector.tensor_copy(total, a[:, TILES - 1, :]))
                link(nc.vector.tensor_tensor(b[:].rearrange("p t e -> p (t e)"), a[:].rearrange("p t e -> p (t e)"),
                                             ps[:, 1, 0:TILES * experts], ALU.subtract))
                link(nc.vector.tensor_tensor(b[:].rearrange("p t e -> p (t e)"), b[:].rearrange("p t e -> p (t e)"),
                                             ps[:, 0, 0:TILES * experts], ALU.add))
                link(nc.vector.tensor_scalar(ends_int[:], total, 127.0, None, ALU.add))
                link(nc.vector.tensor_single_scalar(ends_int[:], ends_int[:], 7, ALU.arith_shift_right))
                link(nc.vector.tensor_copy(padded, ends_int[:]))
                link(nc.vector.tensor_copy(one, padded))
                step = 1
                while step < experts:
                    nc.vector.tensor_copy(other[:, 0:step], one[:, 0:step])
                    link(nc.vector.tensor_tensor(other[:, step:], one[:, step:], one[:, 0:experts - step], ALU.add))
                    one, other, step = other, one, 2 * step
                link(nc.vector.tensor_tensor(start, one, padded, ALU.subtract))
                link(nc.vector.tensor_scalar(start, start, 128.0, None, ALU.mult))
                link(nc.vector.tensor_tensor(b[:], b[:], over(start[:, None, :]), ALU.add))
                for k in range(taken):
                    link(nc.vector.tensor_tensor(a[:], chosen[k][:], b[:], ALU.mult))
                    link(nc.vector.tensor_reduce(out=slot_of[:], in_=a[:], axis=AX.X, op=ALU.add))
                    nc.vector.tensor_copy(position[:, k, :], slot_of[:]).then_inc(placed, 1)
                shape = [128, tiles, experts]
                link(nc.vector.tensor_tensor(past[:], over(one[:, None, :], shape),
                                             over(consts["tile"][:, 0:tiles, None], shape), ALU.is_le))
                link(nc.vector.tensor_reduce(out=expert_of[:], in_=past[:], axis=AX.X, op=ALU.add))
                link(nc.vector.tensor_scalar(tile_expert[:], expert_of[:], float(experts - 1), None, ALU.min))
                dve.wait_ge(exp_ready, 1)
                if taken == 2:
                    link(nc.vector.tensor_scalar(counts[:], total, 1.0, None, ALU.max))
                    link(nc.vector.reciprocal(counts[:], counts[:]))
                    link(nc.vector.tensor_scalar(slot_of[:], first[:], 1.0, None, ALU.add))
                    link(nc.vector.reciprocal(slot_of[:], slot_of[:]))
                    link(nc.vector.tensor_tensor(first[:], first[:], slot_of[:], ALU.mult))
                    link(nc.vector.tensor_tensor(chosen[0][:], chosen[0][:], over(slot_of[:, :, None]), ALU.mult))
                    link(nc.vector.tensor_tensor(chosen[1][:], chosen[1][:], over(first[:, :, None]), ALU.mult))
                    link(nc.vector.tensor_tensor(weight[:], chosen[0][:], chosen[1][:], ALU.add))
                else:
                    link(nc.vector.tensor_reduce(out=slot_of[:], in_=scratch[:], axis=AX.X, op=ALU.add))
                    link(nc.vector.reciprocal(weight[:], slot_of[:]))


def young(s):
    return isinstance(s, int) and s < 2


def slot_loop(count):
    def run(engine, step):
        for s in range(4):
            step(s, s % 2, False)
        with engine.Fori(0, (count - 6) // 2) as i:
            step(2 * i + 4, 0, False)
            step(2 * i + 5, 1, False)
        step(count - 2, 0, False)
        step(count - 1, 1, True)
    return run


def expert_sums(nc, slots, tile_expert, w1T, sums, consts, ps):
    run = slot_loop(S2)
    with stage(nc, "sums") as (sb, sem):

        xs = sb("xs", [128, 2, C])
        xT = sb("xT", [128, 2, 128])
        hidden = sb("hidden", [128, 2, F])
        loaded = [sem(f"loaded{u}") for u in range(2)]
        turned, xT_ready, up_done, hidden_ready, summed, added = (
            sem(n) for n in ("turned", "xT_ready", "up_done", "hidden_ready", "summed", "added"))
        TURN, UP, SUM = 0, 2, 4

        with nc.Block() as block:
            @block.sync
            def _(sp):
                def step(s, u, last):
                    at = s * 128 if isinstance(s, int) else sp.snap(s * 128)
                    if not young(s):
                        sp.wait_ge(turned, s - 1)
                    sp.dma_start(xs[:, u, :], slots[bass.ds(at, 128), :]).then_inc(loaded[u], 16)
                run(sp, step)

            @block.tensor
            def _(pe):
                def turn(s, u):
                    pe.wait_ge(loaded[u], 8 * s + 16 - 8 * u)
                    if not young(s):
                        pe.wait_ge(xT_ready, s - 1)
                    nc.tensor.transpose(ps[:, TURN + u, 0:128], xs[:, u, :], consts["ident"][:]).then_inc(turned, 1)

                def total(s, u):
                    pe.wait_ge(hidden_ready, s + 1)
                    if not young(s):
                        pe.wait_ge(added, s)
                    nc.tensor.matmul(ps[:, SUM + u, :], consts["ones"][:], hidden[:, u, :], start=True,
                                     stop=True).then_inc(summed, 1)

                turn(0, 0)

                def step(s, u, last):
                    e = pe.value_load(tile_expert[0:1, bass.ds(s, 1)], min_val=0, max_val=E2 - 1)
                    if not last:
                        turn(s + 1, 1 - u)
                    pe.wait_ge(xT_ready, s + 1)
                    if not young(s):
                        pe.wait_ge(hidden_ready, s - 1)
                    nc.tensor.matmul(ps[:, UP + u, :], xT[:, u, :], w1T[:, bass.ds(e, 1), :].rearrange("p a f -> p (a f)"),
                                     start=True, stop=True).then_inc(up_done, 1)
                    if not (isinstance(s, int) and s == 0):
                        total(s - 1, 1 - u)
                run(pe, step)
                total(S2 - 1, 1)

            @block.scalar
            def _(act):
                def step(s, u, last):
                    act.wait_ge(up_done, s + 1)
                    if not young(s):
                        act.wait_ge(summed, s - 1)
                    nc.scalar.activation(hidden[:, u, :], ps[:, UP + u, :], ACT.Silu).then_inc(hidden_ready, 1)
                run(act, step)

            @block.vector
            def _(dve):
                nc.vector.memset(sums[:], 0.0).then_inc(added, 1)

                def take(s, u):
                    dve.wait_ge(turned, s + 1)
                    if not young(s):
                        dve.wait_ge(up_done, s - 1)
                    nc.vector.tensor_copy(xT[:, u, :], ps[:, TURN + u, 0:128]).then_inc(xT_ready, 1)

                take(0, 0)

                def step(s, u, last):
                    e = dve.value_load(tile_expert[0:1, bass.ds(s, 1)], min_val=0, max_val=E2 - 1)
                    if not last:
                        take(s + 1, 1 - u)
                    dve.wait_ge(summed, s + 1)
                    dve.wait_ge(added, s + 1)
                    at = sums[:, bass.ds(e, 1), :].rearrange("p a f -> p (a f)")
                    nc.vector.tensor_tensor(at, at, ps[:, SUM + u, :], ALU.add).then_inc(added, 1)
                run(dve, step)


def mix_means(nc, sums, w2, inverse, weight, tokens, consts, ps):
    PARTS = TILES * E2 // 128
    PER = 128 // E2
    with stage(nc, "mix") as (sb, sem):

        product = sb("product", [128, F])
        means = sb("means", [128, PER, E2])
        meansT = sb("meansT", [128, C])
        spread = sb("spread", [128, PER, C])
        weightT = sb("weightT", [128, PARTS, 128])
        turned, weightT_ready, means_ready, means_turned, spread_ready, mixed, added, chained = (
            sem(n) for n in ("turned", "weightT_ready", "means_ready", "means_turned", "spread_ready", "mixed",
                             "added", "chained"))
        with nc.Block() as block:
            @block.tensor
            def _(pe):
                for g in range(PARTS):
                    mm = nc.tensor.transpose(ps[:, 0, g * 128:(g + 1) * 128],
                                             weight[:, g * PER:(g + 1) * PER, :].rearrange("p t e -> p (t e)"),
                                             consts["ident"][:])
                mm.then_inc(turned, 1)
                pe.wait_ge(means_ready, 1)
                nc.tensor.transpose(ps[:, 1, 0:128], means[:].rearrange("p j e -> p (j e)"),
                                    consts["ident"][:]).then_inc(means_turned, 1)
                pe.wait_ge(weightT_ready, 1)
                pe.wait_ge(spread_ready, 1)
                flat = spread[:].rearrange("p j c -> p (j c)")
                for g in range(PARTS):
                    for a in range(2):
                        i = 2 * g + a
                        if i >= 4:
                            pe.wait_ge(added, i - 3)
                        nc.tensor.matmul(ps[:, 2 + i % 4, :], weightT[:, g, :], flat[:, a * 512:(a + 1) * 512],
                                         start=True, stop=True).then_inc(mixed, 1)

            @block.scalar
            def _(act):
                act.wait_ge(turned, 1)
                nc.scalar.activation(weightT[:].rearrange("p g t -> p (g t)"), ps[:, 0, :],
                                     ACT.Copy).then_inc(weightT_ready, 1)

            @block.vector
            def _(dve):
                link = link_on(dve, chained)
                for e in range(E2):
                    link(nc.vector.scalar_tensor_tensor(out=product[:], in0=sums[:, e, :], scalar=inverse[:, e:e + 1],
                                                        in1=w2[:, e, :], op0=ALU.mult, op1=ALU.mult,
                                                        accum_out=means[:, 0, e:e + 1]))
                nc.vector.tensor_copy(means[:, 1:PER, :], means[:, 0:1, :].to_broadcast([128, PER - 1, E2]))\
                    .then_inc(means_ready, 1)
                dve.wait_ge(means_turned, 1)
                link(nc.vector.tensor_copy(meansT[:], ps[:, 1, 0:128]))
                for j in range(PER):
                    last = nc.vector.tensor_scalar(spread[:, j, :], meansT[:], consts["part"][:, j:j + 1], None, ALU.mult)
                last.then_inc(spread_ready, 1)
                for i in range(2 * PARTS):
                    dve.wait_ge(mixed, i + 1)
                    at = tokens[:, 4 * i:4 * i + 4, :]
                    nc.vector.tensor_tensor(at, at, ps[:, 2 + i % 4, :].rearrange("p (t c) -> p t c", c=C),
                                            ALU.add).then_inc(added, 1)


def expert_outputs(nc, slots, outputs, tile_expert, w1, b1, w2, b2, consts, ps):
    run = slot_loop(S3)
    with stage(nc, "expert") as (sb, sem):

        xs = sb("xs", [128, 2, C])
        xT = sb("xT", [128, 2, 128])
        before = sb("before", [128, 2, F])
        hidden = sb("hidden", [128, 2, F])
        hiddenT = sb("hiddenT", [128, 2, FC, 128])
        y = sb("y", [128, 2, C])
        loaded = [sem(f"loaded{u}") for u in range(2)]
        stored = [sem(f"stored{u}") for u in range(2)]
        turned, xT_ready, up_done, before_ready, hidden_ready, hidden_turned, hiddenT_ready, down_done, y_ready = (
            sem(n) for n in ("turned", "xT_ready", "up_done", "before_ready", "hidden_ready", "hidden_turned",
                             "hiddenT_ready", "down_done", "y_ready"))
        TURN, UP, TURN2, DOWN = 0, 2, 4, 6

        with nc.Block() as block:
            @block.sync
            def _(sp):
                def step(s, u, last):
                    at = s * 128 if isinstance(s, int) else sp.snap(s * 128)
                    if not young(s):
                        sp.wait_ge(turned, s - 1)
                    sp.dma_start(xs[:, u, :], slots[bass.ds(at, 128), :]).then_inc(loaded[u], 16)
                run(sp, step)

            @block.gpsimd
            def _(pool):
                def step(s, u, last):
                    at = s * 128 if isinstance(s, int) else pool.snap(s * 128)
                    pool.wait_ge(y_ready, s + 1)
                    pool.dma_start(outputs[bass.ds(at, 128), :], y[:, u, :]).then_inc(stored[u], 16)
                run(pool, step)
                for u in range(2):
                    pool.wait_ge(stored[u], 16 * S3 // 2)

            @block.tensor
            def _(pe):
                def turn(s, u):
                    pe.wait_ge(loaded[u], 8 * s + 16 - 8 * u)
                    if not young(s):
                        pe.wait_ge(xT_ready, s - 1)
                    nc.tensor.transpose(ps[:, TURN + u, 0:128], xs[:, u, :], consts["ident"][:]).then_inc(turned, 1)

                def turn_hidden(s, u):
                    pe.wait_ge(hidden_ready, s + 1)
                    if not young(s):
                        pe.wait_ge(hiddenT_ready, s - 1)
                    for c in range(FC):
                        mm = nc.tensor.transpose(ps[:, TURN2 + u, c * 128:(c + 1) * 128],
                                                 hidden[:, u, c * 128:(c + 1) * 128], consts["ident"][:])
                    mm.then_inc(hidden_turned, 1)

                def down(s, u, e):
                    pe.wait_ge(hiddenT_ready, s + 1)
                    if not young(s):
                        pe.wait_ge(y_ready, s - 1)
                    for c in range(FC):
                        mm = nc.tensor.matmul(ps[:, DOWN + u, 0:C], hiddenT[:, u, c, :],
                                              w2[:, bass.ds(e, 1), c, :].rearrange("p a c -> p (a c)"),
                                              start=c == 0, stop=c == FC - 1)
                    mm.then_inc(down_done, 1)

                turn(0, 0)

                def expert(s):
                    return pe.value_load(tile_expert[0:1, bass.ds(s, 1)], min_val=0, max_val=E3 - 1)

                def step(s, u, last):
                    e = expert(s)
                    if not last:
                        turn(s + 1, 1 - u)
                    pe.wait_ge(xT_ready, s + 1)
                    if not young(s):
                        pe.wait_ge(before_ready, s - 1)
                    nc.tensor.matmul(ps[:, UP + u, :], xT[:, u, :], w1[:, bass.ds(e, 1), :].rearrange("p a f -> p (a f)"),
                                     start=True, stop=True).then_inc(up_done, 1)
                    if not (isinstance(s, int) and s == 0):
                        turn_hidden(s - 1, 1 - u)
                        down(s - 1, 1 - u, expert(s - 1))
                run(pe, step)
                turn_hidden(S3 - 1, 1)
                down(S3 - 1, 1, expert(S3 - 1))

            @block.scalar
            def _(act):
                def gelu(s, u):
                    act.wait_ge(before_ready, s + 1)
                    if not young(s):
                        act.wait_ge(hidden_turned, s - 1)
                    nc.scalar.activation(hidden[:, u, :], before[:, u, :], ACT.Gelu).then_inc(hidden_ready, 1)

                def take(s, u):
                    act.wait_ge(hidden_turned, s + 1)
                    if not young(s):
                        act.wait_ge(down_done, s - 1)
                    nc.scalar.activation(hiddenT[:, u].rearrange("p c n -> p (c n)"), ps[:, TURN2 + u, :],
                                         ACT.Copy).then_inc(hiddenT_ready, 1)

                def step(s, u, last):
                    gelu(s, u)
                    take(s, u)
                run(act, step)

            @block.vector
            def _(dve):
                def take(s, u):
                    dve.wait_ge(turned, s + 1)
                    if not young(s):
                        dve.wait_ge(up_done, s - 1)
                    nc.vector.tensor_copy(xT[:, u, :], ps[:, TURN + u, 0:128]).then_inc(xT_ready, 1)

                def finish(s, u, e):
                    dve.wait_ge(down_done, s + 1)
                    if not young(s):
                        dve.wait_ge(stored[u], 8 * s - 8 * u)
                    nc.vector.tensor_tensor(y[:, u, :], ps[:, DOWN + u, 0:C],
                                            b2[:, bass.ds(e, 1), :].rearrange("p a c -> p (a c)"),
                                            ALU.add).then_inc(y_ready, 1)

                def expert(s):
                    return dve.value_load(tile_expert[0:1, bass.ds(s, 1)], min_val=0, max_val=E3 - 1)

                take(0, 0)

                def step(s, u, last):
                    e = expert(s)
                    if not last:
                        take(s + 1, 1 - u)
                    dve.wait_ge(up_done, s + 1)
                    if not young(s):
                        dve.wait_ge(hidden_ready, s - 1)
                    nc.vector.tensor_tensor(before[:, u, :], ps[:, UP + u, :],
                                            b1[:, bass.ds(e, 1), :].rearrange("p a f -> p (a f)"),
                                            ALU.add).then_inc(before_ready, 1)
                    if not (isinstance(s, int) and s == 0):
                        finish(s - 1, 1 - u, expert(s - 1))
                run(dve, step)
                finish(S3 - 1, 1, expert(S3 - 1))


def gather_outputs(nc, outputs, position, weight, tokens, gathered, out_dram, consts, ps):
    with stage(nc, "last") as (sb, sem):

        result = sb("result", [128, 8, 512])
        arrived = [sem(f"arrived{g}") for g in range(8)]
        scaled, added, turned, taken, stored = (sem(n) for n in ("scaled", "added", "turned", "taken", "stored"))
        with nc.Block() as block:
            @block.gpsimd
            def _(pool):
                for t in range(TILES):
                    nc.gpsimd.indirect_dma_start(
                        out=gathered[:, t, :], out_offset=None, in_=outputs[:, :],
                        in_offset=bass.IndirectOffsetOnAxis(ap=position[:, 0, t:t + 1], axis=0),
                        bounds_check=S3 * 128 - 1).then_inc(arrived[t // 4], 16)

            @block.vector
            def _(dve):
                for g in range(8):
                    at = slice(4 * g, 4 * g + 4)
                    dve.wait_ge(arrived[g], 64)
                    nc.vector.tensor_tensor(gathered[:, at, :], gathered[:, at, :],
                                            weight[:, at, None].to_broadcast([128, 4, C]), ALU.mult).then_inc(scaled, 1)
                    dve.wait_ge(scaled, g + 1)
                    nc.vector.tensor_tensor(tokens[:, at, :], tokens[:, at, :], gathered[:, at, :],
                                            ALU.add).then_inc(added, 1)

            @block.tensor
            def _(pe):
                for g in range(8):
                    pe.wait_ge(added, g + 1)
                    if g >= 2:
                        pe.wait_ge(taken, g - 1)
                    for a in range(4):
                        mm = nc.tensor.transpose(ps[:, g % 2, a * 128:(a + 1) * 128], tokens[:, 4 * g + a, :],
                                                 consts["ident"][:])
                    mm.then_inc(turned, 1)

            @block.scalar
            def _(act):
                for g in range(8):
                    act.wait_ge(turned, g + 1)
                    nc.scalar.activation(result[:, g, :], ps[:, g % 2, :], ACT.Copy).then_inc(taken, 1)

            @block.sync
            def _(sp):
                for g in range(8):
                    sp.wait_ge(taken, g + 1)
                    sp.dma_start(out_dram[2 * g:2 * g + 2].rearrange("b c h w -> c b (h w)"),
                                 result[:, g, :].rearrange("p (b n) -> p b n", b=2)).then_inc(stored, 16)
                sp.wait_ge(stored, 16 * 8)


def build(nc, a, out):
    with ExitStack() as ctx:
        def sb(name, shape, dt=FP32, into=ctx):
            return into.enter_context(nc.sbuf_tensor(name, shape, dt))

        def sem(name):
            return ctx.enter_context(nc.semaphore(name))

        ps = ctx.enter_context(nc.psum_tensor("ps", [128, 8, 512], FP32))
        tokens = sb("tokens", [128, TILES, C])
        xf = sb("xf", [128, TOKENS])
        normed = sb("normed", [128, TILES, C])

        shapes = {"ident": [128, 128], "group": [128, 128], "before": [128, 128],
                  "ones": [128, 128], "lo_rows": [128, 2], "causal": [128, 2 * N],
                  "index": [128, E2], "tile": [128, S2], "part": [128, 128 // E2]}
        consts = {k: sb(f"const_{k}", v) for k, v in shapes.items()}
        ident16 = sb("ident16", [128, 128], BF16)
        window = sb("window", [128, 2 * N], BF16)

        first = {"wq_r": (a["L0_conv_wq_r"].rearrange("(c o) -> c o", o=1), [C, 1]),
                 "wv_r": (a["L0_conv_wv_r"], [C2, C]), "w_up": (a["L0_conv_w_up"], [C, C2]),
                 "wq_l": (a["L0_conv_wq_l"], [C2, C]), "wv_l": (a["L0_conv_wv_l"], [C2, C])}
        w = {k: sb(f"w_{k}", shape) for k, (_, shape) in first.items()}
        wqk = [sb(f"wqk{i}", [C, 8, 128]) for i in range(3)]
        wv = [sb(f"wv{i}", [C, 128]) for i in range(3)]
        wo = [sb(f"wo{i}", [128, C]) for i in range(3)]
        q_bias = sb("q_bias", [128, 8])
        v_bias = sb("v_bias", [128, 128])
        o_bias = sb("o_bias", [1, 2, C])
        gate2 = sb("gate2", [C, E2])
        gate3 = sb("gate3", [C, E3])
        gate3_bias = sb("gate3_bias", [128, E3])
        position = sb("position", [128, K2, TILES], UINT32)
        tile_expert = sb("tile_expert", [128, S2], INT32)
        weight2 = sb("weight2", [128, TILES, E2])
        weight3 = sb("weight3", [128, TILES])
        inverse = sb("inverse", [128, E2])

        slots = nc.dram_tensor("slots", (S2 * 128, C), FP32, kind="Internal").ap()
        outputs = nc.dram_tensor("slot_outputs", (S3 * 128, C), FP32, kind="Internal").ap()

        consts_in = sem("consts_in")
        raw_in = sem("raw_in")
        experts_in = sem("experts_in")
        last_in = sem("last_in")

        experts2 = ctx.enter_context(ExitStack())
        w1_raw = sb("w1_raw", [128, E2 * FC, C], into=experts2)
        w2 = sb("w2", [128, E2, F], into=experts2)

        with ExitStack() as prep:
            window32 = sb("window32", [128, 2 * N], into=prep)
            raw_fc = sb("raw_fc", [128, 3, C], into=prep)
            raw = sb("raw", [128, 5, C], into=prep)
            raw_qkv = sb("raw_qkv", [C, 2, 128], into=prep)
            raw_gate = sb("raw_gate", [E2, C], into=prep)
            fc_bias = sb("fc_bias", [1, 3 * 128], into=prep)
            fcT = sb("fcT", [C, 3 * 128], into=prep)
            wide_bias = sb("wide_bias", [1, 8 * 128], into=prep)
            turned, copied, biased = sem("turned"), sem("copied"), sem("biased")
            with nc.Block() as block:
                @block.sync
                def _(sp):
                    for k, tile in consts.items():
                        sp.dma_start(tile[:], a[f"const_{k}"][:, :]).then_inc(consts_in, 16)
                    sp.dma_start(window32[:], a["const_window"]).then_inc(raw_in, 16)
                    for k, (source, _) in first.items():
                        sp.dma_start(w[k][:], source).then_inc(consts_in, 16)
                    sp.dma_start(raw_fc[:], a["L1_conv_W_fc"].rearrange("(t p) c -> p t c", p=128)).then_inc(raw_in, 16)
                    sp.dma_start(raw[:, 0, :], a["L1_conv_W_last"]).then_inc(raw_in, 16)
                    for i, k in enumerate(("Wq", "Wk", "Wv", "Wo")):
                        sp.dma_start(raw[:, 1 + i, :], a[f"L2_attn_{k}"]).then_inc(raw_in, 16)
                    for i, k in enumerate(("Wq", "Wk")):
                        sp.dma_start(raw_qkv[:, i, :], a[f"L3_attn_{k}"]).then_inc(raw_in, 16)
                    sp.dma_start(wv[2][:], a["L3_attn_Wv"]).then_inc(raw_in, 16)
                    sp.dma_start(wo[2][:], a["L3_attn_Wo"]).then_inc(raw_in, 16)
                    sp.dma_start(raw_gate[:], a["L2_ffn_gate_weight"]).then_inc(raw_in, 16)
                    sp.dma_start(gate3[:], a["L3_ffn_Ws"]).then_inc(raw_in, 16)
                    sp.dma_start(fc_bias[:], a["L1_conv_b_fc"].rearrange("(o n) -> o n", o=1)).then_inc(raw_in, 16)
                    sp.dma_start(o_bias[:, 0, :], a["L1_conv_b_last"].rearrange("(o n) -> o n", o=1)).then_inc(raw_in, 16)
                    sp.dma_start(o_bias[:, 1, :], a["L3_attn_bo"].rearrange("(o n) -> o n", o=1)).then_inc(raw_in, 16)
                    sp.dma_start(gate3_bias[:], a["L3_ffn_bs"].rearrange("(o n) -> o n", o=1).to_broadcast([128, E3]))\
                        .then_inc(raw_in, 16)
                    sp.dma_start(w1_raw[:], a["L2_ffn_w1"].rearrange("e (k p) d -> p (e k) d", p=128)).then_inc(experts_in, 16)
                    sp.dma_start(w2[:], a["L2_ffn_w2"].rearrange("e d f -> d e f")).then_inc(experts_in, 16)
                    sp.wait_ge(consts_in, 16 * (len(consts) + len(first)))
                    sp.wait_ge(raw_in, 16 * 17)

                @block.tensor
                def _(pe):
                    pe.wait_ge(consts_in, 16 * (len(consts) + len(first)))
                    pe.wait_ge(raw_in, 16 * 17)
                    for t in range(3):
                        nc.tensor.transpose(ps[:, 0, t * 128:(t + 1) * 128], raw_fc[:, t, :], consts["ident"][:])
                    for i in range(4):
                        nc.tensor.transpose(ps[:, 1, i * 128:(i + 1) * 128], raw[:, i, :], consts["ident"][:])
                    nc.tensor.transpose(ps[:, 2, 0:128], raw[:, 4, :], consts["ident"][:])
                    nc.tensor.transpose(ps[:, 3, 0:E2], raw_gate[:], consts["ident"][0:E2, 0:E2]).then_inc(turned, 1)
                    pe.wait_ge(biased, 1)
                    for g in range(8):
                        nc.tensor.matmul(ps[:, 4, g:g + 1], wide_bias[:, g * 128:(g + 1) * 128],
                                         consts["ones"][0:1, 0:1], start=True, stop=True)
                    mm = nc.tensor.matmul(ps[:, 5, 0:128], consts["ones"][0:1, 0:128],
                                          fc_bias[:].rearrange("o (h t d) -> o t h d", h=H, t=3)[:, 2],
                                          start=True, stop=True)
                    mm.then_inc(turned, 1)

                @block.vector
                def _(dve):
                    def repeat(out, heads, scale):
                        part = heads.shape[0]
                        return nc.vector.tensor_scalar(
                            out.rearrange("p (h r d) -> p h r d", h=H, r=4),
                            heads[:, :, None, :].to_broadcast([part, H, 4, D]), scale, None, ALU.mult)

                    dve.wait_ge(turned, 1)
                    nc.vector.tensor_copy(ident16[:], consts["ident"][:])
                    nc.vector.tensor_copy(window[:], window32[:])
                    nc.vector.tensor_copy(fcT[:], ps[:, 0, 0:384]).then_inc(copied, 1)
                    nc.vector.tensor_copy(wo[0][:], ps[:, 1, 0:128])
                    nc.vector.tensor_copy(wv[1][:], ps[:, 1, 384:512])
                    nc.vector.tensor_copy(wo[1][:], ps[:, 2, 0:128])
                    nc.vector.tensor_copy(gate2[:], ps[:, 3, 0:E2])
                    dve.wait_ge(copied, 1)
                    fc = fcT[:].rearrange("p (h t d) -> p t h d", h=H, t=3)
                    bias = fc_bias[:].rearrange("p (h t d) -> p t h d", h=H, t=3)
                    scale = float(D) ** -0.5
                    qk = [(fc[:, 0], fc[:, 1], scale),
                          tuple(ps[:, 1, i:i + 128].rearrange("p (h d) -> p h d", h=H) for i in (128, 256)) + (scale,),
                          tuple(raw_qkv[:, i, :].rearrange("p (h d) -> p h d", h=H) for i in (0, 1)) + (1.0,)]
                    for i, (q, k, s) in enumerate(qk):
                        flat = wqk[i][:].rearrange("p g n -> p (g n)")
                        repeat(flat[:, 0:512], q, s)
                        repeat(flat[:, 512:1024], k, 1.0)
                    nc.vector.tensor_copy(wv[0][:].rearrange("p (h d) -> p h d", h=H), fc[:, 2])
                    repeat(wide_bias[:, 0:512], bias[:, 0], scale)
                    repeat(wide_bias[:, 512:1024], bias[:, 1], 1.0).then_inc(biased, 1)
                    dve.wait_ge(turned, 2)
                    nc.vector.tensor_copy(q_bias[:], ps[:, 4, 0:8])
                    nc.vector.tensor_copy(v_bias[:], ps[:, 5, 0:128])

        ident, ones_row, lo = consts["ident"], consts["ones"], consts["lo_rows"]
        masks = {"ident": ident16, "rows": window, "keep": consts["causal"]}

        spatial_gate(nc, a["x"], w, xf, tokens, consts, ps)
        attention(nc, "softmax", xf, tokens, wqk[0], wv[0], wo[0], ident, q_bias, v_bias, o_bias[:, 0, :], lo,
                  ones_row, masks, ps)
        layer_norm(nc, "norm0", tokens, normed, xf, ident, ps)
        attention(nc, "window", xf, tokens, wqk[1], wv[1], wo[1], ident, None, None, None, lo, ones_row, masks, ps)
        layer_norm(nc, "norm1", tokens, normed, None, ident, ps, gate2)
        route(nc, "route2", E2, K2, S2, None, consts, normed, slots, position, tile_expert, weight2, inverse, ps)

        with ExitStack() as turning:
            w1T = sb("w1T", [128, E2, F], into=turning)
            transposed, taken = sem("w1_turned"), sem("w1_taken")
            with nc.Block() as block:
                @block.tensor
                def _(pe):
                    pe.wait_ge(experts_in, 32)
                    for e in range(E2):
                        if e >= 8:
                            pe.wait_ge(taken, e - 7)
                        for k in range(FC):
                            mm = nc.tensor.transpose(ps[:, e % 8, k * 128:(k + 1) * 128], w1_raw[:, e * FC + k, :], ident[:])
                        mm.then_inc(transposed, 1)

                @block.vector
                def _(dve):
                    for e in range(E2):
                        dve.wait_ge(transposed, e + 1)
                        nc.vector.tensor_copy(w1T[:, e, :], ps[:, e % 8, :]).then_inc(taken, 1)

            sums = w1_raw[:].rearrange("p (e k) d -> p e (k d)", e=E2)
            expert_sums(nc, slots, tile_expert, w1T, sums, consts, ps)
            mix_means(nc, sums, w2, inverse, weight2, tokens, consts, ps)
        experts2.close()

        w1 = sb("w1", [128, E3, F])
        w2 = sb("w2_last", [128, E3, FC, C])
        b1 = sb("b1", [128, E3, F])
        b2 = sb("b2", [128, E3, C])
        with nc.Block() as block:
            @block.sync
            def _(sp):
                sp.dma_start(w1[:], a["L3_ffn_W1"].rearrange("e d f -> d e f")).then_inc(last_in, 16)
                sp.dma_start(w2[:], a["L3_ffn_W2"].rearrange("e (k p) d -> p (e k) d", p=128)
                             .rearrange("p (e k) d -> p e k d", e=E3)).then_inc(last_in, 16)
                for tile, name in ((b1, "L3_ffn_b1"), (b2, "L3_ffn_b2")):
                    flat = a[name].rearrange("(o e) n -> o (e n)", o=1)
                    sp.dma_start(tile[:].rearrange("p e n -> p (e n)"), flat.to_broadcast([128, flat.shape[1]]))\
                        .then_inc(last_in, 16)
        layer_norm(nc, "norm2", tokens, normed, xf, ident, ps)
        attention(nc, "linear", xf, tokens, wqk[2], wv[2], wo[2], ident, None, None, o_bias[:, 1, :], lo, ones_row,
                  masks, ps)
        layer_norm(nc, "norm3", tokens, normed, None, ident, ps, gate3)
        route(nc, "route3", E3, K3, S3, gate3_bias, consts, normed, slots, position, tile_expert[:, 0:S3], weight3, None, ps)
        with nc.Block() as block:
            @block.sync
            def _(sp):
                sp.wait_ge(last_in, 64)
        expert_outputs(nc, slots, outputs, tile_expert, w1, b1, w2, b2, consts, ps)
        gathered = normed
        gather_outputs(nc, outputs, position, weight3, tokens, gathered, out, consts, ps)


def constants():
    import numpy as np

    p = np.arange(128)[:, None]
    row, column = np.arange(128)[:, None], np.arange(N)[None]
    halves = [row + 128 * i - column for i in range(2)]
    window = np.concatenate([np.where((d >= 0) & (d < WINDOW), 0, MASKED) for d in halves], 1)
    causal = np.concatenate([column - (row + 128 * i) >= 0 for i in range(2)], 1)
    rows = p % 64
    return {
        "ident": np.eye(128, dtype=np.float32),
        "group": (p // GROUP == p.T // GROUP).astype(np.float32) / GROUP,
        "before": (p < p.T).astype(np.float32),
        "ones": np.ones((128, 128), np.float32),
        "lo_rows": -np.concatenate([rows // 16 % 2, rows // 32], 1).astype(np.float32),
        "window": window.astype(np.float32),
        "causal": causal.astype(np.float32),
        "index": np.tile(np.arange(E2, dtype=np.float32) - E2, (128, 1)),
        "tile": np.tile(np.arange(S2, dtype=np.float32), (128, 1)),
        "part": (p // E2 == np.arange(128 // E2)[None]).astype(np.float32),
    }


def kernel(**inputs):
    import numpy as np
    import concourse.bacc as bacc
    from concourse.bass_utils import run_bass_kernel_spmd

    nc = bacc.Bacc("TRN2", target_bir_lowering=False, num_devices=1)
    given = {k: np.ascontiguousarray(v) for k, v in inputs.items()}
    given.update({f"const_{k}": v for k, v in constants().items()})
    arrays, tensors = {}, {}
    for name, value in given.items():
        arrays[f"in_{name}"] = value
        tensors[name] = nc.dram_tensor(f"in_{name}", value.shape, mybir.dt.from_np(value.dtype),
                                       kind="ExternalInput").ap()
    out = nc.dram_tensor("out", (IMAGES, C, 16, 16), FP32, kind="ExternalOutput").ap()
    build(nc, tensors, out)
    result = run_bass_kernel_spmd(nc, [arrays], core_ids=[0])
    return result.results[0]["out"]
```

```python
import concourse.bass as bass
from concourse import mybir
from contextlib import ExitStack, contextmanager

FP32 = mybir.dt.float32
FP32R = mybir.dt.float32r
BF16 = mybir.dt.bfloat16
INT32 = mybir.dt.int32
UINT32 = mybir.dt.uint32
ALU = mybir.AluOpType
ACT = mybir.ActivationFunctionType
AX = mybir.AxisListType

C = 128
IMAGES, N = 16, 256
TOKENS = IMAGES * N
TILES = TOKENS // 128
H, D = 8, 16
WINDOW = 64
GROUP = 4
C2 = C // 2
F = 512
FC = F // 128
E2, K2 = 16, 2
E3, K3 = 8, 1
GN_EPS, LN_EPS, LINEAR_EPS = 1e-5, 1e-5, 0.001
MASKED = -1e30


def slot_tiles(experts, taken):
    most = (TOKENS * taken + experts * 127) // 128
    return most + -most % 8


S2, S3 = slot_tiles(E2, K2), slot_tiles(E3, K3)


@contextmanager
def stage(nc, name):
    taken = []
    with ExitStack() as ctx:
        def sb(n, shape, dt=FP32):
            return ctx.enter_context(nc.sbuf_tensor(f"{name}_{n}", shape, dt))

        def sem(n):
            taken.append(ctx.enter_context(nc.semaphore(f"{name}_{n}")))
            return taken[-1]

        yield sb, sem
        with nc.Block() as block:
            @block.gpsimd
            def _(pool):
                for s in taken:
                    pool.sem_clear(s)


def link_on(engine, sem):
    count = [0]

    def link(instruction):
        count[0] += 1
        instruction.then_inc(sem, 1)
        engine.wait_ge(sem, count[0])
    return link


def spatial_gate(nc, x_dram, w, xf, tokens, consts, ps):
    with stage(nc, "gate") as (sb, sem):

        x = sb("x", [128, IMAGES, N])
        xn = sb("xn", [128, IMAGES, N])
        stats = sb("stats", [128, IMAGES, 6])
        small = sb("small", [128, 12, IMAGES])
        mean, dev, square, spread, rstd, peak, total, pooled, gate, summed, vw, halves = (
            small[:, i, :] for i in range(12))
        group_mean = sb("group_mean", [128, IMAGES])
        prob = sb("prob", [128, 2, 2, N])
        weighted = sb("weighted", [128, 2, 2, N])
        wq_wide = sb("wq_wide", [128, 128])
        v_wide = sb("v_wide", [128, 4, 128])
        turned = sb("turned", [128, 3, 128])
        squeezed = sb("squeezed", [C2, IMAGES])
        q_small = sb("q_small", [IMAGES, C2])
        q_exp = sb("q_exp", [IMAGES, C2])
        q_one = sb("q_one", [IMAGES, 3])
        qT = sb("qT", [C2, IMAGES])
        place = sb("place", [128, 2, 2, N])
        gated = sb("gated", [128, 2, 2, N])
        out = sb("out", [128, 2, 2 * N])

        x_in = [sem(f"x_in{i}") for i in range(4)]
        weights_turned = sem("weights_turned")
        weights_ready = sem("weights_ready")
        stats_ready = sem("stats_ready")
        mean_ready = sem("mean_ready")
        grouped = sem("grouped")
        spread_ready = sem("spread_ready")
        var_ready = sem("var_ready")
        std_ready = sem("std_ready")
        xn_ready = sem("xn_ready")
        logits_ready = sem("logits_ready")
        peak_ready = sem("peak_ready")
        prob_ready = sem("prob_ready")
        weighted_ready = sem("weighted_ready")
        pooled_part = sem("pooled_part")
        pooled_ready = sem("pooled_ready")
        small_on_pe = sem("small_on_pe")
        small_on_dve = sem("small_on_dve")
        small_on_act = sem("small_on_act")
        wide_ready = sem("wide_ready")
        place_on_pe = sem("place_on_pe")
        place_ready = sem("place_ready")
        gated_ready = sem("gated_ready")
        out_ready = sem("out_ready")
        xf_ready = sem("xf_ready")
        out_turned = sem("out_turned")
        tokens_ready = sem("tokens_ready")
        chained = sem("chained")

        with nc.Block() as block:
            @block.sync
            def _(sp):
                for i in range(4):
                    sp.dma_start(x[:, 4 * i:4 * i + 4, :],
                                 x_dram[4 * i:4 * i + 4].rearrange("b c h w -> c b (h w)")).then_inc(x_in[i], 16)

            @block.tensor
            def _(pe):
                for i, name in enumerate(("wv_r", "w_up", "wq_l")):
                    rows, cols = w[name].shape
                    mm = nc.tensor.transpose(ps[0:cols, 7, i * 128:i * 128 + rows], w[name][:, :],
                                             consts["ident"][0:rows, 0:rows])
                mm.then_inc(weights_turned, 1)
                pe.wait_ge(mean_ready, 1)
                nc.tensor.matmul(ps[:, 0, 0:IMAGES], consts["group"][:], mean, start=True,
                                 stop=True).then_inc(grouped, 1)
                pe.wait_ge(spread_ready, 1)
                nc.tensor.matmul(ps[:, 0, 0:IMAGES], consts["group"][:], spread, start=True,
                                 stop=True).then_inc(grouped, 1)
                pe.wait_ge(weights_ready, 2)
                for m in range(IMAGES // 2):
                    pe.wait_ge(xn_ready, 2 * m + 2)
                    if m >= 2:
                        pe.wait_ge(prob_ready, m - 1)
                    nc.tensor.matmul(ps[:, 1 + m % 2, :], wq_wide[:],
                                     xn[:, 2 * m:2 * m + 2, :].rearrange("p b n -> p (b n)"),
                                     start=True, stop=True).then_inc(logits_ready, 1)
                pe.wait_ge(pooled_ready, 1)
                nc.tensor.matmul(ps[0:C2, 0, 0:IMAGES], turned[:, 0, 0:C2], pooled, start=True,
                                 stop=True).then_inc(small_on_pe, 1)
                pe.wait_ge(small_on_dve, 1)
                nc.tensor.matmul(ps[:, 0, 32:32 + IMAGES], turned[0:C2, 1, :], squeezed[:], start=True,
                                 stop=True).then_inc(small_on_pe, 1)
                pe.wait_ge(small_on_dve, 2)
                nc.tensor.matmul(ps[0:IMAGES, 3, 0:C2], summed, turned[:, 2, 0:C2], start=True,
                                 stop=True).then_inc(small_on_pe, 1)
                pe.wait_ge(small_on_dve, 4)
                nc.tensor.transpose(ps[0:C2, 4, 0:IMAGES], q_small[:], consts["ident"][0:IMAGES, 0:IMAGES])\
                    .then_inc(small_on_pe, 1)
                pe.wait_ge(small_on_dve, 5)
                nc.tensor.matmul(ps[:, 3, 0:IMAGES], w["wv_l"][:, :], qT[:], start=True,
                                 stop=True).then_inc(small_on_pe, 1)

                def turn_out(m):
                    pe.wait_ge(out_ready, m + 1)
                    if m >= 2:
                        pe.wait_ge(tokens_ready, m - 1)
                    for a in range(4):
                        mm = nc.tensor.transpose(ps[:, 5 + m % 2, a * 128:(a + 1) * 128],
                                                 out[:, m % 2, a * 128:(a + 1) * 128], consts["ident"][:])
                    mm.then_inc(out_turned, 1)

                for m in range(IMAGES // 2):
                    pe.wait_ge(wide_ready, 2 * m + 2)
                    if m >= 2:
                        pe.wait_ge(place_ready, m - 1)
                    for a in range(2):
                        b = 2 * m + a
                        mm = nc.tensor.matmul(ps[:, 1 + m % 2, a * N:(a + 1) * N], v_wide[:, b % 4, :], xn[:, b, :],
                                              start=True, stop=True)
                    mm.then_inc(place_on_pe, 1)
                    if m >= 1:
                        turn_out(m - 1)
                turn_out(IMAGES // 2 - 1)

            @block.scalar
            def _(act):
                act.wait_ge(var_ready, 1)
                nc.scalar.activation(square, dev, ACT.Sqrt).then_inc(std_ready, 1)
                for m in range(IMAGES // 2):
                    act.wait_ge(peak_ready, m + 1)
                    if m >= 2:
                        act.wait_ge(weighted_ready, m - 1)
                    for a in range(2):
                        b = 2 * m + a
                        last = nc.scalar.activation(prob[:, m % 2, a, :], ps[:, 1 + m % 2, a * N:(a + 1) * N], ACT.Exp,
                                                    bias=peak[:, b:b + 1], accum_out=total[:, b:b + 1])
                    last.then_inc(prob_ready, 1)
                act.wait_ge(small_on_pe, 2)
                nc.scalar.activation(gate, ps[:, 0, 32:32 + IMAGES], ACT.Sigmoid).then_inc(small_on_act, 1)
                act.wait_ge(small_on_dve, 3)
                nc.scalar.activation(q_exp[:], ps[0:IMAGES, 3, 0:C2], ACT.Exp, bias=q_one[:, 0:1],
                                     accum_out=q_one[:, 1:2]).then_inc(small_on_act, 1)
                for m in range(IMAGES // 2):
                    act.wait_ge(place_on_pe, m + 1)
                    if m >= 2:
                        act.wait_ge(gated_ready, m - 1)
                    nc.scalar.activation(place[:, m % 2].rearrange("p a n -> p (a n)"), ps[:, 1 + m % 2, :],
                                         ACT.Sigmoid).then_inc(place_ready, 1)
                    act.wait_ge(out_ready, m + 1)
                    nc.scalar.activation(xf[:, 2 * m * N:(2 * m + 2) * N], out[:, m % 2, :],
                                         ACT.Copy).then_inc(xf_ready, 1)
                    if m >= 1:
                        act.wait_ge(out_turned, m)
                        nc.scalar.activation(tokens[:, 4 * m - 4:4 * m, :].rearrange("p a c -> p (a c)"),
                                             ps[:, 5 + (m - 1) % 2, :], ACT.Copy).then_inc(tokens_ready, 1)
                m = IMAGES // 2
                act.wait_ge(out_turned, m)
                nc.scalar.activation(tokens[:, 4 * m - 4:4 * m, :].rearrange("p a c -> p (a c)"),
                                     ps[:, 5 + (m - 1) % 2, :], ACT.Copy).then_inc(tokens_ready, 1)

            @block.gpsimd
            def _(pool):
                for m in range(IMAGES // 2):
                    pool.wait_ge(prob_ready, m + 1)
                    if m >= 2:
                        pool.wait_ge(pooled_part, m - 1)
                    nc.gpsimd.tensor_tensor(weighted[:, m % 2], prob[:, m % 2], xn[:, 2 * m:2 * m + 2, :],
                                            ALU.mult).then_inc(weighted_ready, 1)
                for m in range(IMAGES // 2):
                    pool.wait_ge(gated_ready, m + 1)
                    if m >= 2:
                        pool.wait_ge(xf_ready, m - 1)
                        pool.wait_ge(out_turned, m - 1)
                    nc.gpsimd.tensor_tensor(out[:, m % 2, :], gated[:, m % 2].rearrange("p a n -> p (a n)"),
                                            x[:, 2 * m:2 * m + 2, :].rearrange("p b n -> p (b n)"),
                                            ALU.add).then_inc(out_ready, 1)

            @block.vector
            def _(dve):
                link = link_on(dve, chained)
                dve.wait_ge(weights_turned, 1)
                nc.vector.tensor_copy(turned[:, 0, 0:C2], ps[:, 7, 0:C2])
                nc.vector.tensor_copy(turned[0:C2, 1, :], ps[0:C2, 7, 128:256])
                nc.vector.tensor_copy(turned[:, 2, 0:C2], ps[:, 7, 256:256 + C2]).then_inc(weights_ready, 1)
                nc.vector.tensor_copy(wq_wide[:], w["wq_r"][:, 0:1].to_broadcast([128, 128])).then_inc(weights_ready, 1)
                for b in range(IMAGES):
                    if b % 4 == 0:
                        dve.wait_ge(x_in[b // 4], 16)
                    last = nc.vector.bn_stats(stats[:, b, :], x[:, b, :])
                last.then_inc(stats_ready, 1)
                dve.wait_ge(stats_ready, 1)
                even, odd = stats[:, :, 1], stats[:, :, 4]
                link(nc.vector.tensor_tensor(mean, even, odd, ALU.add))
                link(nc.vector.tensor_scalar(mean, mean, 0.5, None, ALU.mult))
                last = nc.vector.tensor_tensor(dev, even, odd, ALU.subtract)
                last.then_inc(mean_ready, 1)
                dve.wait_ge(mean_ready, 1)
                link(nc.vector.tensor_tensor(square, dev, dev, ALU.mult))
                link(nc.vector.tensor_scalar(square, square, N / 4.0, None, ALU.mult))
                link(nc.vector.tensor_tensor(square, square, stats[:, :, 2], ALU.add))
                link(nc.vector.tensor_tensor(square, square, stats[:, :, 5], ALU.add))
                dve.wait_ge(grouped, 1)
                link(nc.vector.tensor_copy(group_mean[:], ps[:, 0, 0:IMAGES]))
                link(nc.vector.tensor_tensor(halves, mean, group_mean[:], ALU.subtract))
                link(nc.vector.tensor_tensor(spread, halves, halves, ALU.mult))
                link(nc.vector.tensor_scalar(spread, spread, float(N), None, ALU.mult))
                nc.vector.tensor_tensor(spread, spread, square, ALU.add).then_inc(spread_ready, 1)
                dve.wait_ge(grouped, 2)
                nc.vector.tensor_scalar(dev, ps[:, 0, 0:IMAGES], 1.0 / N, GN_EPS, ALU.mult,
                                        ALU.add).then_inc(var_ready, 1)
                dve.wait_ge(std_ready, 1)
                link(nc.vector.reciprocal(rstd, square))
                for b in range(IMAGES):
                    nc.vector.tensor_scalar(xn[:, b, :], x[:, b, :], group_mean[:, b:b + 1], rstd[:, b:b + 1],
                                            ALU.subtract, ALU.mult).then_inc(xn_ready, 1)
                for m in range(IMAGES // 2 + 2):
                    if m < IMAGES // 2:
                        dve.wait_ge(logits_ready, m + 1)
                        nc.vector.tensor_reduce(out=peak[:, 2 * m:2 * m + 2],
                                                in_=ps[:, 1 + m % 2, :].rearrange("p (b n) -> p b n", b=2),
                                                axis=AX.X, op=ALU.max, negate=True).then_inc(peak_ready, 1)
                    if m >= 2:
                        dve.wait_ge(weighted_ready, m - 1)
                        nc.vector.tensor_reduce(out=pooled[:, 2 * m - 4:2 * m - 2], in_=weighted[:, (m - 2) % 2],
                                                axis=AX.X, op=ALU.add).then_inc(pooled_part, 1)
                dve.wait_ge(prob_ready, IMAGES // 2)
                dve.wait_ge(pooled_part, IMAGES // 2)
                link(nc.vector.reciprocal(peak, total))
                nc.vector.tensor_tensor(pooled, pooled, peak, ALU.mult).then_inc(pooled_ready, 1)
                dve.wait_ge(small_on_pe, 1)
                nc.vector.tensor_copy(squeezed[:], ps[0:C2, 0, 0:IMAGES]).then_inc(small_on_dve, 1)
                dve.wait_ge(small_on_act, 1)
                link(nc.vector.tensor_tensor(summed, halves, rstd, ALU.mult))
                nc.vector.tensor_tensor(summed, summed, gate, ALU.mult).then_inc(small_on_dve, 1)
                dve.wait_ge(small_on_pe, 3)
                nc.vector.tensor_reduce(out=q_one[:, 0:1], in_=ps[0:IMAGES, 3, 0:C2], axis=AX.X, op=ALU.max,
                                        negate=True).then_inc(small_on_dve, 1)
                dve.wait_ge(small_on_act, 2)
                link(nc.vector.reciprocal(q_one[:, 2:3], q_one[:, 1:2]))
                nc.vector.tensor_scalar(q_small[:], q_exp[:], q_one[:, 2:3], None, ALU.mult).then_inc(small_on_dve, 1)
                dve.wait_ge(small_on_pe, 4)
                nc.vector.tensor_copy(qT[:], ps[0:C2, 4, 0:IMAGES]).then_inc(small_on_dve, 1)
                dve.wait_ge(small_on_pe, 5)
                link(nc.vector.tensor_tensor(vw, ps[:, 3, 0:IMAGES], gate, ALU.mult))

                def widen(b):
                    if b >= 4:
                        dve.wait_ge(place_on_pe, (b - 4) // 2 + 1)
                    nc.vector.tensor_copy(v_wide[:, b % 4, :], vw[:, b:b + 1].to_broadcast([128, 128]))\
                        .then_inc(wide_ready, 1)

                for b in range(4):
                    widen(b)
                for m in range(IMAGES // 2):
                    dve.wait_ge(place_ready, m + 1)
                    if m >= 2:
                        dve.wait_ge(out_ready, m - 1)
                    for a in range(2):
                        b = 2 * m + a
                        last = nc.vector.scalar_tensor_tensor(out=gated[:, m % 2, a, :], in0=xn[:, b, :],
                                                              scalar=gate[:, b:b + 1], in1=place[:, m % 2, a, :],
                                                              op0=ALU.mult, op1=ALU.mult)
                    last.then_inc(gated_ready, 1)
                    for b in (2 * m + 4, 2 * m + 5):
                        if b < IMAGES:
                            widen(b)


def attention(nc, mode, src, tokens, wqk, wv, wo, ident, q_bias, v_bias, o_bias, lo_rows, ones_row, mask, ps):
    softmax = mode != "linear"
    with stage(nc, mode) as (sb, sem):

        xs = sb("xs", [128, 2, N])
        full = sb("full", [128, 2, 2, N])
        high = sb("high", [128, 2, 2, N], FP32R)
        stack = sb("stack", [128, 2, 8, N], FP32R)
        vaug = sb("vaug", [128, 2, 2, H, 32])
        negmax = sb("negmax", [128, 2, 2])
        prob = sb("prob", [128, 2, 2, N])
        probT = sb("probT", [128, 2, 2, N])
        heads = sb("heads", [128, 2, 2, 128])
        recip = sb("recip", [128, 2, 2, 4])
        normed = sb("normed", [128, 2, 2, 4, 16])
        normedT = sb("normedT", [128, 2, 128])

        xs_ready = [sem(f"xs_ready{u}") for u in range(2)]
        qk_projected = sem("qk_projected")
        full_ready = sem("full_ready")
        high_ready = sem("high_ready")
        stack_ready = sem("stack_ready")
        v_projected = sem("v_projected")
        vaug_ready = sem("vaug_ready")
        vaug_set = sem("vaug_set")
        scored = sem("scored")
        max_ready = sem("max_ready")
        exp_ready = sem("exp_ready")
        transposed = sem("transposed")
        even_copied = sem("even_copied")
        odd_copied = sem("odd_copied")
        weighted = sem("weighted")
        heads_ready = sem("heads_ready")
        heads_turned = sem("heads_turned")
        recip_ready = sem("recip_ready")
        normed_ready = sem("normed_ready")
        normed_turned = sem("normed_turned")
        normedT_ready = sem("normedT_ready")
        out_projected = sem("out_projected")
        tokens_ready = sem("tokens_ready")

        PROJ, SCORE, TURN, HEADS, MISC = 0, 2, 4, 6, 7

        def images(step):
            def run(engine):
                step(0, 0, True, False)
                with engine.Fori(0, (IMAGES - 2) // 2) as i:
                    step(2 * i + 1, 1, False, False)
                    step(2 * i + 2, 0, False, False)
                step(IMAGES - 1, 1, False, True)
            return run

        with nc.Block() as block:
            @block.gpsimd
            def _(pool):
                nc.gpsimd.memset(vaug[:], 0.0).then_inc(vaug_set, 1)
                pool.wait_ge(vaug_set, 1)
                nc.gpsimd.memset(vaug[:, :, :, :, 16:17], 1.0).then_inc(vaug_set, 1)

            @block.sync
            def _(sp):
                def load(n, u, fresh):
                    at = n * N if fresh else sp.snap(n * N)
                    if not fresh:
                        sp.wait_ge(qk_projected, 4 * n - 4)
                    sp.dma_start(xs[:, u, :], src[:, bass.ds(at, N)]).then_inc(xs_ready[u], 16)

                load(0, 0, True)
                load(1, 1, True)

                def step(n, u, first, last):
                    if not first and not last:
                        load(n + 1, 1 - u, False)

                images(step)(sp)

            @block.tensor
            def _(pe):
                def project(n, u, fresh, j):
                    pe.wait_ge(xs_ready[u], 8 * n + 16 - 8 * u)
                    if not (fresh and j < 2):
                        pe.wait_ge(full_ready, 4 * n + j - 1)
                    for g in range(2):
                        mm = nc.tensor.matmul(ps[:, PROJ + j % 2, g * N:(g + 1) * N], wqk[:, 2 * j + g, :],
                                              xs[:, u, :], start=True, stop=True)
                    mm.then_inc(qk_projected, 1)

                def project_v(n, u, fresh):
                    pe.wait_ge(xs_ready[u], 8 * n + 16 - 8 * u)
                    if not fresh:
                        pe.wait_ge(vaug_ready, n)
                        pe.wait_ge(tokens_ready, n - 1)
                    elif n:
                        pe.wait_ge(vaug_ready, n)
                    for a in range(2):
                        mm = nc.tensor.matmul(ps[:, MISC, a * 128:(a + 1) * 128], xs[:, u, a * 128:(a + 1) * 128],
                                              wv[:], start=True, stop=True)
                    mm.then_inc(v_projected, 1)

                def score(n, u, fresh, k):
                    if k == 0:
                        pe.wait_ge(stack_ready, 4 * n + 4)
                    if not (fresh and k < 2):
                        if softmax:
                            pe.wait_ge(exp_ready, 8 * n + k - 1)
                        else:
                            pe.wait_ge(even_copied, 8 * n + k - 1)
                    rows = slice(64 * (k % 2), 64 * (k % 2) + 64)
                    q, key = stack[rows, u, k // 2, :], stack[rows, u, 4 + k // 2, :]
                    one, other = (q, key) if softmax else (key, q)
                    for a in range(2):
                        if mode == "window":
                            nc.tensor.matmul(ps[:, SCORE + k % 2, a * N:(a + 1) * N], mask["ident"][:],
                                             mask["rows"][:, a * N:(a + 1) * N], start=True, stop=False)
                        mm = nc.tensor.matmul(ps[:, SCORE + k % 2, a * N:(a + 1) * N],
                                              one[:, a * 128:(a + 1) * 128], other,
                                              start=mode != "window", stop=True)
                    mm.then_inc(scored, 1)

                def turn(n, fresh, k):
                    pe.wait_ge(exp_ready, 8 * n + k + 1)
                    if not (fresh and k < 2):
                        pe.wait_ge(odd_copied if k % 2 else even_copied, 4 * n + k // 2)
                    for b in range(2):
                        for a in range(2):
                            mm = nc.tensor.transpose(ps[:, TURN + k % 2, (2 * b + a) * 128:(2 * b + a + 1) * 128],
                                                     prob[:, k % 2, a, b * 128:(b + 1) * 128], ident[:])
                    mm.then_inc(transposed, 1)

                def weigh(n, u, fresh, k):
                    if k == 0:
                        pe.wait_ge(vaug_ready, n + 1)
                        if not fresh:
                            pe.wait_ge(heads_ready, n)
                    if softmax:
                        pe.wait_ge(odd_copied if k % 2 else even_copied, 4 * n + k // 2 + 1)
                        keys = probT
                    else:
                        pe.wait_ge(even_copied, 8 * n + k + 1)
                        keys = prob
                    r, c = 32 * (k % 4), (k // 4) * N
                    for b in range(2):
                        mm = nc.tensor.matmul(ps[r:r + 32, HEADS, c:c + N], vaug[:, u, b, k, :],
                                              keys[:, k % 2, b, :], start=b == 0, stop=b == 1)
                    mm.then_inc(weighted, 1)

                def turn_heads(n, last):
                    pe.wait_ge(heads_ready, n + 1)
                    pe.wait_ge(vaug_ready, IMAGES if last else n + 2)
                    if last:
                        pe.wait_ge(tokens_ready, n)
                    for g in range(2):
                        for a in range(2):
                            mm = nc.tensor.transpose(ps[:, MISC, (2 * g + a) * 128:(2 * g + a + 1) * 128],
                                                     heads[:, g, a, :], ident[:])
                    mm.then_inc(heads_turned, 1)

                def turn_normed(n):
                    pe.wait_ge(normed_ready, 2 * n + 2)
                    for a in range(2):
                        mm = nc.tensor.transpose(ps[:, MISC, a * 128:(a + 1) * 128],
                                                 normed[:, a].rearrange("p g h d -> p (g h d)"), ident[:])
                    mm.then_inc(normed_turned, 1)

                def project_out(n):
                    pe.wait_ge(normedT_ready, n + 1)
                    for a in range(2):
                        mm = nc.tensor.matmul(ps[:, MISC, a * 128:(a + 1) * 128], normedT[:, a, :], wo[:],
                                              start=True, stop=o_bias is None)
                        if o_bias is not None:
                            mm = nc.tensor.matmul(ps[:, MISC, a * 128:(a + 1) * 128], ones_row[0:1, 0:128],
                                                  o_bias[0:1, :], start=False, stop=True)
                    mm.then_inc(out_projected, 1)

                for j in range(3):
                    project(0, 0, True, j)
                project_v(0, 0, True)
                project(0, 0, True, 3)

                def step(n, u, first, last):
                    for k in range(8):
                        score(n, u, first, k)
                        if not first:
                            if k == 0:
                                turn_heads(n - 1, False)
                            if k == 2:
                                turn_normed(n - 1)
                            if k == 4:
                                project_out(n - 1)
                        if not last:
                            if k in (1, 3, 5, 7):
                                project(n + 1, 1 - u, False, k // 2)
                            if k == 6:
                                project_v(n + 1, 1 - u, first)
                        if softmax and k >= 1:
                            turn(n, first, k - 1)
                        if k >= 2:
                            weigh(n, u, first, k - 2)
                    if softmax:
                        turn(n, first, 7)
                    weigh(n, u, first, 6)
                    weigh(n, u, first, 7)

                images(step)(pe)
                turn_heads(IMAGES - 1, True)
                turn_normed(IMAGES - 1)
                project_out(IMAGES - 1)

            @block.scalar
            def _(act):
                def evacuate(n, fresh, j):
                    act.wait_ge(qk_projected, 4 * n + j + 1)
                    if not (fresh and j < 2):
                        act.wait_ge(stack_ready, 4 * n + j - 1)
                    if q_bias is None:
                        nc.scalar.activation(full[:, j % 2].rearrange("p g n -> p (g n)"), ps[:, PROJ + j % 2, :],
                                             ACT.Copy).then_inc(full_ready, 1)
                    else:
                        for g in range(2):
                            last = nc.scalar.activation(full[:, j % 2, g, :], ps[:, PROJ + j % 2, g * N:(g + 1) * N],
                                                        ACT.Identity, bias=q_bias[:, 2 * j + g:2 * j + g + 1])
                        last.then_inc(full_ready, 1)

                def round_high(n, fresh, j):
                    act.wait_ge(full_ready, 4 * n + j + 1)
                    if not (fresh and j < 2):
                        act.wait_ge(stack_ready, 4 * n + j - 1)
                    nc.scalar.activation(high[:, j % 2], full[:, j % 2], ACT.Copy).then_inc(high_ready, 1)

                def exponential(n, fresh, k):
                    act.wait_ge(max_ready, 8 * n + k + 1)
                    if not (fresh and k < 2):
                        act.wait_ge(transposed, 8 * n + k - 1)
                    for g in range(2):
                        last = nc.scalar.activation(prob[:, k % 2, g, :], ps[:, SCORE + k % 2, g * N:(g + 1) * N],
                                                    ACT.Exp, bias=negmax[:, k % 2, g:g + 1])
                    last.then_inc(exp_ready, 1)

                def copy_odd(n, fresh, k):
                    act.wait_ge(transposed, 8 * n + k + 1)
                    if not (fresh and k < 2):
                        act.wait_ge(weighted, 8 * n + k - 1)
                    nc.scalar.activation(probT[:, 1].rearrange("p b n -> p (b n)"), ps[:, TURN + 1, :],
                                         ACT.Copy).then_inc(odd_copied, 1)

                def take_heads(n, fresh):
                    act.wait_ge(weighted, 8 * n + 8)
                    if not fresh:
                        act.wait_ge(heads_turned, n)
                    nc.scalar.activation(heads[:].rearrange("p g a n -> p (g a n)"), ps[:, HEADS, :],
                                         ACT.Copy).then_inc(heads_ready, 1)

                def take_normed(n, fresh):
                    act.wait_ge(normed_turned, n + 1)
                    if not fresh:
                        act.wait_ge(out_projected, n)
                    nc.scalar.activation(normedT[:].rearrange("p a n -> p (a n)"), ps[:, MISC, 0:N],
                                         ACT.Copy).then_inc(normedT_ready, 1)

                for j in range(4):
                    if softmax:
                        evacuate(0, True, j)
                    else:
                        round_high(0, True, j)

                def step(n, u, first, last):
                    for k in range(8):
                        if softmax:
                            exponential(n, first, k)
                        if not first and k == 3:
                            take_normed(n - 1, False)
                        if not last and k in (1, 3, 5, 7):
                            if softmax:
                                evacuate(n + 1, False, k // 2)
                            else:
                                round_high(n + 1, False, k // 2)
                        if softmax and k in (2, 4, 6):
                            copy_odd(n, first, k - 1)
                    if softmax:
                        copy_odd(n, first, 7)
                    take_heads(n, first)

                images(step)(act)
                take_normed(IMAGES - 1, False)

            @block.vector
            def _(dve):
                def evacuate(n, fresh, j):
                    dve.wait_ge(qk_projected, 4 * n + j + 1)
                    if not (fresh and j < 2):
                        dve.wait_ge(stack_ready, 4 * n + j - 1)
                    nc.vector.tensor_scalar(full[:, j % 2].rearrange("p g n -> p (g n)"), ps[:, PROJ + j % 2, :],
                                            0.0, LINEAR_EPS, ALU.max, ALU.add).then_inc(full_ready, 1)

                def round_high(n, j):
                    dve.wait_ge(full_ready, 4 * n + j + 1)
                    nc.vector.tensor_copy(high[:, j % 2], full[:, j % 2]).then_inc(high_ready, 1)

                def split(n, u, fresh, j):
                    dve.wait_ge(high_ready, 4 * n + j + 1)
                    if not fresh and j == 0:
                        dve.wait_ge(scored, 8 * n - 8)
                    nc.vector.scalar_tensor_tensor(
                        out=stack[:, u, 2 * j:2 * j + 2, :], in0=high[:, j % 2].bitcast(FP32),
                        scalar=lo_rows[:, j // 2:j // 2 + 1], in1=full[:, j % 2], op0=ALU.mult,
                        op1=ALU.add).then_inc(stack_ready, 1)

                def take_values(n, u, fresh):
                    dve.wait_ge(v_projected, n + 1)
                    if fresh and n == 0:
                        dve.wait_ge(vaug_set, 2)
                    if not fresh:
                        dve.wait_ge(weighted, 8 * n - 8)
                    for a in range(2):
                        out = vaug[:, u, a, :, 0:16]
                        got = ps[:, MISC, a * 128:(a + 1) * 128].rearrange("p (h d) -> p h d", d=D)
                        if v_bias is None:
                            last = nc.vector.tensor_copy(out, got)
                        else:
                            last = nc.vector.tensor_tensor(out, got, v_bias[:].rearrange("p (h d) -> p h d", d=D),
                                                           ALU.add)
                    last.then_inc(vaug_ready, 1)

                def maximum(n, fresh, k):
                    dve.wait_ge(scored, 8 * n + k + 1)
                    if not (fresh and k < 2):
                        dve.wait_ge(exp_ready, 8 * n + k - 1)
                    nc.vector.tensor_reduce(out=negmax[:, k % 2, :],
                                            in_=ps[:, SCORE + k % 2, :].rearrange("p (g n) -> p g n", n=N),
                                            axis=AX.X, op=ALU.max, negate=True).then_inc(max_ready, 1)

                def copy_even(n, fresh, k):
                    dve.wait_ge(transposed, 8 * n + k + 1)
                    if not (fresh and k < 2):
                        dve.wait_ge(weighted, 8 * n + k - 1)
                    nc.vector.tensor_copy(probT[:, 0].rearrange("p b n -> p (b n)"),
                                          ps[:, TURN, :]).then_inc(even_copied, 1)

                def causal(n, fresh, k):
                    dve.wait_ge(scored, 8 * n + k + 1)
                    if not (fresh and k < 2):
                        dve.wait_ge(weighted, 8 * n + k - 1)
                    nc.vector.tensor_tensor(prob[:, k % 2].rearrange("p g n -> p (g n)"), ps[:, SCORE + k % 2, :],
                                            mask["keep"][:], ALU.mult).then_inc(even_copied, 1)

                def normalise(n, fresh):
                    dve.wait_ge(heads_turned, n + 1)
                    turned = ps[:, MISC, :].rearrange("p (g a h d) -> p g a h d", g=2, a=2, h=4)
                    for g in range(2):
                        nc.vector.reciprocal(recip[:, g], turned[:, g, :, :, 16]).then_inc(recip_ready, 1)
                    dve.wait_ge(recip_ready, 2 * n + 2)
                    if not fresh:
                        dve.wait_ge(normed_turned, n)
                    for a in range(2):
                        nc.vector.tensor_tensor(
                            normed[:, a], turned[:, :, a, :, 0:16],
                            recip[:, :, a, :, None].to_broadcast([128, 2, 4, 16]), ALU.mult).then_inc(normed_ready, 1)

                def add_out(n):
                    dve.wait_ge(out_projected, n + 1)
                    at = tokens[:, bass.ds(2 * n, 2), :]
                    nc.vector.tensor_tensor(at, at, ps[:, MISC, 0:N].rearrange("p (a c) -> p a c", a=2),
                                            ALU.add).then_inc(tokens_ready, 1)

                for j in range(4):
                    if not softmax:
                        evacuate(0, True, j)
                    else:
                        round_high(0, j)
                    split(0, 0, True, j)
                take_values(0, 0, True)

                def step(n, u, first, last):
                    for k in range(8):
                        if softmax:
                            maximum(n, first, k)
                        else:
                            causal(n, first, k)
                        if not first:
                            if k == 1:
                                normalise(n - 1, False)
                            if k == 5:
                                add_out(n - 1)
                        if not last:
                            if k in (1, 3, 5, 7) and not softmax:
                                evacuate(n + 1, False, k // 2)
                            if k in (3, 5, 7):
                                split(n + 1, 1 - u, first, k // 2 - 1)
                            if k in (2, 4, 6) and softmax:
                                round_high(n + 1, k // 2 - 1)
                            if k == 7:
                                take_values(n + 1, 1 - u, first)
                        if softmax and k in (1, 3, 5, 7):
                            copy_even(n, first, k - 1)
                    if not last:
                        if softmax:
                            round_high(n + 1, 3)
                        split(n + 1, 1 - u, first, 3)

                images(step)(dve)
                normalise(IMAGES - 1, False)
                add_out(IMAGES - 1)


def layer_norm(nc, name, tokens, normed, xf, ident, ps, gate=None):
    CHUNK = 8
    CHUNKS = TILES // CHUNK
    with stage(nc, name) as (sb, sem):

        squares = sb("squares", [128, 2, CHUNK, C])
        stat = sb("stat", [128, 4, TILES])
        mean, var, std, rstd = (stat[:, i, :] for i in range(4))
        turned_sb = sb("turned", [128, 2, CHUNK * 128]) if gate is not None else None

        mean_ready, centred, squared, var_ready, std_ready, rstd_ready, normed_ready, turned, taken, logits_ready = (
            sem(n) for n in ("mean_ready", "centred", "squared", "var_ready", "std_ready", "rstd_ready",
                             "normed_ready", "turned", "taken", "logits_ready"))
        chained = sem("chained")

        def part(c):
            return slice(c * CHUNK, (c + 1) * CHUNK)

        with nc.Block() as block:
            @block.vector
            def _(dve):
                link = link_on(dve, chained)

                def centre(c):
                    link(nc.vector.tensor_reduce(out=mean[:, part(c)], in_=tokens[:, part(c), :], axis=AX.X,
                                                 op=ALU.add))
                    link(nc.vector.tensor_scalar(mean[:, part(c)], mean[:, part(c)], 1.0 / C, None, ALU.mult))
                    nc.vector.tensor_tensor(normed[:, part(c), :], tokens[:, part(c), :],
                                            mean[:, part(c), None].to_broadcast([128, CHUNK, C]),
                                            ALU.subtract).then_inc(centred, 1)

                def variance(c):
                    dve.wait_ge(squared, c + 1)
                    link(nc.vector.tensor_reduce(out=var[:, part(c)], in_=squares[:, c % 2], axis=AX.X, op=ALU.add))
                    nc.vector.tensor_scalar(var[:, part(c)], var[:, part(c)], 1.0 / C, LN_EPS, ALU.mult,
                                            ALU.add).then_inc(var_ready, 1)

                def scale(c):
                    dve.wait_ge(std_ready, c + 1)
                    link(nc.vector.reciprocal(rstd[:, part(c)], std[:, part(c)]))
                    nc.vector.tensor_tensor(normed[:, part(c), :], normed[:, part(c), :],
                                            rstd[:, part(c), None].to_broadcast([128, CHUNK, C]),
                                            ALU.mult).then_inc(normed_ready, 1)

                for c in range(CHUNKS + 2):
                    if c < CHUNKS:
                        centre(c)
                    if 1 <= c <= CHUNKS:
                        variance(c - 1)
                    if c >= 2:
                        scale(c - 2)

            @block.scalar
            def _(act):
                def take(c):
                    act.wait_ge(turned, c + 1)
                    if xf is not None:
                        out = xf[:, c * CHUNK * 128:(c + 1) * CHUNK * 128]
                    else:
                        if c >= 2:
                            act.wait_ge(logits_ready, c - 1)
                        out = turned_sb[:, c % 2, :]
                    nc.scalar.activation(out, ps[:, 2 * (c % 2):2 * (c % 2) + 2, :].rearrange("p a n -> p (a n)"),
                                         ACT.Copy).then_inc(taken, 1)

                for c in range(CHUNKS + 3):
                    if c < CHUNKS:
                        act.wait_ge(centred, c + 1)
                        if c >= 2:
                            act.wait_ge(var_ready, c - 1)
                        nc.scalar.activation(squares[:, c % 2], normed[:, part(c), :], ACT.Square).then_inc(squared, 1)
                    if 1 <= c <= CHUNKS:
                        act.wait_ge(var_ready, c)
                        nc.scalar.activation(std[:, part(c - 1)], var[:, part(c - 1)], ACT.Sqrt).then_inc(std_ready, 1)
                    if c >= 3:
                        take(c - 3)

            @block.tensor
            def _(pe):
                def logits(c):
                    pe.wait_ge(taken, c + 1)
                    experts = gate.shape[1]
                    for a in range(CHUNK):
                        at = (c * CHUNK + a) * experts
                        mm = nc.tensor.matmul(ps[:, 7, at:at + experts], turned_sb[:, c % 2, a * 128:(a + 1) * 128],
                                              gate[:, :], start=True, stop=True)
                    mm.then_inc(logits_ready, 1)

                for c in range(CHUNKS):
                    pe.wait_ge(normed_ready, c + 1)
                    if c >= 2:
                        pe.wait_ge(taken, c - 1)
                    for a in range(CHUNK):
                        mm = nc.tensor.transpose(ps[:, 2 * (c % 2) + a // 4, a % 4 * 128:(a % 4 + 1) * 128],
                                                 normed[:, c * CHUNK + a, :], ident[:])
                    mm.then_inc(turned, 1)
                    if gate is not None and c >= 1:
                        logits(c - 1)
                if gate is not None:
                    logits(CHUNKS - 1)


def route(nc, name, experts, taken, tiles, bias, consts, normed, slots, position, tile_expert, weight, counts,
          tile_choice, ps):
    with stage(nc, name) as (sb, sem):

        wide = [128, TILES, experts]
        logits = sb("logits", wide)
        chosen = [sb(f"chosen{k}", wide) for k in range(taken)]
        scratch = sb("scratch", wide)
        select = sb("select", wide) if taken > 1 else chosen[0]
        running = [sb(f"running{i}", wide) for i in range(2)]
        top = sb("top", [128, taken, TILES])
        first = sb("first", [128, TILES])
        ends = sb("ends", [128, 6, experts])
        ends_int = sb("ends_int", [128, experts], INT32)
        slot_of = sb("slot_of", [128, TILES])
        past = sb("past", [128, tiles, experts])
        expert_of = sb("expert_of", [128, tiles])
        own_expert = sb("own_expert", [128, 1])
        zero = sb("zero", [128, 4, C])

        chosen_ready = sem("chosen_ready")
        counted = sem("counted")
        gap_ready = sem("gap_ready")
        exp_ready = sem("exp_ready")
        zero_set = sem("zero_set")
        cleared = sem("cleared")
        placed = sem("placed")
        scattered = sem("scattered")
        chained = sem("chained")

        def over(ap, shape=None):
            return ap.to_broadcast(shape or wide)

        with nc.Block() as block:
            @block.tensor
            def _(pe):
                pe.wait_ge(chosen_ready, 1)
                flat = select[:].rearrange("p t e -> p (t e)")
                nc.tensor.matmul(ps[:, 0, 0:TILES * experts], consts["before"][:], flat, start=True,
                                 stop=True).then_inc(counted, 1)
                nc.tensor.matmul(ps[:, 1, 0:TILES * experts], consts["ones"][:], flat, start=True,
                                 stop=True).then_inc(counted, 1)

            @block.scalar
            def _(act):
                act.wait_ge(gap_ready, 1)
                if taken == 2:
                    nc.scalar.activation(first[:], first[:], ACT.Exp).then_inc(exp_ready, 1)
                else:
                    nc.scalar.activation(scratch[:].rearrange("p t e -> p (t e)"),
                                         scratch[:].rearrange("p t e -> p (t e)"), ACT.Exp).then_inc(exp_ready, 1)

            @block.sync
            def _(sp):
                sp.wait_ge(zero_set, 1)
                for i in range(tiles // 4):
                    sp.dma_start(slots[512 * i:512 * i + 512, :].rearrange("(a p) c -> p a c", p=128), zero[:])\
                        .then_inc(cleared, 16)
                sp.wait_ge(cleared, tiles // 4 * 16)

            @block.gpsimd
            def _(pool):
                nc.gpsimd.memset(zero[:], 0.0).then_inc(zero_set, 1)
                pool.wait_ge(cleared, tiles // 4 * 16)
                for k in range(taken):
                    pool.wait_ge(placed, k + 1)
                    for t in range(TILES):
                        nc.gpsimd.indirect_dma_start(
                            out=slots[:, :], out_offset=bass.IndirectOffsetOnAxis(ap=position[:, k, t:t + 1], axis=0),
                            in_=normed[:, t, :], in_offset=None, bounds_check=tiles * 128 - 1).then_inc(scattered, 16)
                pool.wait_ge(scattered, 16 * taken * TILES)

            @block.vector
            def _(dve):
                link = link_on(dve, chained)
                got = ps[:, 7, 0:TILES * experts].rearrange("p (t e) -> p t e", e=experts)
                if bias is None:
                    link(nc.vector.tensor_copy(logits[:], got))
                else:
                    link(nc.vector.tensor_tensor(logits[:], got, over(bias[:, None, :]), ALU.add))
                index = over(consts["index"][:, None, 0:experts])
                work = logits
                for k in range(taken):
                    link(nc.vector.tensor_reduce(out=top[:, k, :], in_=work[:], axis=AX.X, op=ALU.max))
                    link(nc.vector.tensor_tensor(scratch[:], work[:], over(top[:, k, :, None]), ALU.is_equal))
                    link(nc.vector.tensor_tensor(scratch[:], scratch[:], index, ALU.mult))
                    link(nc.vector.tensor_reduce(out=first[:], in_=scratch[:], axis=AX.X, op=ALU.min))
                    picked = nc.vector.tensor_tensor(chosen[k][:], index, over(first[:, :, None]), ALU.is_equal)
                    if taken == 1:
                        picked.then_inc(chosen_ready, 1)
                        dve.wait_ge(chosen_ready, 1)
                    else:
                        link(picked)
                    if k + 1 < taken:
                        link(nc.vector.scalar_tensor_tensor(
                            out=running[0][:].rearrange("p t e -> p (t e)"),
                            in0=chosen[k][:].rearrange("p t e -> p (t e)"), scalar=MASKED,
                            in1=work[:].rearrange("p t e -> p (t e)"), op0=ALU.mult, op1=ALU.add))
                        work = running[0]
                if taken == 2:
                    nc.vector.tensor_tensor(select[:], chosen[0][:], chosen[1][:], ALU.add).then_inc(chosen_ready, 1)
                    nc.vector.tensor_tensor(first[:], top[:, 1, :], top[:, 0, :], ALU.subtract).then_inc(gap_ready, 1)
                else:
                    nc.vector.tensor_tensor(scratch[:], logits[:], over(top[:, 0, :, None]), ALU.subtract)\
                        .then_inc(gap_ready, 1)
                dve.wait_ge(counted, 2)
                link(nc.vector.tensor_copy(running[0][:].rearrange("p t e -> p (t e)"), ps[:, 1, 0:TILES * experts]))
                a, b, step = running[0], running[1], 1
                while step < TILES:
                    nc.vector.tensor_copy(b[:, 0:step, :], a[:, 0:step, :])
                    link(nc.vector.tensor_tensor(b[:, step:, :], a[:, step:, :], a[:, 0:TILES - step, :], ALU.add))
                    a, b, step = b, a, 2 * step
                total, padded, one, other, start = (ends[:, i, :] for i in range(5))
                link(nc.vector.tensor_copy(total, a[:, TILES - 1, :]))
                link(nc.vector.tensor_tensor(b[:].rearrange("p t e -> p (t e)"), a[:].rearrange("p t e -> p (t e)"),
                                             ps[:, 1, 0:TILES * experts], ALU.subtract))
                link(nc.vector.tensor_tensor(b[:].rearrange("p t e -> p (t e)"), b[:].rearrange("p t e -> p (t e)"),
                                             ps[:, 0, 0:TILES * experts], ALU.add))
                link(nc.vector.tensor_scalar(ends_int[:], total, 127.0, None, ALU.add))
                link(nc.vector.tensor_single_scalar(ends_int[:], ends_int[:], 7, ALU.arith_shift_right))
                link(nc.vector.tensor_copy(padded, ends_int[:]))
                link(nc.vector.tensor_copy(one, padded))
                step = 1
                while step < experts:
                    nc.vector.tensor_copy(other[:, 0:step], one[:, 0:step])
                    link(nc.vector.tensor_tensor(other[:, step:], one[:, step:], one[:, 0:experts - step], ALU.add))
                    one, other, step = other, one, 2 * step
                link(nc.vector.tensor_tensor(start, one, padded, ALU.subtract))
                link(nc.vector.tensor_scalar(start, start, 128.0, None, ALU.mult))
                link(nc.vector.tensor_tensor(b[:], b[:], over(start[:, None, :]), ALU.add))
                for k in range(taken):
                    link(nc.vector.tensor_tensor(a[:], chosen[k][:], b[:], ALU.mult))
                    link(nc.vector.tensor_reduce(out=slot_of[:], in_=a[:], axis=AX.X, op=ALU.add))
                    nc.vector.tensor_copy(position[:, k, :], slot_of[:]).then_inc(placed, 1)
                shape = [128, tiles, experts]
                link(nc.vector.tensor_tensor(past[:], over(one[:, None, :], shape),
                                             over(consts["tile"][:, 0:tiles, None], shape), ALU.is_le))
                link(nc.vector.tensor_reduce(out=expert_of[:], in_=past[:], axis=AX.X, op=ALU.add))
                link(nc.vector.tensor_scalar(tile_expert[:], expert_of[:], float(experts - 1), None, ALU.min))
                dve.wait_ge(exp_ready, 1)
                if taken == 2:
                    link(nc.vector.tensor_scalar(tile_choice[:], one, consts["row"][:, 0:1], None, ALU.is_le))
                    link(nc.vector.tensor_reduce(out=own_expert[:], in_=tile_choice[:], axis=AX.X, op=ALU.add))
                    link(nc.vector.tensor_scalar(own_expert[:], own_expert[:], float(experts - 1), -float(experts),
                                                 ALU.min, ALU.add))
                    link(nc.vector.tensor_scalar(tile_choice[:], consts["index"][:, 0:experts], own_expert[:, 0:1], None,
                                                 ALU.is_equal))
                    link(nc.vector.tensor_scalar(counts[:], total, 1.0, None, ALU.max))
                    link(nc.vector.reciprocal(counts[:], counts[:]))
                    link(nc.vector.tensor_scalar(slot_of[:], first[:], 1.0, None, ALU.add))
                    link(nc.vector.reciprocal(slot_of[:], slot_of[:]))
                    link(nc.vector.tensor_tensor(first[:], first[:], slot_of[:], ALU.mult))
                    link(nc.vector.tensor_tensor(chosen[0][:], chosen[0][:], over(slot_of[:, :, None]), ALU.mult))
                    link(nc.vector.tensor_tensor(chosen[1][:], chosen[1][:], over(first[:, :, None]), ALU.mult))
                    link(nc.vector.tensor_tensor(weight[:], chosen[0][:], chosen[1][:], ALU.add))
                else:
                    link(nc.vector.tensor_reduce(out=slot_of[:], in_=scratch[:], axis=AX.X, op=ALU.add))
                    link(nc.vector.reciprocal(weight[:], slot_of[:]))


BODY = 8
GROUPED = 4


def past(s, tiles):
    return not isinstance(s, int) or s >= tiles


def slot_loop(engine, count, step):
    for r in range(BODY):
        step(r, r)
    with engine.Fori(1, count // BODY - 1) as i:
        for r in range(BODY):
            step(BODY * i + r, r)
    for r in range(BODY):
        step(count - BODY + r, r)


def load_slots(sp, slots, xs, loaded, turned, count):
    def step(s, r):
        if r % GROUPED:
            return
        u = r // GROUPED
        at = s * 128 if isinstance(s, int) else sp.snap(s * 128)
        if past(s, BODY):
            sp.wait_ge(turned, s - GROUPED)
        sp.dma_start(xs[:, u], slots[bass.ds(at, GROUPED * 128), :].rearrange("(a p) c -> p a c", p=128))\
            .then_inc(loaded[u], 16)
    slot_loop(sp, count, step)


def turn_slots(nc, pe, xs, loaded, xT_ready, turned, ident, ps, bank, s, r):
    if r % GROUPED == 0:
        u = r // GROUPED
        pe.wait_ge(loaded[u], 2 * s + 16 - 8 * u)
    if past(s, 2):
        pe.wait_ge(xT_ready, s - 1)
    nc.tensor.transpose(ps[:, bank + r % 2, 0:128], xs[:, r // GROUPED, r % GROUPED, :], ident[:]).then_inc(turned, 1)


def take_turned(nc, act, xT, turned, up_done, xT_ready, ps, bank, s, r):
    act.wait_ge(turned, s + 1)
    if past(s, 4):
        act.wait_ge(up_done, s - 3)
    nc.scalar.activation(xT[:, r % 4, :], ps[:, bank + r % 2, 0:128], ACT.Copy).then_inc(xT_ready, 1)


def fetch_weights(nc, dve, w1, own, tile_expert, experts, up_done, own_ready, s, r):
    e = dve.value_load(tile_expert[0:1, bass.ds(s, 1)], min_val=0, max_val=experts - 1)
    if past(s, 4):
        dve.wait_ge(up_done, s - 3)
    nc.vector.tensor_copy(own[:, r % 4, :], w1[:, bass.ds(e, 1), :].rearrange("p a f -> p (a f)"))\
        .then_inc(own_ready, 1)


def multiply_up(nc, pe, own, xT, own_ready, xT_ready, read, up_done, ps, bank, s, r):
    pe.wait_ge(own_ready, s + 1)
    pe.wait_ge(xT_ready, s + 1)
    if past(s, 2):
        pe.wait_ge(read, s - 1)
    for c in range(FC):
        mm = nc.tensor.matmul(ps[:, bank + r % 2, c * 128:(c + 1) * 128], own[:, r % 4, c * 128:(c + 1) * 128],
                              xT[:, r % 4, :], start=True, stop=True)
    mm.then_inc(up_done, 1)


def expert_sums(nc, slots, tile_expert, w1T, partial, consts, ps):
    with stage(nc, "sums") as (sb, sem):
        xs = sb("xs", [128, 2, GROUPED, C])
        xT = sb("xT", [128, 4, 128])
        own = sb("own", [128, 4, F])
        hidden = sb("hidden", [128, 2, F])
        loaded = [sem(f"loaded{u}") for u in range(2)]
        turned, xT_ready, own_ready, up_done, hidden_ready, summed = (
            sem(n) for n in ("turned", "xT_ready", "own_ready", "up_done", "hidden_ready", "summed"))
        TURN, UP = 0, 2

        def inside(s):
            return not isinstance(s, int) or s < S2

        with nc.Block() as block:
            @block.sync
            def _(sp):
                load_slots(sp, slots, xs, loaded, turned, S2)

            @block.tensor
            def _(pe):
                def turn(s, r):
                    turn_slots(nc, pe, xs, loaded, xT_ready, turned, consts["ident"], ps, TURN, s, r)

                turn(0, 0)
                turn(1, 1)

                def step(s, r):
                    if inside(s + 2):
                        turn(s + 2, (r + 2) % BODY)
                    multiply_up(nc, pe, own, xT, own_ready, xT_ready, hidden_ready, up_done, ps, UP, s, r)
                slot_loop(pe, S2, step)

            @block.scalar
            def _(act):
                def take(s, r):
                    take_turned(nc, act, xT, turned, up_done, xT_ready, ps, TURN, s, r)

                take(0, 0)
                take(1, 1)

                def step(s, r):
                    if inside(s + 2):
                        take(s + 2, (r + 2) % BODY)
                    act.wait_ge(up_done, s + 1)
                    if past(s, 2):
                        act.wait_ge(summed, s - 1)
                    nc.scalar.activation(hidden[:, r % 2, :], ps[:, UP + r % 2, :], ACT.Silu).then_inc(hidden_ready, 1)
                slot_loop(act, S2, step)

            @block.vector
            def _(dve):
                def fetch(s, r):
                    fetch_weights(nc, dve, w1T, own, tile_expert, E2, up_done, own_ready, s, r)

                def total(s, r):
                    dve.wait_ge(hidden_ready, s + 1)
                    nc.vector.tensor_reduce(out=partial[:, bass.ds(s, 1), :].rearrange("p s c -> p (s c)"),
                                            in_=hidden[:, r % 2, :].rearrange("p (c n) -> p c n", c=FC),
                                            axis=AX.X, op=ALU.add).then_inc(summed, 1)

                for s in range(3):
                    fetch(s, s)

                def step(s, r):
                    if inside(s + 3):
                        fetch(s + 3, (r + 3) % BODY)
                    if past(s, 1):
                        total(s - 1, (r - 1) % BODY)
                slot_loop(dve, S2, step)
                total(S2 - 1, BODY - 1)


def mix_means(nc, partial, tile_choice, w2, inverse, weight, tokens, consts, ps):
    PARTS = TILES * E2 // 128
    PER = 128 // E2
    with stage(nc, "mix") as (sb, sem):

        product = sb("product", [128, F])
        means = sb("means", [128, PER, E2])
        meansT = sb("meansT", [128, C])
        spread = sb("spread", [128, PER, C])
        weightT = sb("weightT", [128, PARTS, 128])
        partialT = sb("partialT", [S2, F])
        partial_turned, partialT_ready, summed, product_done = (
            sem(n) for n in ("partial_turned", "partialT_ready", "summed", "product_done"))
        turned, weightT_ready, means_ready, means_turned, spread_ready, mixed, added, chained = (
            sem(n) for n in ("turned", "weightT_ready", "means_ready", "means_turned", "spread_ready", "mixed",
                             "added", "chained"))
        with nc.Block() as block:
            @block.tensor
            def _(pe):
                for g in range(PARTS):
                    mm = nc.tensor.transpose(ps[:, 0, g * 128:(g + 1) * 128],
                                             weight[:, g * PER:(g + 1) * PER, :].rearrange("p t e -> p (t e)"),
                                             consts["ident"][:])
                mm.then_inc(turned, 1)
                for c in range(FC):
                    mm = nc.tensor.transpose(ps[0:S2, 1, c * 128:(c + 1) * 128], partial[:, :, c], consts["ident"][:])
                mm.then_inc(partial_turned, 1)
                pe.wait_ge(weightT_ready, 1)
                pe.wait_ge(partialT_ready, 1)
                for e in range(E2):
                    if e >= 6:
                        pe.wait_ge(product_done, e - 5)
                    nc.tensor.matmul(ps[:, 2 + e % 6, :], tile_choice[0:S2, e:e + 1].to_broadcast([S2, 128]),
                                     partialT[:], start=True, stop=True).then_inc(summed, 1)
                pe.wait_ge(means_ready, 1)
                nc.tensor.transpose(ps[:, 1, 0:128], means[:].rearrange("p j e -> p (j e)"),
                                    consts["ident"][:]).then_inc(means_turned, 1)
                pe.wait_ge(spread_ready, 1)
                flat = spread[:].rearrange("p j c -> p (j c)")
                for g in range(PARTS):
                    for a in range(2):
                        i = 2 * g + a
                        if i >= 4:
                            pe.wait_ge(added, i - 3)
                        nc.tensor.matmul(ps[:, 2 + i % 4, :], weightT[:, g, :], flat[:, a * 512:(a + 1) * 512],
                                         start=True, stop=True).then_inc(mixed, 1)

            @block.scalar
            def _(act):
                act.wait_ge(turned, 1)
                nc.scalar.activation(weightT[:].rearrange("p g t -> p (g t)"), ps[:, 0, :],
                                     ACT.Copy).then_inc(weightT_ready, 1)

            @block.vector
            def _(dve):
                link = link_on(dve, chained)
                dve.wait_ge(partial_turned, 1)
                nc.vector.tensor_copy(partialT[:], ps[0:S2, 1, :]).then_inc(partialT_ready, 1)
                for e in range(E2):
                    dve.wait_ge(summed, e + 1)
                    if e >= 1:
                        dve.wait_ge(product_done, e)
                    nc.vector.scalar_tensor_tensor(out=product[:], in0=ps[:, 2 + e % 6, :], scalar=inverse[:, e:e + 1],
                                                   in1=w2[:, e, :], op0=ALU.mult, op1=ALU.mult,
                                                   accum_out=means[:, 0, e:e + 1]).then_inc(product_done, 1)
                dve.wait_ge(product_done, E2)
                nc.vector.tensor_copy(means[:, 1:PER, :], means[:, 0:1, :].to_broadcast([128, PER - 1, E2]))\
                    .then_inc(means_ready, 1)
                dve.wait_ge(means_turned, 1)
                link(nc.vector.tensor_copy(meansT[:], ps[:, 1, 0:128]))
                for j in range(PER):
                    last = nc.vector.tensor_scalar(spread[:, j, :], meansT[:], consts["part"][:, j:j + 1], None, ALU.mult)
                last.then_inc(spread_ready, 1)
                for i in range(2 * PARTS):
                    dve.wait_ge(mixed, i + 1)
                    at = tokens[:, 4 * i:4 * i + 4, :]
                    nc.vector.tensor_tensor(at, at, ps[:, 2 + i % 4, :].rearrange("p (t c) -> p t c", c=C),
                                            ALU.add).then_inc(added, 1)


def expert_outputs(nc, slots, outputs, tile_expert, w1, b1_rows, w2, b2, consts, ps):
    with stage(nc, "expert") as (sb, sem):
        xs = sb("xs", [128, 2, GROUPED, C])
        xT = sb("xT", [128, 4, 128])
        own = sb("own", [128, 4, F])
        b1 = sb("b1", [128, E3, FC])
        before = sb("before", [128, 2, F])
        hidden = sb("hidden", [128, 4, F])
        y = sb("y", [128, 2, GROUPED, C])
        loaded = [sem(f"loaded{u}") for u in range(2)]
        stored = [sem(f"stored{u}") for u in range(2)]
        bias_turned, bias_ready = sem("bias_turned"), sem("bias_ready")
        turned, xT_ready, own_ready, up_done, before_ready, hidden_ready, down_done, y_ready = (
            sem(n) for n in ("turned", "xT_ready", "own_ready", "up_done", "before_ready", "hidden_ready",
                             "down_done", "y_ready"))
        TURN, UP, DOWN, BIAS = 0, 2, 4, 6

        def expert(engine, s):
            return engine.value_load(tile_expert[0:1, bass.ds(s, 1)], min_val=0, max_val=E3 - 1)

        def inside(s):
            return not isinstance(s, int) or s < S3

        with nc.Block() as block:
            @block.sync
            def _(sp):
                load_slots(sp, slots, xs, loaded, turned, S3)

            @block.gpsimd
            def _(pool):
                def step(s, r):
                    if r % GROUPED == GROUPED - 1:
                        first = s - (GROUPED - 1)
                        at = first * 128 if isinstance(s, int) else pool.snap(first * 128)
                        pool.wait_ge(y_ready, s + 1)
                        pool.dma_start(outputs[bass.ds(at, GROUPED * 128), :].rearrange("(a p) c -> p a c", p=128),
                                       y[:, r // GROUPED]).then_inc(stored[r // GROUPED], 16)
                slot_loop(pool, S3, step)
                for u in range(2):
                    pool.wait_ge(stored[u], 16 * S3 // BODY)

            @block.tensor
            def _(pe):
                def turn(s, r):
                    turn_slots(nc, pe, xs, loaded, xT_ready, turned, consts["ident"], ps, TURN, s, r)

                def down(s, r):
                    e = expert(pe, s)
                    pe.wait_ge(hidden_ready, s + 1)
                    if past(s, 2):
                        pe.wait_ge(y_ready, s - 1)
                    for c in range(FC):
                        mm = nc.tensor.matmul(ps[:, DOWN + r % 2, 0:C], hidden[:, r % 4, c * 128:(c + 1) * 128],
                                              w2[:, bass.ds(e, 1), c, :].rearrange("p a c -> p (a c)"),
                                              start=c == 0, stop=c == FC - 1)
                    mm.then_inc(down_done, 1)

                nc.tensor.transpose(ps[:, BIAS, 0:E3 * FC], b1_rows[:], consts["ident"][0:E3 * FC, 0:E3 * FC])\
                    .then_inc(bias_turned, 1)
                turn(0, 0)
                turn(1, 1)

                def step(s, r):
                    if inside(s + 2):
                        turn(s + 2, (r + 2) % BODY)
                    multiply_up(nc, pe, own, xT, own_ready, xT_ready, before_ready, up_done, ps, UP, s, r)
                    if past(s, 2):
                        down(s - 2, (r - 2) % BODY)
                slot_loop(pe, S3, step)
                down(S3 - 2, BODY - 2)
                down(S3 - 1, BODY - 1)

            @block.scalar
            def _(act):
                def take(s, r):
                    take_turned(nc, act, xT, turned, up_done, xT_ready, ps, TURN, s, r)

                take(0, 0)
                take(1, 1)

                def step(s, r):
                    if inside(s + 2):
                        take(s + 2, (r + 2) % BODY)
                    act.wait_ge(before_ready, s + 1)
                    if past(s, 4):
                        act.wait_ge(down_done, s - 3)
                    nc.scalar.activation(hidden[:, r % 4, :], before[:, r % 2, :], ACT.Gelu).then_inc(hidden_ready, 1)
                slot_loop(act, S3, step)

            @block.vector
            def _(dve):
                def fetch(s, r):
                    fetch_weights(nc, dve, w1, own, tile_expert, E3, up_done, own_ready, s, r)

                def finish(s, r):
                    e = expert(dve, s)
                    dve.wait_ge(down_done, s + 1)
                    if r % GROUPED == 0 and past(s, BODY):
                        u = r // GROUPED
                        dve.wait_ge(stored[u], 2 * s - 8 * u)
                    nc.vector.tensor_tensor(y[:, r // GROUPED, r % GROUPED, :], ps[:, DOWN + r % 2, 0:C],
                                            b2[:, bass.ds(e, 1), :].rearrange("p a c -> p (a c)"),
                                            ALU.add).then_inc(y_ready, 1)

                for s in range(3):
                    fetch(s, s)
                dve.wait_ge(bias_turned, 1)
                nc.vector.tensor_copy(b1[:].rearrange("p e c -> p (e c)"), ps[:, BIAS, 0:E3 * FC]).then_inc(bias_ready, 1)
                dve.wait_ge(bias_ready, 1)

                def step(s, r):
                    if inside(s + 3):
                        fetch(s + 3, (r + 3) % BODY)
                    e = expert(dve, s)
                    dve.wait_ge(up_done, s + 1)
                    if past(s, 2):
                        dve.wait_ge(hidden_ready, s - 1)
                    nc.vector.tensor_tensor(before[:, r % 2, :].rearrange("p (c n) -> p c n", c=FC),
                                            ps[:, UP + r % 2, :].rearrange("p (c n) -> p c n", c=FC),
                                            b1[:, bass.ds(e, 1), :].rearrange("p a c -> p (a c)")[:, :, None]
                                            .to_broadcast([128, FC, 128]), ALU.add).then_inc(before_ready, 1)
                    if past(s, 2):
                        finish(s - 2, (r - 2) % BODY)
                slot_loop(dve, S3, step)
                finish(S3 - 2, BODY - 2)
                finish(S3 - 1, BODY - 1)


def gather_outputs(nc, outputs, position, weight, tokens, gathered, out_dram, consts, ps):
    with stage(nc, "last") as (sb, sem):

        result = sb("result", [128, 8, 512])
        arrived = [sem(f"arrived{g}") for g in range(8)]
        scaled, added, turned, taken, stored = (sem(n) for n in ("scaled", "added", "turned", "taken", "stored"))
        with nc.Block() as block:
            @block.gpsimd
            def _(pool):
                for t in range(TILES):
                    nc.gpsimd.indirect_dma_start(
                        out=gathered[:, t, :], out_offset=None, in_=outputs[:, :],
                        in_offset=bass.IndirectOffsetOnAxis(ap=position[:, 0, t:t + 1], axis=0),
                        bounds_check=S3 * 128 - 1).then_inc(arrived[t // 4], 16)

            @block.vector
            def _(dve):
                for g in range(8):
                    at = slice(4 * g, 4 * g + 4)
                    dve.wait_ge(arrived[g], 64)
                    nc.vector.tensor_tensor(gathered[:, at, :], gathered[:, at, :],
                                            weight[:, at, None].to_broadcast([128, 4, C]), ALU.mult).then_inc(scaled, 1)
                    dve.wait_ge(scaled, g + 1)
                    nc.vector.tensor_tensor(tokens[:, at, :], tokens[:, at, :], gathered[:, at, :],
                                            ALU.add).then_inc(added, 1)

            @block.tensor
            def _(pe):
                for g in range(8):
                    pe.wait_ge(added, g + 1)
                    if g >= 2:
                        pe.wait_ge(taken, g - 1)
                    for a in range(4):
                        mm = nc.tensor.transpose(ps[:, g % 2, a * 128:(a + 1) * 128], tokens[:, 4 * g + a, :],
                                                 consts["ident"][:])
                    mm.then_inc(turned, 1)

            @block.scalar
            def _(act):
                for g in range(8):
                    act.wait_ge(turned, g + 1)
                    nc.scalar.activation(result[:, g, :], ps[:, g % 2, :], ACT.Copy).then_inc(taken, 1)

            @block.sync
            def _(sp):
                for g in range(8):
                    sp.wait_ge(taken, g + 1)
                    sp.dma_start(out_dram[2 * g:2 * g + 2].rearrange("b c h w -> c b (h w)"),
                                 result[:, g, :].rearrange("p (b n) -> p b n", b=2)).then_inc(stored, 16)
                sp.wait_ge(stored, 16 * 8)


def build(nc, a, out):
    with ExitStack() as ctx:
        def sb(name, shape, dt=FP32, into=ctx):
            return into.enter_context(nc.sbuf_tensor(name, shape, dt))

        def sem(name):
            return ctx.enter_context(nc.semaphore(name))

        ps = ctx.enter_context(nc.psum_tensor("ps", [128, 8, 512], FP32))
        tokens = sb("tokens", [128, TILES, C])
        xf = sb("xf", [128, TOKENS])
        normed = sb("normed", [128, TILES, C])

        shapes = {"ident": [128, 128], "group": [128, 128], "before": [128, 128],
                  "ones": [128, 128], "lo_rows": [128, 2], "causal": [128, 2 * N],
                  "index": [128, E2], "row": [128, 1], "tile": [128, S2], "part": [128, 128 // E2]}
        consts = {k: sb(f"const_{k}", v) for k, v in shapes.items()}
        ident16 = sb("ident16", [128, 128], BF16)
        window = sb("window", [128, 2 * N], BF16)

        first = {"wq_r": (a["L0_conv_wq_r"].rearrange("(c o) -> c o", o=1), [C, 1]),
                 "wv_r": (a["L0_conv_wv_r"], [C2, C]), "w_up": (a["L0_conv_w_up"], [C, C2]),
                 "wq_l": (a["L0_conv_wq_l"], [C2, C]), "wv_l": (a["L0_conv_wv_l"], [C2, C])}
        w = {k: sb(f"w_{k}", shape) for k, (_, shape) in first.items()}
        wqk = [sb(f"wqk{i}", [C, 8, 128]) for i in range(3)]
        wv = [sb(f"wv{i}", [C, 128]) for i in range(3)]
        wo = [sb(f"wo{i}", [128, C]) for i in range(3)]
        q_bias = sb("q_bias", [128, 8])
        v_bias = sb("v_bias", [128, 128])
        o_bias = sb("o_bias", [1, 2, C])
        gate2 = sb("gate2", [C, E2])
        gate3 = sb("gate3", [C, E3])
        gate3_bias = sb("gate3_bias", [128, E3])
        position = sb("position", [128, K2, TILES], UINT32)
        tile_expert = sb("tile_expert", [128, S2], INT32)
        tile_choice = sb("tile_choice", [128, E2])
        partial = sb("partial", [128, S2, FC])
        weight2 = sb("weight2", [128, TILES, E2])
        weight3 = sb("weight3", [128, TILES])
        inverse = sb("inverse", [128, E2])

        slots = nc.dram_tensor("slots", (S2 * 128, C), FP32, kind="Internal").ap()
        outputs = nc.dram_tensor("slot_outputs", (S3 * 128, C), FP32, kind="Internal").ap()

        consts_in = sem("consts_in")
        raw_in = sem("raw_in")
        experts_in = sem("experts_in")
        last_in = sem("last_in")

        experts2 = ctx.enter_context(ExitStack())
        w1_raw = sb("w1_raw", [128, E2 * FC, C], into=experts2)
        w2 = sb("w2", [128, E2, F], into=experts2)

        with ExitStack() as prep:
            window32 = sb("window32", [128, 2 * N], into=prep)
            raw_fc = sb("raw_fc", [128, 3, C], into=prep)
            raw = sb("raw", [128, 5, C], into=prep)
            raw_qkv = sb("raw_qkv", [C, 2, 128], into=prep)
            raw_gate = sb("raw_gate", [E2, C], into=prep)
            fc_bias = sb("fc_bias", [1, 3 * 128], into=prep)
            fcT = sb("fcT", [C, 3 * 128], into=prep)
            wide_bias = sb("wide_bias", [1, 8 * 128], into=prep)
            turned, copied, biased = sem("turned"), sem("copied"), sem("biased")
            with nc.Block() as block:
                @block.sync
                def _(sp):
                    for k, tile in consts.items():
                        sp.dma_start(tile[:], a[f"const_{k}"][:, :]).then_inc(consts_in, 16)
                    sp.dma_start(window32[:], a["const_window"]).then_inc(raw_in, 16)
                    for k, (source, _) in first.items():
                        sp.dma_start(w[k][:], source).then_inc(consts_in, 16)
                    sp.dma_start(raw_fc[:], a["L1_conv_W_fc"].rearrange("(t p) c -> p t c", p=128)).then_inc(raw_in, 16)
                    sp.dma_start(raw[:, 0, :], a["L1_conv_W_last"]).then_inc(raw_in, 16)
                    for i, k in enumerate(("Wq", "Wk", "Wv", "Wo")):
                        sp.dma_start(raw[:, 1 + i, :], a[f"L2_attn_{k}"]).then_inc(raw_in, 16)
                    for i, k in enumerate(("Wq", "Wk")):
                        sp.dma_start(raw_qkv[:, i, :], a[f"L3_attn_{k}"]).then_inc(raw_in, 16)
                    sp.dma_start(wv[2][:], a["L3_attn_Wv"]).then_inc(raw_in, 16)
                    sp.dma_start(wo[2][:], a["L3_attn_Wo"]).then_inc(raw_in, 16)
                    sp.dma_start(raw_gate[:], a["L2_ffn_gate_weight"]).then_inc(raw_in, 16)
                    sp.dma_start(gate3[:], a["L3_ffn_Ws"]).then_inc(raw_in, 16)
                    sp.dma_start(fc_bias[:], a["L1_conv_b_fc"].rearrange("(o n) -> o n", o=1)).then_inc(raw_in, 16)
                    sp.dma_start(o_bias[:, 0, :], a["L1_conv_b_last"].rearrange("(o n) -> o n", o=1)).then_inc(raw_in, 16)
                    sp.dma_start(o_bias[:, 1, :], a["L3_attn_bo"].rearrange("(o n) -> o n", o=1)).then_inc(raw_in, 16)
                    sp.dma_start(gate3_bias[:], a["L3_ffn_bs"].rearrange("(o n) -> o n", o=1).to_broadcast([128, E3]))\
                        .then_inc(raw_in, 16)
                    sp.dma_start(w1_raw[:], a["L2_ffn_w1"].rearrange("e (k p) d -> p (e k) d", p=128)).then_inc(experts_in, 16)
                    sp.dma_start(w2[:], a["L2_ffn_w2"].rearrange("e d f -> d e f")).then_inc(experts_in, 16)
                    sp.wait_ge(consts_in, 16 * (len(consts) + len(first)))
                    sp.wait_ge(raw_in, 16 * 17)

                @block.tensor
                def _(pe):
                    pe.wait_ge(consts_in, 16 * (len(consts) + len(first)))
                    pe.wait_ge(raw_in, 16 * 17)
                    for t in range(3):
                        nc.tensor.transpose(ps[:, 0, t * 128:(t + 1) * 128], raw_fc[:, t, :], consts["ident"][:])
                    for i in range(4):
                        nc.tensor.transpose(ps[:, 1, i * 128:(i + 1) * 128], raw[:, i, :], consts["ident"][:])
                    nc.tensor.transpose(ps[:, 2, 0:128], raw[:, 4, :], consts["ident"][:])
                    nc.tensor.transpose(ps[:, 3, 0:E2], raw_gate[:], consts["ident"][0:E2, 0:E2]).then_inc(turned, 1)
                    pe.wait_ge(biased, 1)
                    for g in range(8):
                        nc.tensor.matmul(ps[:, 4, g:g + 1], wide_bias[:, g * 128:(g + 1) * 128],
                                         consts["ones"][0:1, 0:1], start=True, stop=True)
                    mm = nc.tensor.matmul(ps[:, 5, 0:128], consts["ones"][0:1, 0:128],
                                          fc_bias[:].rearrange("o (h t d) -> o t h d", h=H, t=3)[:, 2],
                                          start=True, stop=True)
                    mm.then_inc(turned, 1)

                @block.vector
                def _(dve):
                    def repeat(out, heads, scale):
                        part = heads.shape[0]
                        return nc.vector.tensor_scalar(
                            out.rearrange("p (h r d) -> p h r d", h=H, r=4),
                            heads[:, :, None, :].to_broadcast([part, H, 4, D]), scale, None, ALU.mult)

                    dve.wait_ge(turned, 1)
                    nc.vector.tensor_copy(ident16[:], consts["ident"][:])
                    nc.vector.tensor_copy(window[:], window32[:])
                    nc.vector.tensor_copy(fcT[:], ps[:, 0, 0:384]).then_inc(copied, 1)
                    nc.vector.tensor_copy(wo[0][:], ps[:, 1, 0:128])
                    nc.vector.tensor_copy(wv[1][:], ps[:, 1, 384:512])
                    nc.vector.tensor_copy(wo[1][:], ps[:, 2, 0:128])
                    nc.vector.tensor_copy(gate2[:], ps[:, 3, 0:E2])
                    dve.wait_ge(copied, 1)
                    fc = fcT[:].rearrange("p (h t d) -> p t h d", h=H, t=3)
                    bias = fc_bias[:].rearrange("p (h t d) -> p t h d", h=H, t=3)
                    scale = float(D) ** -0.5
                    qk = [(fc[:, 0], fc[:, 1], scale),
                          tuple(ps[:, 1, i:i + 128].rearrange("p (h d) -> p h d", h=H) for i in (128, 256)) + (scale,),
                          tuple(raw_qkv[:, i, :].rearrange("p (h d) -> p h d", h=H) for i in (0, 1)) + (1.0,)]
                    for i, (q, k, s) in enumerate(qk):
                        flat = wqk[i][:].rearrange("p g n -> p (g n)")
                        repeat(flat[:, 0:512], q, s)
                        repeat(flat[:, 512:1024], k, 1.0)
                    nc.vector.tensor_copy(wv[0][:].rearrange("p (h d) -> p h d", h=H), fc[:, 2])
                    repeat(wide_bias[:, 0:512], bias[:, 0], scale)
                    repeat(wide_bias[:, 512:1024], bias[:, 1], 1.0).then_inc(biased, 1)
                    dve.wait_ge(turned, 2)
                    nc.vector.tensor_copy(q_bias[:], ps[:, 4, 0:8])
                    nc.vector.tensor_copy(v_bias[:], ps[:, 5, 0:128])

        ident, ones_row, lo = consts["ident"], consts["ones"], consts["lo_rows"]
        masks = {"ident": ident16, "rows": window, "keep": consts["causal"]}

        spatial_gate(nc, a["x"], w, xf, tokens, consts, ps)
        attention(nc, "softmax", xf, tokens, wqk[0], wv[0], wo[0], ident, q_bias, v_bias, o_bias[:, 0, :], lo,
                  ones_row, masks, ps)
        layer_norm(nc, "norm0", tokens, normed, xf, ident, ps)
        attention(nc, "window", xf, tokens, wqk[1], wv[1], wo[1], ident, None, None, None, lo, ones_row, masks, ps)
        layer_norm(nc, "norm1", tokens, normed, None, ident, ps, gate2)
        route(nc, "route2", E2, K2, S2, None, consts, normed, slots, position, tile_expert, weight2, inverse,
              tile_choice, ps)

        with ExitStack() as turning:
            w1T = sb("w1T", [128, E2, F], into=turning)
            transposed, taken = sem("w1_turned"), sem("w1_taken")
            with nc.Block() as block:
                @block.tensor
                def _(pe):
                    pe.wait_ge(experts_in, 32)
                    for e in range(E2):
                        if e >= 8:
                            pe.wait_ge(taken, e - 7)
                        for k in range(FC):
                            mm = nc.tensor.transpose(ps[:, e % 8, k * 128:(k + 1) * 128], w1_raw[:, e * FC + k, :], ident[:])
                        mm.then_inc(transposed, 1)

                @block.vector
                def _(dve):
                    for e in range(E2):
                        dve.wait_ge(transposed, e + 1)
                        nc.vector.tensor_copy(w1T[:, e, :], ps[:, e % 8, :]).then_inc(taken, 1)

            expert_sums(nc, slots, tile_expert, w1T, partial, consts, ps)
            mix_means(nc, partial, tile_choice, w2, inverse, weight2, tokens, consts, ps)
        experts2.close()

        w1 = sb("w1", [128, E3, F])
        w2 = sb("w2_last", [128, E3, FC, C])
        b1_rows = sb("b1_rows", [E3 * FC, 128])
        b2 = sb("b2", [128, E3, C])
        with nc.Block() as block:
            @block.sync
            def _(sp):
                sp.dma_start(w1[:], a["L3_ffn_W1"].rearrange("e d f -> d e f")).then_inc(last_in, 16)
                sp.dma_start(w2[:], a["L3_ffn_W2"].rearrange("e (k p) d -> p (e k) d", p=128)
                             .rearrange("p (e k) d -> p e k d", e=E3)).then_inc(last_in, 16)
                sp.dma_start(b1_rows[:], a["L3_ffn_b1"].rearrange("e (k p) -> (e k) p", p=128)).then_inc(last_in, 16)
                flat = a["L3_ffn_b2"].rearrange("(o e) n -> o (e n)", o=1)
                sp.dma_start(b2[:].rearrange("p e n -> p (e n)"), flat.to_broadcast([128, flat.shape[1]]))\
                    .then_inc(last_in, 16)
        layer_norm(nc, "norm2", tokens, normed, xf, ident, ps)
        attention(nc, "linear", xf, tokens, wqk[2], wv[2], wo[2], ident, None, None, o_bias[:, 1, :], lo, ones_row,
                  masks, ps)
        layer_norm(nc, "norm3", tokens, normed, None, ident, ps, gate3)
        route(nc, "route3", E3, K3, S3, gate3_bias, consts, normed, slots, position, tile_expert[:, 0:S3], weight3, None,
              None, ps)
        with nc.Block() as block:
            @block.sync
            def _(sp):
                sp.wait_ge(last_in, 64)
        expert_outputs(nc, slots, outputs, tile_expert, w1, b1_rows, w2, b2, consts, ps)
        gathered = normed
        gather_outputs(nc, outputs, position, weight3, tokens, gathered, out, consts, ps)


def constants():
    import numpy as np

    p = np.arange(128)[:, None]
    row, column = np.arange(128)[:, None], np.arange(N)[None]
    halves = [row + 128 * i - column for i in range(2)]
    window = np.concatenate([np.where((d >= 0) & (d < WINDOW), 0, MASKED) for d in halves], 1)
    causal = np.concatenate([column - (row + 128 * i) >= 0 for i in range(2)], 1)
    rows = p % 64
    return {
        "ident": np.eye(128, dtype=np.float32),
        "group": (p // GROUP == p.T // GROUP).astype(np.float32) / GROUP,
        "before": (p < p.T).astype(np.float32),
        "ones": np.ones((128, 128), np.float32),
        "lo_rows": -np.concatenate([rows // 16 % 2, rows // 32], 1).astype(np.float32),
        "window": window.astype(np.float32),
        "causal": causal.astype(np.float32),
        "index": np.tile(np.arange(E2, dtype=np.float32) - E2, (128, 1)),
        "row": p.astype(np.float32),
        "tile": np.tile(np.arange(S2, dtype=np.float32), (128, 1)),
        "part": (p // E2 == np.arange(128 // E2)[None]).astype(np.float32),
    }


def kernel(**inputs):
    import numpy as np
    import concourse.bacc as bacc
    from concourse.bass_utils import run_bass_kernel_spmd

    nc = bacc.Bacc("TRN2", target_bir_lowering=False, num_devices=1)
    given = {k: np.ascontiguousarray(v) for k, v in inputs.items()}
    given.update({f"const_{k}": v for k, v in constants().items()})
    arrays, tensors = {}, {}
    for name, value in given.items():
        arrays[f"in_{name}"] = value
        tensors[name] = nc.dram_tensor(f"in_{name}", value.shape, mybir.dt.from_np(value.dtype),
                                       kind="ExternalInput").ap()
    out = nc.dram_tensor("out", (IMAGES, C, 16, 16), FP32, kind="ExternalOutput").ap()
    build(nc, tensors, out)
    result = run_bass_kernel_spmd(nc, [arrays], core_ids=[0])
    return result.results[0]["out"]
```

```python
import concourse.bass as bass
from concourse import mybir
from contextlib import ExitStack, contextmanager

FP32 = mybir.dt.float32
FP32R = mybir.dt.float32r
BF16 = mybir.dt.bfloat16
INT32 = mybir.dt.int32
UINT32 = mybir.dt.uint32
ALU = mybir.AluOpType
ACT = mybir.ActivationFunctionType
AX = mybir.AxisListType

C = 128
IMAGES, N = 16, 256
TOKENS = IMAGES * N
TILES = TOKENS // 128
H, D = 8, 16
WINDOW = 64
GROUP = 4
C2 = C // 2
F = 512
FC = F // 128
E2, K2 = 16, 2
E3, K3 = 8, 1
GN_EPS, LN_EPS, LINEAR_EPS = 1e-5, 1e-5, 0.001
MASKED = -1e30


def slot_tiles(experts, taken):
    most = (TOKENS * taken + experts * 127) // 128
    return most + -most % 8


S2, S3 = slot_tiles(E2, K2), slot_tiles(E3, K3)


@contextmanager
def stage(nc, name):
    taken = []
    with ExitStack() as ctx:
        def sb(n, shape, dt=FP32):
            return ctx.enter_context(nc.sbuf_tensor(f"{name}_{n}", shape, dt))

        def sem(n):
            taken.append(ctx.enter_context(nc.semaphore(f"{name}_{n}")))
            return taken[-1]

        yield sb, sem
        with nc.Block() as block:
            @block.gpsimd
            def _(pool):
                for s in taken:
                    pool.sem_clear(s)


def link_on(engine, sem):
    count = [0]

    def link(instruction):
        count[0] += 1
        instruction.then_inc(sem, 1)
        engine.wait_ge(sem, count[0])
    return link


def spatial_gate(nc, x, x_in, w, xf, tokens, consts, ps):
    with stage(nc, "gate") as (sb, sem):

        xn = sb("xn", [128, IMAGES, N])
        stats = sb("stats", [128, IMAGES, 6])
        small = sb("small", [128, 12, IMAGES])
        mean, dev, square, spread, rstd, peak, total, pooled, gate, summed, vw, halves = (
            small[:, i, :] for i in range(12))
        group_mean = sb("group_mean", [128, IMAGES])
        prob = sb("prob", [128, 2, 2, N])
        weighted = sb("weighted", [128, 2, 2, N])
        wq_wide = sb("wq_wide", [128, 128])
        v_wide = sb("v_wide", [128, 4, 128])
        turned = sb("turned", [128, 3, 128])
        squeezed = sb("squeezed", [C2, IMAGES])
        q_small = sb("q_small", [IMAGES, C2])
        q_exp = sb("q_exp", [IMAGES, C2])
        q_one = sb("q_one", [IMAGES, 3])
        qT = sb("qT", [C2, IMAGES])
        place = sb("place", [128, 2, 2, N])
        gated = sb("gated", [128, 2, 2, N])
        out = sb("out", [128, 2, 2 * N])

        weights_turned = sem("weights_turned")
        weights_ready = sem("weights_ready")
        stats_ready = sem("stats_ready")
        mean_ready = sem("mean_ready")
        grouped = sem("grouped")
        spread_ready = sem("spread_ready")
        var_ready = sem("var_ready")
        std_ready = sem("std_ready")
        xn_ready = sem("xn_ready")
        logits_ready = sem("logits_ready")
        peak_ready = sem("peak_ready")
        prob_ready = sem("prob_ready")
        weighted_ready = sem("weighted_ready")
        pooled_part = sem("pooled_part")
        pooled_ready = sem("pooled_ready")
        small_on_pe = sem("small_on_pe")
        small_on_dve = sem("small_on_dve")
        small_on_act = sem("small_on_act")
        wide_ready = sem("wide_ready")
        place_on_pe = sem("place_on_pe")
        place_ready = sem("place_ready")
        gated_ready = sem("gated_ready")
        out_ready = sem("out_ready")
        xf_ready = sem("xf_ready")
        out_turned = sem("out_turned")
        tokens_ready = sem("tokens_ready")
        chained = sem("chained")

        with nc.Block() as block:
            @block.tensor
            def _(pe):
                for i, name in enumerate(("wv_r", "w_up", "wq_l")):
                    rows, cols = w[name].shape
                    mm = nc.tensor.transpose(ps[0:cols, 7, i * 128:i * 128 + rows], w[name][:, :],
                                             consts["ident"][0:rows, 0:rows])
                mm.then_inc(weights_turned, 1)
                pe.wait_ge(mean_ready, 1)
                nc.tensor.matmul(ps[:, 0, 0:IMAGES], consts["group"][:], mean, start=True,
                                 stop=True).then_inc(grouped, 1)
                pe.wait_ge(spread_ready, 1)
                nc.tensor.matmul(ps[:, 0, 0:IMAGES], consts["group"][:], spread, start=True,
                                 stop=True).then_inc(grouped, 1)
                pe.wait_ge(weights_ready, 2)
                for m in range(IMAGES // 2):
                    pe.wait_ge(xn_ready, 2 * m + 2)
                    if m >= 2:
                        pe.wait_ge(prob_ready, m - 1)
                    nc.tensor.matmul(ps[:, 1 + m % 2, :], wq_wide[:],
                                     xn[:, 2 * m:2 * m + 2, :].rearrange("p b n -> p (b n)"),
                                     start=True, stop=True).then_inc(logits_ready, 1)
                pe.wait_ge(pooled_ready, 1)
                nc.tensor.matmul(ps[0:C2, 0, 0:IMAGES], turned[:, 0, 0:C2], pooled, start=True,
                                 stop=True).then_inc(small_on_pe, 1)
                pe.wait_ge(small_on_dve, 1)
                nc.tensor.matmul(ps[:, 0, 32:32 + IMAGES], turned[0:C2, 1, :], squeezed[:], start=True,
                                 stop=True).then_inc(small_on_pe, 1)
                pe.wait_ge(small_on_dve, 2)
                nc.tensor.matmul(ps[0:IMAGES, 3, 0:C2], summed, turned[:, 2, 0:C2], start=True,
                                 stop=True).then_inc(small_on_pe, 1)
                pe.wait_ge(small_on_dve, 4)
                nc.tensor.transpose(ps[0:C2, 4, 0:IMAGES], q_small[:], consts["ident"][0:IMAGES, 0:IMAGES])\
                    .then_inc(small_on_pe, 1)
                pe.wait_ge(small_on_dve, 5)
                nc.tensor.matmul(ps[:, 3, 0:IMAGES], w["wv_l"][:, :], qT[:], start=True,
                                 stop=True).then_inc(small_on_pe, 1)

                def turn_out(m):
                    pe.wait_ge(out_ready, m + 1)
                    if m >= 2:
                        pe.wait_ge(tokens_ready, m - 1)
                    for a in range(4):
                        mm = nc.tensor.transpose(ps[:, 5 + m % 2, a * 128:(a + 1) * 128],
                                                 out[:, m % 2, a * 128:(a + 1) * 128], consts["ident"][:])
                    mm.then_inc(out_turned, 1)

                for m in range(IMAGES // 2):
                    pe.wait_ge(wide_ready, 2 * m + 2)
                    if m >= 2:
                        pe.wait_ge(place_ready, m - 1)
                    for a in range(2):
                        b = 2 * m + a
                        mm = nc.tensor.matmul(ps[:, 1 + m % 2, a * N:(a + 1) * N], v_wide[:, b % 4, :], xn[:, b, :],
                                              start=True, stop=True)
                    mm.then_inc(place_on_pe, 1)
                    if m >= 2:
                        turn_out(m - 2)
                for m in (IMAGES // 2 - 2, IMAGES // 2 - 1):
                    turn_out(m)

            @block.scalar
            def _(act):
                act.wait_ge(var_ready, 1)
                nc.scalar.activation(square, dev, ACT.Sqrt).then_inc(std_ready, 1)
                for m in range(IMAGES // 2):
                    act.wait_ge(peak_ready, m + 1)
                    if m >= 2:
                        act.wait_ge(weighted_ready, m - 1)
                    for a in range(2):
                        b = 2 * m + a
                        last = nc.scalar.activation(prob[:, m % 2, a, :], ps[:, 1 + m % 2, a * N:(a + 1) * N], ACT.Exp,
                                                    bias=peak[:, b:b + 1], accum_out=total[:, b:b + 1])
                    last.then_inc(prob_ready, 1)
                act.wait_ge(small_on_pe, 2)
                nc.scalar.activation(gate, ps[:, 0, 32:32 + IMAGES], ACT.Sigmoid).then_inc(small_on_act, 1)
                act.wait_ge(small_on_dve, 3)
                nc.scalar.activation(q_exp[:], ps[0:IMAGES, 3, 0:C2], ACT.Exp, bias=q_one[:, 0:1],
                                     accum_out=q_one[:, 1:2]).then_inc(small_on_act, 1)

                def take_place(m):
                    act.wait_ge(place_on_pe, m + 1)
                    if m >= 2:
                        act.wait_ge(gated_ready, m - 1)
                    nc.scalar.activation(place[:, m % 2].rearrange("p a n -> p (a n)"), ps[:, 1 + m % 2, :],
                                         ACT.Sigmoid).then_inc(place_ready, 1)

                take_place(0)
                for m in range(IMAGES // 2 + 2):
                    if m + 1 < IMAGES // 2:
                        take_place(m + 1)
                    if 1 <= m <= IMAGES // 2:
                        act.wait_ge(out_ready, m)
                        nc.scalar.activation(xf[:, (2 * m - 2) * N:2 * m * N], out[:, (m - 1) % 2, :],
                                             ACT.Copy).then_inc(xf_ready, 1)
                    if m >= 2:
                        act.wait_ge(out_turned, m - 1)
                        nc.scalar.activation(tokens[:, 4 * m - 8:4 * m - 4, :].rearrange("p a c -> p (a c)"),
                                             ps[:, 5 + m % 2, :], ACT.Copy).then_inc(tokens_ready, 1)

            @block.gpsimd
            def _(pool):
                for m in range(IMAGES // 2):
                    pool.wait_ge(prob_ready, m + 1)
                    if m >= 2:
                        pool.wait_ge(pooled_part, m - 1)
                    nc.gpsimd.tensor_tensor(weighted[:, m % 2], prob[:, m % 2], xn[:, 2 * m:2 * m + 2, :],
                                            ALU.mult).then_inc(weighted_ready, 1)
                for m in range(IMAGES // 2):
                    pool.wait_ge(gated_ready, m + 1)
                    if m >= 2:
                        pool.wait_ge(xf_ready, m - 1)
                        pool.wait_ge(out_turned, m - 1)
                    nc.gpsimd.tensor_tensor(out[:, m % 2, :], gated[:, m % 2].rearrange("p a n -> p (a n)"),
                                            x[:, 2 * m:2 * m + 2, :].rearrange("p b n -> p (b n)"),
                                            ALU.add).then_inc(out_ready, 1)

            @block.vector
            def _(dve):
                link = link_on(dve, chained)
                dve.wait_ge(weights_turned, 1)
                nc.vector.tensor_copy(turned[:, 0, 0:C2], ps[:, 7, 0:C2])
                nc.vector.tensor_copy(turned[0:C2, 1, :], ps[0:C2, 7, 128:256])
                nc.vector.tensor_copy(turned[:, 2, 0:C2], ps[:, 7, 256:256 + C2]).then_inc(weights_ready, 1)
                nc.vector.tensor_copy(wq_wide[:], w["wq_r"][:, 0:1].to_broadcast([128, 128])).then_inc(weights_ready, 1)
                for b in range(IMAGES):
                    if b % 4 == 0:
                        dve.wait_ge(x_in[b // 4], 16)
                    last = nc.vector.bn_stats(stats[:, b, :], x[:, b, :])
                last.then_inc(stats_ready, 1)
                dve.wait_ge(stats_ready, 1)
                even, odd = stats[:, :, 1], stats[:, :, 4]
                link(nc.vector.tensor_tensor(mean, even, odd, ALU.add))
                link(nc.vector.tensor_scalar(mean, mean, 0.5, None, ALU.mult))
                last = nc.vector.tensor_tensor(dev, even, odd, ALU.subtract)
                last.then_inc(mean_ready, 1)
                dve.wait_ge(mean_ready, 1)
                link(nc.vector.tensor_tensor(square, dev, dev, ALU.mult))
                link(nc.vector.tensor_scalar(square, square, N / 4.0, None, ALU.mult))
                link(nc.vector.tensor_tensor(square, square, stats[:, :, 2], ALU.add))
                link(nc.vector.tensor_tensor(square, square, stats[:, :, 5], ALU.add))
                dve.wait_ge(grouped, 1)
                link(nc.vector.tensor_copy(group_mean[:], ps[:, 0, 0:IMAGES]))
                link(nc.vector.tensor_tensor(halves, mean, group_mean[:], ALU.subtract))
                link(nc.vector.tensor_tensor(spread, halves, halves, ALU.mult))
                link(nc.vector.tensor_scalar(spread, spread, float(N), None, ALU.mult))
                nc.vector.tensor_tensor(spread, spread, square, ALU.add).then_inc(spread_ready, 1)
                dve.wait_ge(grouped, 2)
                nc.vector.tensor_scalar(dev, ps[:, 0, 0:IMAGES], 1.0 / N, GN_EPS, ALU.mult,
                                        ALU.add).then_inc(var_ready, 1)
                dve.wait_ge(std_ready, 1)
                link(nc.vector.reciprocal(rstd, square))
                for b in range(IMAGES):
                    nc.vector.tensor_scalar(xn[:, b, :], x[:, b, :], group_mean[:, b:b + 1], rstd[:, b:b + 1],
                                            ALU.subtract, ALU.mult).then_inc(xn_ready, 1)
                for m in range(IMAGES // 2 + 2):
                    if m < IMAGES // 2:
                        dve.wait_ge(logits_ready, m + 1)
                        nc.vector.tensor_reduce(out=peak[:, 2 * m:2 * m + 2],
                                                in_=ps[:, 1 + m % 2, :].rearrange("p (b n) -> p b n", b=2),
                                                axis=AX.X, op=ALU.max, negate=True).then_inc(peak_ready, 1)
                    if m >= 2:
                        dve.wait_ge(weighted_ready, m - 1)
                        nc.vector.tensor_reduce(out=pooled[:, 2 * m - 4:2 * m - 2], in_=weighted[:, (m - 2) % 2],
                                                axis=AX.X, op=ALU.add).then_inc(pooled_part, 1)
                dve.wait_ge(prob_ready, IMAGES // 2)
                dve.wait_ge(pooled_part, IMAGES // 2)
                link(nc.vector.reciprocal(peak, total))
                nc.vector.tensor_tensor(pooled, pooled, peak, ALU.mult).then_inc(pooled_ready, 1)
                dve.wait_ge(small_on_pe, 1)
                nc.vector.tensor_copy(squeezed[:], ps[0:C2, 0, 0:IMAGES]).then_inc(small_on_dve, 1)
                dve.wait_ge(small_on_act, 1)
                link(nc.vector.tensor_tensor(summed, halves, rstd, ALU.mult))
                nc.vector.tensor_tensor(summed, summed, gate, ALU.mult).then_inc(small_on_dve, 1)
                dve.wait_ge(small_on_pe, 3)
                nc.vector.tensor_reduce(out=q_one[:, 0:1], in_=ps[0:IMAGES, 3, 0:C2], axis=AX.X, op=ALU.max,
                                        negate=True).then_inc(small_on_dve, 1)
                dve.wait_ge(small_on_act, 2)
                link(nc.vector.reciprocal(q_one[:, 2:3], q_one[:, 1:2]))
                nc.vector.tensor_scalar(q_small[:], q_exp[:], q_one[:, 2:3], None, ALU.mult).then_inc(small_on_dve, 1)
                dve.wait_ge(small_on_pe, 4)
                nc.vector.tensor_copy(qT[:], ps[0:C2, 4, 0:IMAGES]).then_inc(small_on_dve, 1)
                dve.wait_ge(small_on_pe, 5)
                link(nc.vector.tensor_tensor(vw, ps[:, 3, 0:IMAGES], gate, ALU.mult))

                def widen(b):
                    if b >= 4:
                        dve.wait_ge(place_on_pe, (b - 4) // 2 + 1)
                    nc.vector.tensor_copy(v_wide[:, b % 4, :], vw[:, b:b + 1].to_broadcast([128, 128]))\
                        .then_inc(wide_ready, 1)

                for b in range(4):
                    widen(b)
                for m in range(IMAGES // 2):
                    dve.wait_ge(place_ready, m + 1)
                    if m >= 2:
                        dve.wait_ge(out_ready, m - 1)
                    for a in range(2):
                        b = 2 * m + a
                        last = nc.vector.scalar_tensor_tensor(out=gated[:, m % 2, a, :], in0=xn[:, b, :],
                                                              scalar=gate[:, b:b + 1], in1=place[:, m % 2, a, :],
                                                              op0=ALU.mult, op1=ALU.mult)
                    last.then_inc(gated_ready, 1)
                    for b in (2 * m + 4, 2 * m + 5):
                        if b < IMAGES:
                            widen(b)


def attention(nc, mode, src, tokens, w, ident, q_bias, v_bias, o_bias, spread_rows, pick, mask, ps):
    softmax = mode != "linear"
    pieces = [(0, 2, 0), (1, 2, 256)] if mode == "softmax" else [(0, 1, 0), (1, 2, 128)]
    blocks = [(0, 0, 2, 0), (1, 0, 2, 256)] if mode == "softmax" else [(0, 0, 2, 0), (1, 1, 1, 256)]
    WIDE = 128 * sum(m for _, _, m, _ in blocks)
    LAG = 6

    with stage(nc, mode) as (sb, sem):
        xs = sb("xs", [128, 2, N])
        full = None if softmax else sb("full", [128, 2, N])
        high = sb("high", [128, 2, 2, N], FP32R)
        low = sb("low", [128, 2, 2, N], FP32R)
        stack = sb("stack", [128, 2, 8, N], FP32R)
        vaug = sb("vaug", [128, 2, 2, H, 32])
        prob = sb("prob", [128, H, WIDE])
        heads = sb("heads", [128, 2, 2, 128])
        recip = sb("recip", [128, 2, 2, 4])
        normed = sb("normed", [128, 2, 2, 4, 16])
        normedT = sb("normedT", [128, 2, 128])
        if softmax:
            negmax = sb("negmax", [128, 2, 2, 4])
            parts = sb("parts", [128, 2, 2, 2, 64], FP32R)
            maxT = sb("maxT", [128, 2, N], FP32R)

        xs_ready = [sem(f"xs_ready{u}") for u in range(2)]
        qk_projected = sem("qk_projected")
        full_ready = sem("full_ready")
        high_ready = sem("high_ready")
        low_ready = sem("low_ready")
        spread = sem("spread")
        query_stacks = sem("query_stacks")
        key_stacks = sem("key_stacks")
        v_projected = sem("v_projected")
        vaug_ready = sem("vaug_ready")
        zeros_set = sem("zeros_set")
        bias_added = sem("bias_added")
        scored = sem("scored")
        max_ready = sem("max_ready")
        high_max = sem("high_max")
        parts_ready = sem("parts_ready")
        max_turned = sem("max_turned")
        maxT_ready = sem("maxT_ready")
        key_scored = sem("key_scored")
        prob_ready = sem("prob_ready")
        weighted = sem("weighted")
        heads_ready = sem("heads_ready")
        heads_turned = sem("heads_turned")
        recip_ready = sem("recip_ready")
        normed_ready = sem("normed_ready")
        normed_turned = sem("normed_turned")
        normedT_ready = sem("normedT_ready")
        out_projected = sem("out_projected")
        tokens_ready = sem("tokens_ready")

        SCORE, KEY_SCORE, HEADS, MISC = 2, 4, 6, 7
        VALUES, OUTPUT = (MISC, MISC) if softmax else (2, 3)
        score_bank = [0, 1, 1, 0, 1, 0, 0, 1]
        max_bank = [1, 0]

        def steps(engine, step):
            for n in range(3):
                step(n, n % 2)
            with engine.Fori(1, IMAGES // 2 - 1) as i:
                step(2 * i + 1, 1)
                step(2 * i + 2, 0)
            for n in range(IMAGES - 1, IMAGES + 2):
                step(n, n % 2)

        AT = {
            "softmax": {
                "project": 1, "high": 1, "low": 2, "spread": (4, 5, 5, 7), "queries": (4, 6), "keys": (5, 7),
                "project_v": 0, "values": 0, "weigh": (3, 7), "take_heads": 6, "turn_heads": 2, "normalise": 2,
                "turn_normed": 4, "take_normed": 5, "project_out": 7, "add_out": 7,
            },
            "window": {
                "project": 1, "high": 1, "low": 2, "spread": (4, 5, 6, 7), "queries": (4, 6), "keys": (5, 7),
                "project_v": 0, "values": 1, "weigh": (3, 7), "take_heads": 7, "turn_heads": 2, "normalise": 3,
                "turn_normed": 5, "take_normed": 5, "project_out": 7, "add_out": 7,
            },
            "linear": {
                "project": 1, "high": 0, "low": 2, "spread": (4, 5, 6, 7), "queries": (4, 6), "keys": (5, 7),
                "project_v": 0, "values": 0, "weigh": (3, 6), "take_heads": 7, "turn_heads": 1, "normalise": 1,
                "turn_normed": 5, "take_normed": 5, "project_out": 7, "add_out": 7,
            },
        }[mode]

        def runs(n):
            return not isinstance(n, int) or 0 <= n < IMAGES

        def after(n, images):
            return not isinstance(n, int) or n >= images

        def lagging(n, u, k):
            return (n, u, k - LAG) if k >= LAG else (n - 1, 1 - u, k + H - LAG)

        with nc.Block() as block:
            @block.gpsimd
            def _(pool):
                if softmax:
                    nc.gpsimd.memset(parts[:].bitcast(FP32), 0.0).then_inc(zeros_set, 1)
                nc.gpsimd.memset(vaug[:], 0.0).then_inc(zeros_set, 1)
                pool.wait_ge(zeros_set, 2 if softmax else 1)
                nc.gpsimd.memset(vaug[:, :, :, :, 16:17], 1.0).then_inc(zeros_set, 1)
                if o_bias is not None:
                    for t in range(0, TILES, 8):
                        nc.gpsimd.tensor_tensor(tokens[:, t:t + 8, :], tokens[:, t:t + 8, :],
                                                o_bias[:, None, :].to_broadcast([128, 8, C]), ALU.add)\
                            .then_inc(bias_added, 1)

            @block.sync
            def _(sp):
                def load(n, u):
                    at = n * N if isinstance(n, int) else sp.snap(n * N)
                    if after(n, 2):
                        sp.wait_ge(v_projected, n - 1)
                    sp.dma_start(xs[:, u, :], src[:, bass.ds(at, N)]).then_inc(xs_ready[u], 16)

                load(0, 0)
                load(1, 1)

                with sp.Fori(1, IMAGES // 2) as i:
                    load(2 * i, 0)
                    load(2 * i + 1, 1)

            @block.tensor
            def _(pe):
                def project(n, u):
                    if after(n, 1):
                        pe.wait_ge(query_stacks, 2 * n)
                    for i in range(2):
                        mm = nc.tensor.matmul(ps[:, u, i * N:(i + 1) * N], w["qk"][:, i, :],
                                              src[:, bass.ds(n * N, N)],
                                              start=True, stop=True)
                    mm.then_inc(qk_projected, 1)

                def spread_out(n, u, i):
                    if i == 0:
                        pe.wait_ge(high_ready, n + 1)
                        pe.wait_ge(low_ready, n + 1)
                        if after(n, 1):
                            pe.wait_ge(key_stacks, 2 * n)
                    if i >= 2:
                        pe.wait_ge(key_stacks if i % 2 else query_stacks, 2 * n + 1)
                    for g in range(2):
                        pair, kind = 2 * (i // 2) + g, i % 2
                        out = ps[:, (u + i + 1) % 2, g * N:(g + 1) * N]
                        nc.tensor.matmul(out, spread_rows[:, 2 * kind, pair, :], high[:, u, kind, :],
                                         start=True, stop=False)
                        mm = nc.tensor.matmul(out, spread_rows[:, 2 * kind + 1, pair, :], low[:, u, kind, :],
                                              start=False, stop=True)
                    mm.then_inc(spread, 1)

                def project_v(n, u):
                    pe.wait_ge(xs_ready[u], 8 * n + 16 - 8 * u)
                    if softmax and after(n, 2):
                        pe.wait_ge(tokens_ready, n - 1)
                    if after(n, 1):
                        pe.wait_ge(vaug_ready, n)
                    for a in range(2):
                        mm = nc.tensor.matmul(ps[:, VALUES, a * 128:(a + 1) * 128], xs[:, u, a * 128:(a + 1) * 128],
                                              w["v"][:], start=True, stop=True)
                    mm.then_inc(v_projected, 1)

                def stacks(n, k):
                    if k % 4 == 0:
                        pe.wait_ge(query_stacks, 2 * n + 1 + k // 4)
                        pe.wait_ge(key_stacks, 2 * n + 1 + k // 4)

                def score(n, u, k):
                    stacks(n, k)
                    if k == 3 and after(n, 1):
                        pe.wait_ge(maxT_ready, 2 * n)
                    if k == 7:
                        pe.wait_ge(maxT_ready, 2 * n + 1)
                    if k < 2 and after(n, 1):
                        pe.wait_ge(max_ready, 8 * n - 1 + k)
                    if k == 3 and not after(n, 1):
                        pe.wait_ge(max_ready, 1)
                    if k in (2, 4, 5, 6):
                        pe.wait_ge(max_ready, 8 * n + {2: 2, 4: 3, 5: 4, 6: 6}[k])
                    rows = slice(64 * (k % 2), 64 * (k % 2) + 64)
                    q, key = stack[rows, u, k // 2, :], stack[rows, u, 4 + k // 2, :]
                    bank = ps[:, SCORE + score_bank[k], :]
                    if mode == "window":
                        nc.tensor.matmul(bank[:, 0:WIDE], mask["ident"][:], mask["rows"][:], start=True, stop=False)
                    for a, m, at in pieces:
                        mm = nc.tensor.matmul(bank[:, at:at + 128 * m], q[:, a * 128:(a + 1) * 128], key[:, 0:128 * m],
                                              start=mode != "window", stop=mode != "window" or a == 1)
                    mm.then_inc(scored, 1)

                def turn_max(n, g):
                    pe.wait_ge(parts_ready, 2 * n + g + 1)
                    if g == 0:
                        pe.wait_ge(max_ready, 8 * n + 5)
                    elif not isinstance(n, int) or n < IMAGES - 1:
                        pe.wait_ge(max_ready, 8 * n + 9)
                    for a in range(2):
                        mm = nc.tensor.transpose(ps[:, SCORE + max_bank[g], a * 128:(a + 1) * 128],
                                                 parts[:, g, a].bitcast(FP32).rearrange("p r h -> p (r h)"), ident[:])
                    mm.then_inc(max_turned, 1)

                def key_score(n, u, k):
                    stacks(n, k)
                    if softmax and k % 4 == 0:
                        pe.wait_ge(maxT_ready, 2 * n + k // 4 + 1)
                    if after(n, 1) or k >= 2:
                        pe.wait_ge(prob_ready, 8 * n + k - 1)
                    rows = slice(64 * (k % 2), 64 * (k % 2) + 64)
                    q, key = stack[rows, u, k // 2, :], stack[rows, u, 4 + k // 2, :]
                    bank = ps[:, KEY_SCORE + k % 2, :]
                    if mode == "window":
                        nc.tensor.matmul(bank[:, 0:WIDE], mask["ident"][:], mask["columns"][:], start=True, stop=False)
                    for b, a, m, at in blocks:
                        out, queries = bank[:, at:at + 128 * m], slice(a * 128, (a + m) * 128)
                        if softmax:
                            nc.tensor.matmul(out, pick[rows, k % 4, :], maxT[rows, k // 4, queries],
                                             start=mode == "softmax", stop=False)
                        mm = nc.tensor.matmul(out, key[:, b * 128:(b + 1) * 128], q[:, queries],
                                              start=not softmax, stop=mode != "window" or b == 1)
                    mm.then_inc(key_scored, 1)

                def weigh(n, u, g):
                    if g == 0:
                        pe.wait_ge(vaug_ready, n + 1)
                        if after(n, 1):
                            pe.wait_ge(heads_ready, n)
                    pe.wait_ge(prob_ready, 8 * n + 4 * g + 4)
                    if mode == "softmax":
                        products = [(0, 0, 2, 0, True, False), (1, 0, 2, 256, False, True)]
                    else:
                        products = [(0, 0, 1, 0, True, True), (0, 1, 1, 128, True, False), (1, 1, 1, 256, False, True)]
                    for b, a, m, at, start, stop in products:
                        for h in range(4):
                            c = g * N + a * 128
                            mm = nc.tensor.matmul(ps[32 * h:32 * h + 32, HEADS, c:c + m * 128],
                                                  vaug[:, u, b, 4 * g + h, :],
                                                  prob[:, 4 * g + h, at:at + m * 128], start=start, stop=stop)
                    mm.then_inc(weighted, 1)

                def turn_heads(n):
                    pe.wait_ge(heads_ready, n + 1)
                    if softmax:
                        pe.wait_ge(vaug_ready, IMAGES if isinstance(n, int) and n == IMAGES - 1 else n + 2)
                        if after(n, 1):
                            pe.wait_ge(tokens_ready, n)
                    elif after(n, 1):
                        pe.wait_ge(normedT_ready, n)
                    for g in range(2):
                        for a in range(2):
                            mm = nc.tensor.transpose(ps[:, MISC, (2 * g + a) * 128:(2 * g + a + 1) * 128],
                                                     heads[:, g, a, :], ident[:])
                    mm.then_inc(heads_turned, 1)

                def turn_normed(n):
                    pe.wait_ge(normed_ready, 2 * n + 2)
                    for a in range(2):
                        mm = nc.tensor.transpose(ps[:, MISC, a * 128:(a + 1) * 128],
                                                 normed[:, a].rearrange("p g h d -> p (g h d)"), ident[:])
                    mm.then_inc(normed_turned, 1)

                def project_out(n):
                    pe.wait_ge(normedT_ready, n + 1)
                    if not softmax and after(n, 1):
                        pe.wait_ge(tokens_ready, n)
                    for a in range(2):
                        mm = nc.tensor.matmul(ps[:, OUTPUT, a * 128:(a + 1) * 128], normedT[:, a, :], w["o"][:],
                                              start=True, stop=True)
                    mm.then_inc(out_projected, 1)

                project(0, 0)
                for i in range(4):
                    spread_out(0, 0, i)

                def step(n, u):
                    for k in range(H):
                        if softmax and runs(n):
                            score(n, u, k)
                        if not softmax and runs(lagging(n, u, k)[0]):
                            key_score(*lagging(n, u, k))
                        if k == AT["project_v"] and runs(n - 1):
                            project_v(n - 1, 1 - u)
                        if k == 1 and softmax and runs(n - 1):
                            turn_max(n - 1, 1)
                        if k == AT["project"] and runs(n + 1):
                            project(n + 1, 1 - u)
                        if k == AT["turn_heads"] and runs(n - 2):
                            turn_heads(n - 2)
                        if k == AT["weigh"][0] and runs(n - 1):
                            weigh(n - 1, 1 - u, 0)
                        if k == AT["turn_normed"] and runs(n - 2):
                            turn_normed(n - 2)
                        if k == 5 and softmax and runs(n):
                            turn_max(n, 0)
                        if k == AT["project_out"] and runs(n - 2):
                            project_out(n - 2)
                        if k == AT["weigh"][1] and runs(n - 1):
                            weigh(n - 1, 1 - u, 1)
                        for i in range(4):
                            if k == AT["spread"][i] and runs(n + 1):
                                spread_out(n + 1, 1 - u, i)
                        if softmax and runs(lagging(n, u, k)[0]):
                            key_score(*lagging(n, u, k))

                steps(pe, step)

            @block.scalar
            def _(act):
                def round_high(n, u):
                    act.wait_ge(qk_projected if softmax else full_ready, n + 1)
                    if after(n, 2):
                        act.wait_ge(spread, 4 * n - 4)
                    if q_bias is not None:
                        for i in range(2):
                            last = nc.scalar.activation(high[:, u, i, :], ps[:, u, i * N:(i + 1) * N], ACT.Identity,
                                                        bias=q_bias[:, i:i + 1])
                    elif softmax:
                        last = nc.scalar.activation(high[:, u].rearrange("p i n -> p (i n)"), ps[:, u, :], ACT.Copy)
                    else:
                        last = nc.scalar.activation(high[:, u], full[:], ACT.Copy)
                    last.then_inc(high_ready, 1)

                def take_keys(n, u, g):
                    act.wait_ge(spread, 4 * n + 2 * g + 2)
                    if after(n, 2):
                        act.wait_ge(key_scored, 8 * n - 12 + 4 * g)
                    nc.scalar.activation(stack[:, u, 4 + 2 * g:6 + 2 * g, :].rearrange("p g n -> p (g n)"),
                                         ps[:, u, :], ACT.Copy).then_inc(key_stacks, 1)

                def take_queries(n, u, g):
                    act.wait_ge(spread, 4 * n + 2 * g + 1)
                    if after(n, 2):
                        act.wait_ge(key_scored, 8 * n - 12 + 4 * g)
                    nc.scalar.activation(stack[:, u, 2 * g:2 * g + 2, :].rearrange("p g n -> p (g n)"),
                                         ps[:, 1 - u, :], ACT.Copy).then_inc(query_stacks, 1)

                def take_max(n, g):
                    act.wait_ge(max_turned, 2 * n + g + 1)
                    if after(n, 1):
                        act.wait_ge(key_scored, 8 * n + 4 * g - 4)
                    nc.scalar.activation(maxT[:, g, :], ps[:, SCORE + max_bank[g], 0:N],
                                         ACT.Copy).then_inc(maxT_ready, 1)

                def exponential(n, u, k):
                    act.wait_ge(key_scored, 8 * n + k + 1)
                    if after(n, 1):
                        act.wait_ge(weighted, 2 * n + k // 4 - 1)
                    nc.scalar.activation(prob[:, k, :], ps[:, KEY_SCORE + k % 2, 0:WIDE],
                                         ACT.Exp).then_inc(prob_ready, 1)

                def take_heads(n):
                    act.wait_ge(weighted, 2 * n + 2)
                    if after(n, 1):
                        act.wait_ge(heads_turned, n)
                    nc.scalar.activation(heads[:].rearrange("p g a n -> p (g a n)"), ps[:, HEADS, :],
                                         ACT.Copy).then_inc(heads_ready, 1)

                def take_normed(n):
                    act.wait_ge(normed_turned, n + 1)
                    if after(n, 1):
                        act.wait_ge(out_projected, n)
                    nc.scalar.activation(normedT[:].rearrange("p a n -> p (a n)"), ps[:, MISC, 0:N],
                                         ACT.Copy).then_inc(normedT_ready, 1)

                round_high(0, 0)
                for g in range(2):
                    if not softmax:
                        take_queries(0, 0, g)
                    take_keys(0, 0, g)

                def step(n, u):
                    for k in range(H):
                        if k == 1 and softmax and runs(n - 1):
                            take_max(n - 1, 1)
                        if k == AT["high"] and runs(n + 1):
                            round_high(n + 1, 1 - u)
                        if k == 5 and softmax and runs(n):
                            take_max(n, 0)
                        if k == AT["take_normed"] and runs(n - 2):
                            take_normed(n - 2)
                        if softmax and runs(lagging(n, u, k)[0]):
                            exponential(*lagging(n, u, k))
                        for g in range(2):
                            if k == AT["queries"][g] and not softmax and runs(n + 1):
                                take_queries(n + 1, 1 - u, g)
                            if k == AT["keys"][g] and runs(n + 1):
                                take_keys(n + 1, 1 - u, g)
                        if k == AT["take_heads"] and runs(n - 1):
                            take_heads(n - 1)

                steps(act, step)

            @block.vector
            def _(dve):
                def evacuate(n, u):
                    dve.wait_ge(qk_projected, n + 1)
                    if after(n, 1):
                        dve.wait_ge(high_ready, n)
                    nc.vector.tensor_scalar(full[:].rearrange("p g n -> p (g n)"), ps[:, u, :],
                                            0.0, LINEAR_EPS, ALU.max, ALU.add).then_inc(full_ready, 1)

                def find_low(n, u):
                    if after(n, 2):
                        dve.wait_ge(spread, 4 * n - 4)
                    dve.wait_ge(high_ready, n + 1)
                    if q_bias is not None:
                        for i in range(2):
                            last = nc.vector.scalar_tensor_tensor(
                                out=low[:, u, i, :], in0=ps[:, u, i * N:(i + 1) * N], scalar=q_bias[:, i:i + 1],
                                in1=high[:, u, i, :].bitcast(FP32), op0=ALU.add, op1=ALU.subtract)
                    else:
                        whole = ps[:, u, :] if softmax else full[:].rearrange("p g n -> p (g n)")
                        last = nc.vector.tensor_tensor(low[:, u].rearrange("p i n -> p (i n)"), whole,
                                                       high[:, u].bitcast(FP32).rearrange("p i n -> p (i n)"),
                                                       ALU.subtract)
                    last.then_inc(low_ready, 1)

                def take_queries(n, u, g):
                    dve.wait_ge(spread, 4 * n + 2 * g + 1)
                    if after(n, 2):
                        dve.wait_ge(key_scored, 8 * n - 12 + 4 * g)
                    nc.vector.tensor_copy(stack[:, u, 2 * g:2 * g + 2, :].rearrange("p g n -> p (g n)"),
                                          ps[:, 1 - u, :]).then_inc(query_stacks, 1)

                def take_values(n, u):
                    dve.wait_ge(v_projected, n + 1)
                    if not after(n, 1):
                        dve.wait_ge(zeros_set, 3 if softmax else 2)
                    if after(n, 2):
                        dve.wait_ge(weighted, 2 * n - 2)
                    for a in range(2):
                        out = vaug[:, u, a, :, 0:16]
                        got = ps[:, VALUES, a * 128:(a + 1) * 128].rearrange("p (h d) -> p h d", d=D)
                        if v_bias is None:
                            last = nc.vector.tensor_copy(out, got)
                        else:
                            last = nc.vector.tensor_tensor(out, got, v_bias[:].rearrange("p (h d) -> p h d", d=D),
                                                           ALU.add)
                    last.then_inc(vaug_ready, 1)

                def maximum(n, k):
                    dve.wait_ge(scored, 8 * n + k + 1)
                    bank, g, h = ps[:, SCORE + score_bank[k], :], k // 4, k % 4
                    if mode == "softmax":
                        last = nc.vector.tensor_reduce(out=negmax[:, g, :, h],
                                                       in_=bank.rearrange("p (a n) -> p a n", a=2),
                                                       axis=AX.X, op=ALU.max, negate=True)
                    else:
                        for a, m, at in pieces:
                            last = nc.vector.tensor_reduce(out=negmax[:, g, a, h:h + 1], in_=bank[:, at:at + 128 * m],
                                                           axis=AX.X, op=ALU.max, negate=True)
                    last.then_inc(max_ready, 1)

                def split_max(n, g):
                    dve.wait_ge(max_ready, 8 * n + 4 * g + 4)
                    if not after(n, 1):
                        dve.wait_ge(zeros_set, 1)
                    else:
                        dve.wait_ge(max_turned, 2 * n + g - 1)
                    both = negmax[:, g, :, None, :].to_broadcast([128, 2, 2, 4])
                    nc.vector.tensor_copy(parts[:, g, :, :, 0:4], both).then_inc(high_max, 1)
                    dve.wait_ge(high_max, 2 * n + g + 1)
                    nc.vector.tensor_tensor(parts[:, g, :, :, 4:8], both, parts[:, g, :, :, 0:4].bitcast(FP32),
                                            ALU.subtract).then_inc(parts_ready, 1)

                def causal(n, u, k):
                    dve.wait_ge(key_scored, 8 * n + k + 1)
                    if after(n, 1):
                        dve.wait_ge(weighted, 2 * n + k // 4 - 1)
                    nc.vector.tensor_tensor(prob[:, k, :], ps[:, KEY_SCORE + k % 2, 0:WIDE],
                                            mask["keep"][:], ALU.mult).then_inc(prob_ready, 1)

                def normalise(n):
                    dve.wait_ge(heads_turned, n + 1)
                    turned = ps[:, MISC, :].rearrange("p (g a h d) -> p g a h d", g=2, a=2, h=4)
                    for g in range(2):
                        nc.vector.reciprocal(recip[:, g], turned[:, g, :, :, 16]).then_inc(recip_ready, 1)
                    dve.wait_ge(recip_ready, 2 * n + 2)
                    if after(n, 1):
                        dve.wait_ge(normed_turned, n)
                    for a in range(2):
                        nc.vector.tensor_tensor(
                            normed[:, a], turned[:, :, a, :, 0:16],
                            recip[:, :, a, :, None].to_broadcast([128, 2, 4, 16]), ALU.mult).then_inc(normed_ready, 1)

                def add_out(n):
                    dve.wait_ge(out_projected, n + 1)
                    if o_bias is not None and not after(n, 1):
                        dve.wait_ge(bias_added, TILES // 8)
                    at = tokens[:, bass.ds(2 * n, 2), :]
                    nc.vector.tensor_tensor(at, at, ps[:, OUTPUT, 0:N].rearrange("p (a c) -> p a c", a=2),
                                            ALU.add).then_inc(tokens_ready, 1)

                if not softmax:
                    evacuate(0, 0)
                find_low(0, 0)
                if softmax:
                    take_queries(0, 0, 0)
                    take_queries(0, 0, 1)

                def step(n, u):
                    for k in range(H):
                        if softmax and runs(n):
                            maximum(n, k)
                            if k % 4 == 3:
                                split_max(n, k // 4)
                        if not softmax and runs(lagging(n, u, k)[0]):
                            causal(*lagging(n, u, k))
                        if k == AT["project"] and not softmax and runs(n + 1):
                            evacuate(n + 1, 1 - u)
                        if k == AT["values"] and runs(n - 1):
                            take_values(n - 1, 1 - u)
                        if k == AT["low"] and runs(n + 1):
                            find_low(n + 1, 1 - u)
                        if k == AT["normalise"] and runs(n - 2):
                            normalise(n - 2)
                        for g in range(2):
                            if k == AT["queries"][g] and softmax and runs(n + 1):
                                take_queries(n + 1, 1 - u, g)
                        if k == AT["add_out"] and runs(n - 2):
                            add_out(n - 2)

                steps(dve, step)


def layer_norm(nc, name, tokens, normed, xf, ident, ps, gate=None):
    CHUNK = 8 if gate is None else 4
    CHUNKS = TILES // CHUNK
    with stage(nc, name) as (sb, sem):

        stats = sb("stats", [128, TILES, 6])
        small = sb("small", [128, 8, TILES])
        mean, dev, square, rest, var, std, rstd, shift = (small[:, i, :] for i in range(8))
        turned_sb = sb("turned", [128, 2, CHUNK * 128]) if gate is not None else None

        (stats_ready, mean_ready, var_ready, std_ready, scale_ready, act_normed, dve_normed, turned, taken,
         logits_ready) = (
            sem(n) for n in ("stats_ready", "mean_ready", "var_ready", "std_ready", "scale_ready", "act_normed",
                             "dve_normed", "turned", "taken", "logits_ready"))
        chained = sem("chained")

        def part(c):
            return slice(c * CHUNK, (c + 1) * CHUNK)

        with nc.Block() as block:
            @block.vector
            def _(dve):
                link = link_on(dve, chained)

                def measure(c):
                    for t in range(c * CHUNK, (c + 1) * CHUNK):
                        last = nc.vector.bn_stats(stats[:, t, :], tokens[:, t, :])
                    last.then_inc(stats_ready, 1)

                def variance(c):
                    dve.wait_ge(stats_ready, c + 1)
                    at = part(c)
                    even, odd = stats[:, at, 1], stats[:, at, 4]
                    nc.vector.tensor_tensor(dev[:, at], even, odd, ALU.subtract)
                    nc.vector.tensor_tensor(rest[:, at], stats[:, at, 2], stats[:, at, 5], ALU.add)
                    link(nc.vector.tensor_tensor(mean[:, at], even, odd, ALU.add))
                    link(nc.vector.tensor_tensor(square[:, at], dev[:, at], dev[:, at], ALU.mult))
                    nc.vector.tensor_scalar(mean[:, at], mean[:, at], 0.5, None, ALU.mult).then_inc(mean_ready, 1)
                    link(nc.vector.scalar_tensor_tensor(out=var[:, at], in0=square[:, at], scalar=C / 4.0,
                                                        in1=rest[:, at], op0=ALU.mult, op1=ALU.add))
                    nc.vector.tensor_scalar(var[:, at], var[:, at], 1.0 / C, LN_EPS, ALU.mult, ALU.add)\
                        .then_inc(var_ready, 1)

                def scale(c):
                    dve.wait_ge(std_ready, c + 1)
                    at = part(c)
                    link(nc.vector.reciprocal(rstd[:, at], std[:, at]))
                    dve.wait_ge(mean_ready, c + 1)
                    nc.vector.scalar_tensor_tensor(out=shift[:, at], in0=mean[:, at], scalar=-1.0, in1=rstd[:, at],
                                                   op0=ALU.mult, op1=ALU.mult).then_inc(scale_ready, 1)

                def normalise(c):
                    dve.wait_ge(scale_ready, c + 1)
                    for t in range(c * CHUNK, (c + 1) * CHUNK, 2):
                        last = nc.vector.tensor_scalar(normed[:, t, :], tokens[:, t, :], mean[:, t:t + 1],
                                                       rstd[:, t:t + 1], ALU.subtract, ALU.mult)
                    last.then_inc(dve_normed, 1)

                measure(0)
                for c in range(CHUNKS):
                    variance(c)
                    if c + 1 < CHUNKS:
                        measure(c + 1)
                    scale(c)
                    normalise(c)

            @block.scalar
            def _(act):
                def take(c):
                    act.wait_ge(turned, c + 1)
                    if xf is not None:
                        out = xf[:, c * CHUNK * 128:(c + 1) * CHUNK * 128]
                    else:
                        if c >= 2:
                            act.wait_ge(logits_ready, c - 1)
                        out = turned_sb[:, c % 2, :]
                    banks = ps[:, 2 * (c % 2):2 * (c % 2) + CHUNK // 4, :]
                    nc.scalar.activation(out, banks.rearrange("p a n -> p (a n)"), ACT.Copy).then_inc(taken, 1)

                for c in range(CHUNKS + 1):
                    if c < CHUNKS:
                        act.wait_ge(var_ready, c + 1)
                        nc.scalar.activation(std[:, part(c)], var[:, part(c)], ACT.Sqrt).then_inc(std_ready, 1)
                        act.wait_ge(scale_ready, c + 1)
                        for t in range(c * CHUNK + 1, (c + 1) * CHUNK, 2):
                            last = nc.scalar.activation(normed[:, t, :], tokens[:, t, :], ACT.Identity,
                                                        bias=shift[:, t:t + 1], scale=rstd[:, t:t + 1])
                        last.then_inc(act_normed, 1)
                    if c >= 1:
                        take(c - 1)

            @block.tensor
            def _(pe):
                def logits(c):
                    pe.wait_ge(taken, c + 1)
                    experts = gate.shape[1]
                    for a in range(CHUNK):
                        at = (c * CHUNK + a) * experts
                        mm = nc.tensor.matmul(ps[:, 7, at:at + experts], turned_sb[:, c % 2, a * 128:(a + 1) * 128],
                                              gate[:, :], start=True, stop=True)
                    mm.then_inc(logits_ready, 1)

                for c in range(CHUNKS):
                    pe.wait_ge(act_normed, c + 1)
                    pe.wait_ge(dve_normed, c + 1)
                    if c >= 2:
                        pe.wait_ge(taken, c - 1)
                    for a in range(CHUNK):
                        mm = nc.tensor.transpose(ps[:, 2 * (c % 2) + a // 4, a % 4 * 128:(a % 4 + 1) * 128],
                                                 normed[:, c * CHUNK + a, :], ident[:])
                    mm.then_inc(turned, 1)
                    if gate is not None and c >= 1:
                        logits(c - 1)
                if gate is not None:
                    logits(CHUNKS - 1)


def turn_experts(nc, raw, turned, arrived, ident, ps):
    def parts(stage_sem):
        transposed, taken = stage_sem("w1_turned"), stage_sem("w1_taken")

        def tensor(pe):
            pe.wait_ge(arrived, 32)
            for e in range(E2):
                if e >= 4:
                    pe.wait_ge(taken, e - 3)
                for k in range(FC):
                    mm = nc.tensor.transpose(ps[:, 2 + e % 4, k * 128:(k + 1) * 128], raw[:, e * FC + k, :], ident[:])
                mm.then_inc(transposed, 1)

        def scalar(act):
            for e in range(E2):
                act.wait_ge(transposed, e + 1)
                nc.scalar.activation(turned[:, e, :], ps[:, 2 + e % 4, :], ACT.Copy).then_inc(taken, 1)
        return tensor, scalar
    return parts


def route(nc, name, experts, taken, tiles, bias, consts, normed, slots, position, tile_expert, weight, counts,
          tile_choice, ps, beside=None):
    with stage(nc, name) as (sb, sem):

        wide = [128, TILES, experts]
        logits = sb("logits", wide)
        chosen = [sb(f"chosen{k}", wide) for k in range(taken)]
        scratch = sb("scratch", wide)
        select = sb("select", wide) if taken > 1 else chosen[0]
        running = [sb(f"running{i}", wide) for i in range(2)]
        top = sb("top", [128, taken, TILES])
        first = sb("first", [128, TILES])
        ends = sb("ends", [128, 6, experts])
        ends_int = sb("ends_int", [128, experts], INT32)
        slot_of = sb("slot_of", [128, TILES])
        past = sb("past", [128, tiles, experts])
        expert_of = sb("expert_of", [128, tiles])
        own_expert = sb("own_expert", [128, 1])
        width = slots.shape[1]
        zero = sb("zero", [128, 4, width])

        chosen_ready = sem("chosen_ready")
        counted = sem("counted")
        gap_ready = sem("gap_ready")
        exp_ready = sem("exp_ready")
        zero_set = sem("zero_set")
        cleared = sem("cleared")
        placed = sem("placed")
        scattered = sem("scattered")
        chained = sem("chained")

        beside_tensor, beside_scalar = beside(sem) if beside else (None, None)

        def over(ap, shape=None):
            return ap.to_broadcast(shape or wide)

        with nc.Block() as block:
            @block.tensor
            def _(pe):
                pe.wait_ge(chosen_ready, 1)
                flat = select[:].rearrange("p t e -> p (t e)")
                nc.tensor.matmul(ps[:, 0, 0:TILES * experts], consts["before"][:], flat, start=True,
                                 stop=True).then_inc(counted, 1)
                nc.tensor.matmul(ps[:, 1, 0:TILES * experts], consts["ones"][:], flat, start=True,
                                 stop=True).then_inc(counted, 1)
                if beside:
                    beside_tensor(pe)

            @block.scalar
            def _(act):
                act.wait_ge(gap_ready, 1)
                if taken == 2:
                    nc.scalar.activation(first[:], first[:], ACT.Exp).then_inc(exp_ready, 1)
                else:
                    nc.scalar.activation(scratch[:].rearrange("p t e -> p (t e)"),
                                         scratch[:].rearrange("p t e -> p (t e)"), ACT.Exp).then_inc(exp_ready, 1)
                if beside:
                    beside_scalar(act)

            @block.sync
            def _(sp):
                sp.wait_ge(zero_set, 2 if width > C else 1)
                for i in range(tiles // 4):
                    sp.dma_start(slots[512 * i:512 * i + 512, :].rearrange("(a p) c -> p a c", p=128), zero[:])\
                        .then_inc(cleared, 16)
                sp.wait_ge(cleared, tiles // 4 * 16)

            @block.gpsimd
            def _(pool):
                nc.gpsimd.memset(zero[:, :, 0:C], 0.0).then_inc(zero_set, 1)
                if width > C:
                    nc.gpsimd.memset(zero[:, :, C:], 1.0).then_inc(zero_set, 1)
                pool.wait_ge(cleared, tiles // 4 * 16)
                for k in range(taken):
                    pool.wait_ge(placed, k + 1)
                    for t in range(TILES):
                        nc.gpsimd.indirect_dma_start(
                            out=slots[:, :], out_offset=bass.IndirectOffsetOnAxis(ap=position[:, k, t:t + 1], axis=0),
                            in_=normed[:, t, :], in_offset=None, bounds_check=tiles * 128 - 1).then_inc(scattered, 16)
                pool.wait_ge(scattered, 16 * taken * TILES)

            @block.vector
            def _(dve):
                link = link_on(dve, chained)
                got = ps[:, 7, 0:TILES * experts].rearrange("p (t e) -> p t e", e=experts)
                if bias is None:
                    link(nc.vector.tensor_copy(logits[:], got))
                else:
                    link(nc.vector.tensor_tensor(logits[:], got, over(bias[:, None, :]), ALU.add))
                index = over(consts["index"][:, None, 0:experts])
                work = logits
                for k in range(taken):
                    link(nc.vector.tensor_reduce(out=top[:, k, :], in_=work[:], axis=AX.X, op=ALU.max))
                    link(nc.vector.tensor_tensor(scratch[:], work[:], over(top[:, k, :, None]), ALU.is_equal))
                    link(nc.vector.tensor_tensor(scratch[:], scratch[:], index, ALU.mult))
                    link(nc.vector.tensor_reduce(out=first[:], in_=scratch[:], axis=AX.X, op=ALU.min))
                    picked = nc.vector.tensor_tensor(chosen[k][:], index, over(first[:, :, None]), ALU.is_equal)
                    if taken == 1:
                        picked.then_inc(chosen_ready, 1)
                        dve.wait_ge(chosen_ready, 1)
                    else:
                        link(picked)
                    if k + 1 < taken:
                        link(nc.vector.scalar_tensor_tensor(
                            out=running[0][:].rearrange("p t e -> p (t e)"),
                            in0=chosen[k][:].rearrange("p t e -> p (t e)"), scalar=MASKED,
                            in1=work[:].rearrange("p t e -> p (t e)"), op0=ALU.mult, op1=ALU.add))
                        work = running[0]
                if taken == 2:
                    nc.vector.tensor_tensor(select[:], chosen[0][:], chosen[1][:], ALU.add).then_inc(chosen_ready, 1)
                    nc.vector.tensor_tensor(first[:], top[:, 1, :], top[:, 0, :], ALU.subtract).then_inc(gap_ready, 1)
                else:
                    nc.vector.tensor_tensor(scratch[:], logits[:], over(top[:, 0, :, None]), ALU.subtract)\
                        .then_inc(gap_ready, 1)
                dve.wait_ge(counted, 2)
                link(nc.vector.tensor_copy(running[0][:].rearrange("p t e -> p (t e)"), ps[:, 1, 0:TILES * experts]))
                a, b, step = running[0], running[1], 1
                while step < TILES:
                    nc.vector.tensor_copy(b[:, 0:step, :], a[:, 0:step, :])
                    link(nc.vector.tensor_tensor(b[:, step:, :], a[:, step:, :], a[:, 0:TILES - step, :], ALU.add))
                    a, b, step = b, a, 2 * step
                total, padded, one, other, start = (ends[:, i, :] for i in range(5))
                link(nc.vector.tensor_copy(total, a[:, TILES - 1, :]))
                link(nc.vector.tensor_tensor(b[:].rearrange("p t e -> p (t e)"), a[:].rearrange("p t e -> p (t e)"),
                                             ps[:, 1, 0:TILES * experts], ALU.subtract))
                link(nc.vector.tensor_tensor(b[:].rearrange("p t e -> p (t e)"), b[:].rearrange("p t e -> p (t e)"),
                                             ps[:, 0, 0:TILES * experts], ALU.add))
                link(nc.vector.tensor_scalar(ends_int[:], total, 127.0, None, ALU.add))
                link(nc.vector.tensor_single_scalar(ends_int[:], ends_int[:], 7, ALU.arith_shift_right))
                link(nc.vector.tensor_copy(padded, ends_int[:]))
                link(nc.vector.tensor_copy(one, padded))
                step = 1
                while step < experts:
                    nc.vector.tensor_copy(other[:, 0:step], one[:, 0:step])
                    link(nc.vector.tensor_tensor(other[:, step:], one[:, step:], one[:, 0:experts - step], ALU.add))
                    one, other, step = other, one, 2 * step
                link(nc.vector.tensor_tensor(start, one, padded, ALU.subtract))
                link(nc.vector.tensor_scalar(start, start, 128.0, None, ALU.mult))
                link(nc.vector.tensor_tensor(b[:], b[:], over(start[:, None, :]), ALU.add))
                for k in range(taken):
                    link(nc.vector.tensor_tensor(a[:], chosen[k][:], b[:], ALU.mult))
                    link(nc.vector.tensor_reduce(out=slot_of[:], in_=a[:], axis=AX.X, op=ALU.add))
                    nc.vector.tensor_copy(position[:, k, :], slot_of[:]).then_inc(placed, 1)
                shape = [128, tiles, experts]
                link(nc.vector.tensor_tensor(past[:], over(one[:, None, :], shape),
                                             over(consts["tile"][:, 0:tiles, None], shape), ALU.is_le))
                link(nc.vector.tensor_reduce(out=expert_of[:], in_=past[:], axis=AX.X, op=ALU.add))
                link(nc.vector.tensor_scalar(tile_expert[:], expert_of[:], float(experts - 1), None, ALU.min))
                dve.wait_ge(exp_ready, 1)
                if taken == 2:
                    link(nc.vector.tensor_scalar(tile_choice[:], one, consts["row"][:, 0:1], None, ALU.is_le))
                    link(nc.vector.tensor_reduce(out=own_expert[:], in_=tile_choice[:], axis=AX.X, op=ALU.add))
                    link(nc.vector.tensor_scalar(own_expert[:], own_expert[:], float(experts - 1), -float(experts),
                                                 ALU.min, ALU.add))
                    link(nc.vector.tensor_scalar(tile_choice[:], consts["index"][:, 0:experts], own_expert[:, 0:1],
                                                 None, ALU.is_equal))
                    link(nc.vector.tensor_scalar(counts[:], total, 1.0, None, ALU.max))
                    link(nc.vector.reciprocal(counts[:], counts[:]))
                    link(nc.vector.tensor_scalar(slot_of[:], first[:], 1.0, None, ALU.add))
                    link(nc.vector.reciprocal(slot_of[:], slot_of[:]))
                    link(nc.vector.tensor_tensor(first[:], first[:], slot_of[:], ALU.mult))
                    link(nc.vector.tensor_tensor(chosen[0][:], chosen[0][:], over(slot_of[:, :, None]), ALU.mult))
                    link(nc.vector.tensor_tensor(chosen[1][:], chosen[1][:], over(first[:, :, None]), ALU.mult))
                    link(nc.vector.tensor_tensor(weight[:], chosen[0][:], chosen[1][:], ALU.add))
                else:
                    link(nc.vector.tensor_reduce(out=slot_of[:], in_=scratch[:], axis=AX.X, op=ALU.add))
                    link(nc.vector.reciprocal(weight[:], slot_of[:]))


BODY = 8
GROUPED = 4


def past(s, tiles):
    return not isinstance(s, int) or s >= tiles


def slot_loop(engine, count, step):
    for r in range(BODY):
        step(r, r)
    with engine.Fori(1, count // BODY - 1) as i:
        for r in range(BODY):
            step(BODY * i + r, r)
    for r in range(BODY):
        step(count - BODY + r, r)


def load_slots(sp, slots, xs, loaded, used, count):
    def step(s, r):
        if r % GROUPED:
            return
        u = r // GROUPED
        at = s * 128 if isinstance(s, int) else sp.snap(s * 128)
        if past(s, BODY):
            sp.wait_ge(used, s - GROUPED)
        sp.dma_start(xs[:, u], slots[bass.ds(at, GROUPED * 128), :].rearrange("(a p) c -> p a c", p=128))\
            .then_inc(loaded[u], 16)
    slot_loop(sp, count, step)


def turn_slots(nc, pe, xs, loaded, xT_ready, turned, ident, ps, bank, s, r):
    if r % GROUPED == 0:
        u = r // GROUPED
        pe.wait_ge(loaded[u], 2 * s + 16 - 8 * u)
    if past(s, 2):
        pe.wait_ge(xT_ready, s - 1)
    nc.tensor.transpose(ps[:, bank + r % 2, 0:128], xs[:, r // GROUPED, r % GROUPED, 0:C],
                        ident[:]).then_inc(turned, 1)


def take_turned(nc, act, xT, turned, up_done, xT_ready, ps, bank, s, r):
    act.wait_ge(turned, s + 1)
    if past(s, 4):
        act.wait_ge(up_done, s - 3)
    nc.scalar.activation(xT[:, r % 4, :], ps[:, bank + r % 2, 0:128], ACT.Copy).then_inc(xT_ready, 1)


def fetch_weights(nc, dve, weights, own, ring, tile_expert, used, own_ready, s, r):
    e = dve.value_load(tile_expert[0:1, bass.ds(s, 1)], min_val=0, max_val=weights.shape[1] - 1)
    if past(s, ring):
        dve.wait_ge(used, s - ring + 1)
    nc.vector.tensor_copy(own[:, r % ring, :], weights[:, bass.ds(e, 1), :].rearrange("p a f -> p (a f)"))\
        .then_inc(own_ready, 1)


def multiply_up(nc, pe, own, ring, xT, own_ready, xT_ready, read, up_done, ps, bank, s, r):
    pe.wait_ge(own_ready, s + 1)
    pe.wait_ge(xT_ready, s + 1)
    if past(s, 2):
        pe.wait_ge(read, s - 1)
    for c in range(FC):
        mm = nc.tensor.matmul(ps[:, bank + r % 2, c * 128:(c + 1) * 128], own[:, r % ring, c * 128:(c + 1) * 128],
                              xT[:, r % 4, :], start=True, stop=True)
    mm.then_inc(up_done, 1)


def expert_sums(nc, slots, tile_expert, w1T, partial, consts, ps):
    with stage(nc, "sums") as (sb, sem):
        xs = sb("xs", [128, 2, GROUPED, C])
        xT = sb("xT", [128, 4, 128])
        own = sb("own", [128, 4, F])
        hidden = sb("hidden", [128, 2, F])
        loaded = [sem(f"loaded{u}") for u in range(2)]
        turned, xT_ready, own_ready, up_done, hidden_ready, summed = (
            sem(n) for n in ("turned", "xT_ready", "own_ready", "up_done", "hidden_ready", "summed"))
        TURN, UP = 0, 2

        def inside(s):
            return not isinstance(s, int) or s < S2

        with nc.Block() as block:
            @block.sync
            def _(sp):
                load_slots(sp, slots, xs, loaded, turned, S2)

            @block.tensor
            def _(pe):
                def turn(s, r):
                    turn_slots(nc, pe, xs, loaded, xT_ready, turned, consts["ident"], ps, TURN, s, r)

                turn(0, 0)
                turn(1, 1)

                def step(s, r):
                    if inside(s + 2):
                        turn(s + 2, (r + 2) % BODY)
                    multiply_up(nc, pe, own, 4, xT, own_ready, xT_ready, hidden_ready, up_done, ps, UP, s, r)
                slot_loop(pe, S2, step)

            @block.scalar
            def _(act):
                def take(s, r):
                    take_turned(nc, act, xT, turned, up_done, xT_ready, ps, TURN, s, r)

                take(0, 0)
                take(1, 1)

                def step(s, r):
                    if inside(s + 2):
                        take(s + 2, (r + 2) % BODY)
                    act.wait_ge(up_done, s + 1)
                    if past(s, 2):
                        act.wait_ge(summed, s - 1)
                    nc.scalar.activation(hidden[:, r % 2, :], ps[:, UP + r % 2, :], ACT.Silu).then_inc(hidden_ready, 1)
                slot_loop(act, S2, step)

            @block.vector
            def _(dve):
                def fetch(s, r):
                    fetch_weights(nc, dve, w1T, own, 4, tile_expert, up_done, own_ready, s, r)

                def total(s, r):
                    dve.wait_ge(hidden_ready, s + 1)
                    nc.vector.tensor_reduce(out=partial[:, bass.ds(s, 1), :].rearrange("p s c -> p (s c)"),
                                            in_=hidden[:, r % 2, :].rearrange("p (c n) -> p c n", c=FC),
                                            axis=AX.X, op=ALU.add).then_inc(summed, 1)

                for s in range(3):
                    fetch(s, s)

                def step(s, r):
                    if inside(s + 3):
                        fetch(s + 3, (r + 3) % BODY)
                    if past(s, 1):
                        total(s - 1, (r - 1) % BODY)
                slot_loop(dve, S2, step)
                total(S2 - 1, BODY - 1)


def mix_means(nc, partial, tile_choice, w2, inverse, weight, tokens, consts, ps):
    PARTS = TILES * E2 // 128
    PER = 128 // E2
    with stage(nc, "mix") as (sb, sem):

        product = sb("product", [128, F])
        means = sb("means", [128, PER, E2])
        meansT = sb("meansT", [128, C])
        spread = sb("spread", [128, PER, C])
        weightT = sb("weightT", [128, PARTS, 128])
        partial_high, partial_low = sb("partial_high", [S2, F], FP32R), sb("partial_low", [S2, F], FP32R)
        choice = sb("choice", [S2, E2], FP32R)
        partial_turned, high_ready, low_ready, summed, product_done = (
            sem(n) for n in ("partial_turned", "high_ready", "low_ready", "summed", "product_done"))
        turned, weightT_ready, means_ready, means_turned, spread_ready, mixed, added, chained = (
            sem(n) for n in ("turned", "weightT_ready", "means_ready", "means_turned", "spread_ready", "mixed",
                             "added", "chained"))
        with nc.Block() as block:
            @block.tensor
            def _(pe):
                for g in range(PARTS):
                    mm = nc.tensor.transpose(ps[:, 0, g * 128:(g + 1) * 128],
                                             weight[:, g * PER:(g + 1) * PER, :].rearrange("p t e -> p (t e)"),
                                             consts["ident"][:])
                mm.then_inc(turned, 1)
                for c in range(FC):
                    mm = nc.tensor.transpose(ps[0:S2, 1, c * 128:(c + 1) * 128], partial[:, :, c], consts["ident"][:])
                mm.then_inc(partial_turned, 1)
                pe.wait_ge(weightT_ready, 1)
                pe.wait_ge(high_ready, 1)
                pe.wait_ge(low_ready, 2)
                for e in range(E2):
                    if e >= 6:
                        pe.wait_ge(product_done, e - 5)
                    own = choice[:, e:e + 1].to_broadcast([S2, 128])
                    nc.tensor.matmul(ps[:, 2 + e % 6, :], own, partial_high[:], start=True, stop=False)
                    nc.tensor.matmul(ps[:, 2 + e % 6, :], own, partial_low[:], start=False,
                                     stop=True).then_inc(summed, 1)
                pe.wait_ge(means_ready, 1)
                nc.tensor.transpose(ps[:, 1, 0:128], means[:].rearrange("p j e -> p (j e)"),
                                    consts["ident"][:]).then_inc(means_turned, 1)
                pe.wait_ge(spread_ready, 1)
                flat = spread[:].rearrange("p j c -> p (j c)")
                for g in range(PARTS):
                    for a in range(2):
                        i = 2 * g + a
                        if i >= 4:
                            pe.wait_ge(added, i - 3)
                        nc.tensor.matmul(ps[:, 2 + i % 4, :], weightT[:, g, :], flat[:, a * 512:(a + 1) * 512],
                                         start=True, stop=True).then_inc(mixed, 1)

            @block.scalar
            def _(act):
                act.wait_ge(turned, 1)
                nc.scalar.activation(weightT[:].rearrange("p g t -> p (g t)"), ps[:, 0, :],
                                     ACT.Copy).then_inc(weightT_ready, 1)
                act.wait_ge(partial_turned, 1)
                nc.scalar.activation(partial_high[:], ps[0:S2, 1, :], ACT.Copy).then_inc(high_ready, 1)

            @block.vector
            def _(dve):
                link = link_on(dve, chained)
                dve.wait_ge(partial_turned, 1)
                nc.vector.tensor_copy(choice[:], tile_choice[0:S2, :]).then_inc(low_ready, 1)
                dve.wait_ge(high_ready, 1)
                nc.vector.tensor_tensor(partial_low[:], ps[0:S2, 1, :], partial_high[:].bitcast(FP32),
                                        ALU.subtract).then_inc(low_ready, 1)
                for e in range(E2):
                    dve.wait_ge(summed, e + 1)
                    if e >= 1:
                        dve.wait_ge(product_done, e)
                    nc.vector.scalar_tensor_tensor(out=product[:], in0=ps[:, 2 + e % 6, :], scalar=inverse[:, e:e + 1],
                                                   in1=w2[:, e, :], op0=ALU.mult, op1=ALU.mult,
                                                   accum_out=means[:, 0, e:e + 1]).then_inc(product_done, 1)
                dve.wait_ge(product_done, E2)
                nc.vector.tensor_copy(means[:, 1:PER, :], means[:, 0:1, :].to_broadcast([128, PER - 1, E2]))\
                    .then_inc(means_ready, 1)
                dve.wait_ge(means_turned, 1)
                link(nc.vector.tensor_copy(meansT[:], ps[:, 1, 0:128]))
                for j in range(PER):
                    last = nc.vector.tensor_scalar(spread[:, j, :], meansT[:], consts["part"][:, j:j + 1], None,
                                                   ALU.mult)
                last.then_inc(spread_ready, 1)
                for i in range(2 * PARTS):
                    dve.wait_ge(mixed, i + 1)
                    at = tokens[:, 4 * i:4 * i + 4, :]
                    nc.vector.tensor_tensor(at, at, ps[:, 2 + i % 4, :].rearrange("p (t c) -> p t c", c=C),
                                            ALU.add).then_inc(added, 1)


def expert_outputs(nc, slots, outputs, tile_expert, experts, b1_rows, consts, ps):
    with stage(nc, "expert") as (sb, sem):
        xs = sb("xs", [128, 2, GROUPED, C + 1])
        token = sb("token", [128, BODY], UINT32)
        xT = sb("xT", [128, 4, 128])
        own = sb("own", [128, BODY, experts.shape[2]])
        at_w2, at_b1, at_b2 = F, F + FC * C, F + FC * C + FC
        before = sb("before", [128, 2, F])
        hidden = sb("hidden", [128, 4, F])
        y = sb("y", [128, BODY, C])
        loaded = [sem(f"loaded{u}") for u in range(2)]
        stored = [sem(f"stored{r}") for r in range(BODY)]
        token_ready = sem("token_ready")
        bias_turned, bias_ready = sem("bias_turned"), sem("bias_ready")
        turned, xT_ready, own_ready, up_done, before_ready, hidden_ready, down_done, y_ready = (
            sem(n) for n in ("turned", "xT_ready", "own_ready", "up_done", "before_ready", "hidden_ready",
                             "down_done", "y_ready"))
        TURN, UP, DOWN, BIAS = 0, 2, 4, 6

        def inside(s):
            return not isinstance(s, int) or s < S3

        with nc.Block() as block:
            @block.sync
            def _(sp):
                load_slots(sp, slots, xs, loaded, before_ready, S3)

            @block.gpsimd
            def _(pool):
                def step(s, r):
                    pool.wait_ge(y_ready, s + 1)
                    bound = s + TOKENS if isinstance(s, int) else pool.snap(s + TOKENS)
                    nc.gpsimd.indirect_dma_start(
                        out=outputs[:, :], out_offset=bass.IndirectOffsetOnAxis(ap=token[:, r:r + 1], axis=0),
                        in_=y[:, r, :], in_offset=None, bounds_check=bound, oob_is_err=False).then_inc(stored[r], 16)
                slot_loop(pool, S3, step)
                for r in range(BODY):
                    pool.wait_ge(stored[r], 16 * S3 // BODY)

            @block.tensor
            def _(pe):
                def turn(s, r):
                    turn_slots(nc, pe, xs, loaded, xT_ready, turned, consts["ident"], ps, TURN, s, r)

                def down(s, r):
                    pe.wait_ge(hidden_ready, s + 1)
                    if past(s, 2):
                        pe.wait_ge(y_ready, s - 1)
                    for c in range(FC):
                        mm = nc.tensor.matmul(ps[:, DOWN + r % 2, 0:C], hidden[:, r % 4, c * 128:(c + 1) * 128],
                                              own[:, r, at_w2 + c * C:at_w2 + (c + 1) * C],
                                              start=c == 0, stop=c == FC - 1)
                    mm.then_inc(down_done, 1)

                nc.tensor.transpose(ps[:, BIAS, 0:E3 * FC], b1_rows[:], consts["ident"][0:E3 * FC, 0:E3 * FC])\
                    .then_inc(bias_turned, 1)
                turn(0, 0)
                turn(1, 1)

                def step(s, r):
                    if inside(s + 2):
                        turn(s + 2, (r + 2) % BODY)
                    multiply_up(nc, pe, own, BODY, xT, own_ready, xT_ready, before_ready, up_done, ps, UP, s, r)
                    if past(s, 2):
                        down(s - 2, (r - 2) % BODY)
                slot_loop(pe, S3, step)
                down(S3 - 2, BODY - 2)
                down(S3 - 1, BODY - 1)

            @block.scalar
            def _(act):
                def take(s, r):
                    take_turned(nc, act, xT, turned, up_done, xT_ready, ps, TURN, s, r)

                take(0, 0)
                take(1, 1)

                def step(s, r):
                    if inside(s + 2):
                        take(s + 2, (r + 2) % BODY)
                    act.wait_ge(before_ready, s + 1)
                    if past(s, 4):
                        act.wait_ge(down_done, s - 3)
                    nc.scalar.activation(hidden[:, r % 4, :], before[:, r % 2, :], ACT.Gelu).then_inc(hidden_ready, 1)
                slot_loop(act, S3, step)

            @block.vector
            def _(dve):
                def fetch(s, r):
                    fetch_weights(nc, dve, experts, own, BODY, tile_expert, y_ready, own_ready, s, r)

                def finish(s, r):
                    dve.wait_ge(down_done, s + 1)
                    nc.vector.tensor_tensor(y[:, r, :], ps[:, DOWN + r % 2, 0:C],
                                            own[:, r, at_b2:at_b2 + C], ALU.add).then_inc(y_ready, 1)

                dve.wait_ge(bias_turned, 1)
                nc.vector.tensor_copy(experts[:, :, at_b1:at_b2],
                                      ps[:, BIAS, 0:E3 * FC].rearrange("p (e c) -> p e c", c=FC))\
                    .then_inc(bias_ready, 1)
                dve.wait_ge(bias_ready, 1)
                for s in range(3):
                    fetch(s, s)

                def step(s, r):
                    if inside(s + 3):
                        fetch(s + 3, (r + 3) % BODY)
                    dve.wait_ge(up_done, s + 1)
                    if past(s, BODY):
                        dve.wait_ge(stored[r], 2 * s - 2 * r)
                    nc.vector.tensor_copy(token[:, r:r + 1], xs[:, r // GROUPED, r % GROUPED, C:].bitcast(UINT32))\
                        .then_inc(token_ready, 1)
                    dve.wait_ge(token_ready, s + 1)
                    if past(s, 2):
                        dve.wait_ge(hidden_ready, s - 1)
                    nc.vector.tensor_tensor(before[:, r % 2, :].rearrange("p (c n) -> p c n", c=FC),
                                            ps[:, UP + r % 2, :].rearrange("p (c n) -> p c n", c=FC),
                                            own[:, r, at_b1:at_b2, None]
                                            .to_broadcast([128, FC, 128]), ALU.add).then_inc(before_ready, 1)
                    if past(s, 2):
                        finish(s - 2, (r - 2) % BODY)
                slot_loop(dve, S3, step)
                finish(S3 - 2, BODY - 2)
                finish(S3 - 1, BODY - 1)


def add_outputs(nc, outputs, weight, tokens, gathered, out_dram, consts, ps):
    with stage(nc, "last") as (sb, sem):

        result = sb("result", [128, 8, 512])
        arrived = [sem(f"arrived{g}") for g in range(8)]
        scaled, added, turned, taken, stored = (sem(n) for n in ("scaled", "added", "turned", "taken", "stored"))
        with nc.Block() as block:
            @block.vector
            def _(dve):
                for g in range(8):
                    at = slice(4 * g, 4 * g + 4)
                    dve.wait_ge(arrived[g], 16)
                    nc.vector.tensor_tensor(gathered[:, at, :], gathered[:, at, :],
                                            weight[:, at, None].to_broadcast([128, 4, C]), ALU.mult).then_inc(scaled, 1)
                    dve.wait_ge(scaled, g + 1)
                    nc.vector.tensor_tensor(tokens[:, at, :], tokens[:, at, :], gathered[:, at, :],
                                            ALU.add).then_inc(added, 1)

            @block.tensor
            def _(pe):
                for g in range(8):
                    pe.wait_ge(added, g + 1)
                    if g >= 2:
                        pe.wait_ge(taken, g - 1)
                    for a in range(4):
                        mm = nc.tensor.transpose(ps[:, g % 2, a * 128:(a + 1) * 128], tokens[:, 4 * g + a, :],
                                                 consts["ident"][:])
                    mm.then_inc(turned, 1)

            @block.scalar
            def _(act):
                for g in range(8):
                    act.wait_ge(turned, g + 1)
                    nc.scalar.activation(result[:, g, :], ps[:, g % 2, :], ACT.Copy).then_inc(taken, 1)

            @block.sync
            def _(sp):
                for g in range(8):
                    sp.dma_start(gathered[:, 4 * g:4 * g + 4, :],
                                 outputs[512 * g:512 * g + 512, :].rearrange("(a p) c -> p a c", p=128))\
                        .then_inc(arrived[g], 16)
                for g in range(8):
                    sp.wait_ge(taken, g + 1)
                    sp.dma_start(out_dram[2 * g:2 * g + 2].rearrange("b c h w -> c b (h w)"),
                                 result[:, g, :].rearrange("p (b n) -> p b n", b=2)).then_inc(stored, 16)
                sp.wait_ge(stored, 16 * 8)


CONSTS = {"ident": 128, "group": 128, "before": 128, "ones": 128, "causal": 3 * 128, "index": E2, "row": 1,
          "token": TILES, "tile": S2, "part": 128 // E2}


def build(nc, a, out):
    with ExitStack() as ctx:
        def sb(name, shape, dt=FP32, into=ctx):
            return into.enter_context(nc.sbuf_tensor(name, shape, dt))

        def sem(name):
            return ctx.enter_context(nc.semaphore(name))

        ps = ctx.enter_context(nc.psum_tensor("ps", [128, 8, 512], FP32))
        tokens = sb("tokens", [128, TILES, C])
        xf = sb("xf", [128, TOKENS])
        rows = sb("rows", [128, TILES, C + 1])
        normed = rows[:, :, 0:C]

        const_all = sb("const_all", [128, sum(width for width in CONSTS.values())])
        consts, at = {}, 0
        for k, width in CONSTS.items():
            consts[k] = const_all[:, at:at + width]
            at += width
        ident16 = sb("ident16", [128, 128], BF16)
        window = sb("window", [128, 2, 3 * 128], BF16)
        spread_rows = sb("spread_rows", [128, 4, 4, 128], FP32R)
        pick = sb("pick", [128, 4, 128], FP32R)

        first = {"wq_r": (a["L0_conv_wq_r"].rearrange("(c o) -> c o", o=1), [C, 1]),
                 "wv_r": (a["L0_conv_wv_r"], [C2, C]), "w_up": (a["L0_conv_w_up"], [C, C2]),
                 "wq_l": (a["L0_conv_wq_l"], [C2, C]), "wv_l": (a["L0_conv_wv_l"], [C2, C])}
        w = {k: sb(f"w_{k}", shape) for k, (_, shape) in first.items()}
        wqk = [sb(f"wqk{i}", [C, 2, 128]) for i in range(3)]
        wv = [sb(f"wv{i}", [C, 128]) for i in range(3)]
        wo = [sb(f"wo{i}", [128, C]) for i in range(3)]
        q_bias = sb("q_bias", [128, 2])
        v_bias = sb("v_bias", [128, 128])
        o_bias = sb("o_bias", [128, 2, C])
        gate2 = sb("gate2", [C, E2])
        gate3 = sb("gate3", [C, E3])
        gate3_bias = sb("gate3_bias", [128, E3])
        position = sb("position", [128, K2, TILES], UINT32)
        tile_expert = sb("tile_expert", [128, S2], INT32)
        tile_choice = sb("tile_choice", [128, E2])
        partial = sb("partial", [128, S2, FC])
        weight2 = sb("weight2", [128, TILES, E2])
        weight3 = sb("weight3", [128, TILES])
        inverse = sb("inverse", [128, E2])

        slots = nc.dram_tensor("slots", (S2 * 128, C), FP32, kind="Internal").ap()
        slots3 = nc.dram_tensor("slots3", (S3 * 128, C + 1), FP32, kind="Internal").ap()
        outputs = nc.dram_tensor("outputs", (TOKENS, C), FP32, kind="Internal").ap()

        consts_in = sem("consts_in")
        raw_in = sem("raw_in")
        experts_in = sem("experts_in")
        last_in = sem("last_in")

        experts2 = ctx.enter_context(ExitStack())
        w1_raw = sb("w1_raw", [128, E2 * FC, C], into=experts2)
        w2 = sb("w2", [128, E2, F], into=experts2)

        first_input = ctx.enter_context(ExitStack())
        x = sb("x", [128, IMAGES, N], into=first_input)
        x_in = [sem(f"x_in{i}") for i in range(4)]

        with ExitStack() as prep:
            prep_widths = (2 * 3 * 128, 4 * 4 * 128, 4)
            const_prep = sb("const_prep", [128, sum(prep_widths)], into=prep)
            window32 = const_prep[:, 0:prep_widths[0]]
            spread32 = const_prep[:, prep_widths[0]:sum(prep_widths[0:2])]
            pick32 = const_prep[:, sum(prep_widths[0:2]):]
            raw_fc = sb("raw_fc", [128, 3, C], into=prep)
            raw = sb("raw", [128, 5, C], into=prep)
            raw_gate = sb("raw_gate", [E2, C], into=prep)
            fc_bias = sb("fc_bias", [1, 3 * 128], into=prep)
            fcT = sb("fcT", [C, 3 * 128], into=prep)
            wide_bias = sb("wide_bias", [1, 2 * 128], into=prep)
            turned, copied, biased = sem("turned"), sem("copied"), sem("biased")
            with nc.Block() as block:
                @block.sync
                def _(sp):
                    sp.dma_start(const_all[:], a["const_all"]).then_inc(consts_in, 16)
                    sp.dma_start(const_prep[:], a["const_prep"]).then_inc(raw_in, 16)
                    for k, (source, _) in first.items():
                        sp.dma_start(w[k][:], source).then_inc(consts_in, 16)
                    sp.dma_start(raw_fc[:], a["L1_conv_W_fc"].rearrange("(t p) c -> p t c", p=128)).then_inc(raw_in, 16)
                    sp.dma_start(raw[:, 0, :], a["L1_conv_W_last"]).then_inc(raw_in, 16)
                    for i, k in enumerate(("Wq", "Wk", "Wv", "Wo")):
                        sp.dma_start(raw[:, 1 + i, :], a[f"L2_attn_{k}"]).then_inc(raw_in, 16)
                    for i, k in enumerate(("Wq", "Wk")):
                        sp.dma_start(wqk[2][:, i, :], a[f"L3_attn_{k}"]).then_inc(raw_in, 16)
                    sp.dma_start(wv[2][:], a["L3_attn_Wv"]).then_inc(raw_in, 16)
                    sp.dma_start(wo[2][:], a["L3_attn_Wo"]).then_inc(raw_in, 16)
                    sp.dma_start(raw_gate[:], a["L2_ffn_gate_weight"]).then_inc(raw_in, 16)
                    sp.dma_start(gate3[:], a["L3_ffn_Ws"]).then_inc(raw_in, 16)
                    sp.dma_start(fc_bias[:], a["L1_conv_b_fc"].rearrange("(o n) -> o n", o=1)).then_inc(raw_in, 16)
                    for i, k in enumerate(("L1_conv_b_last", "L3_attn_bo")):
                        sp.dma_start(o_bias[:, i, :], a[k].rearrange("(o n) -> o n", o=1).to_broadcast([128, C]))\
                            .then_inc(raw_in, 16)
                    sp.dma_start(gate3_bias[:], a["L3_ffn_bs"].rearrange("(o n) -> o n", o=1).to_broadcast([128, E3]))\
                        .then_inc(raw_in, 16)
                    for i in range(4):
                        sp.dma_start(x[:, 4 * i:4 * i + 4, :],
                                     a["x"][4 * i:4 * i + 4].rearrange("b c h w -> c b (h w)")).then_inc(x_in[i], 16)
                    sp.dma_start(w1_raw[:], a["L2_ffn_w1"].rearrange("e (k p) d -> p (e k) d", p=128))\
                        .then_inc(experts_in, 16)
                    sp.dma_start(w2[:], a["L2_ffn_w2"].rearrange("e d f -> d e f")).then_inc(experts_in, 16)
                    sp.wait_ge(consts_in, 16 * (1 + len(first)))
                    sp.wait_ge(raw_in, 16 * 17)

                @block.tensor
                def _(pe):
                    pe.wait_ge(consts_in, 16 * (1 + len(first)))
                    pe.wait_ge(raw_in, 16 * 17)
                    for t in range(3):
                        nc.tensor.transpose(ps[:, 0, t * 128:(t + 1) * 128], raw_fc[:, t, :], consts["ident"][:])
                    for i in range(4):
                        nc.tensor.transpose(ps[:, 1, i * 128:(i + 1) * 128], raw[:, i, :], consts["ident"][:])
                    nc.tensor.transpose(ps[:, 2, 0:128], raw[:, 4, :], consts["ident"][:])
                    nc.tensor.transpose(ps[:, 3, 0:E2], raw_gate[:], consts["ident"][0:E2, 0:E2]).then_inc(turned, 1)
                    pe.wait_ge(biased, 1)
                    for g in range(2):
                        nc.tensor.matmul(ps[:, 4, g:g + 1], wide_bias[:, g * 128:(g + 1) * 128],
                                         consts["ones"][0:1, 0:1], start=True, stop=True)
                    mm = nc.tensor.matmul(ps[:, 5, 0:128], consts["ones"][0:1, 0:128],
                                          fc_bias[:].rearrange("o (h t d) -> o t h d", h=H, t=3)[:, 2],
                                          start=True, stop=True)
                    mm.then_inc(turned, 1)

                @block.vector
                def _(dve):
                    dve.wait_ge(turned, 1)
                    nc.vector.tensor_copy(ident16[:], consts["ident"][:])
                    nc.vector.tensor_copy(window[:].rearrange("p i n -> p (i n)"), window32)
                    nc.vector.tensor_copy(spread_rows[:].rearrange("p i g n -> p (i g n)"), spread32)
                    nc.vector.tensor_copy(rows[:, :, C:C + 1].bitcast(UINT32), consts["token"][:, :, None])
                    nc.vector.tensor_copy(pick[:], pick32[:, :, None].to_broadcast([128, 4, 128]))
                    nc.vector.tensor_copy(fcT[:], ps[:, 0, 0:384]).then_inc(copied, 1)
                    nc.vector.tensor_copy(wo[0][:], ps[:, 1, 0:128])
                    nc.vector.tensor_copy(wv[1][:], ps[:, 1, 384:512])
                    nc.vector.tensor_copy(wo[1][:], ps[:, 2, 0:128])
                    nc.vector.tensor_copy(gate2[:], ps[:, 3, 0:E2])
                    dve.wait_ge(copied, 1)
                    fc = fcT[:].rearrange("p (h t d) -> p t h d", h=H, t=3)
                    bias = fc_bias[:].rearrange("p (h t d) -> p t h d", h=H, t=3)
                    scale = float(D) ** -0.5
                    nc.vector.tensor_scalar(wqk[0][:, 0, :].rearrange("p (h d) -> p h d", h=H), fc[:, 0], scale,
                                            None, ALU.mult)
                    nc.vector.tensor_copy(wqk[0][:, 1, :].rearrange("p (h d) -> p h d", h=H), fc[:, 1])
                    nc.vector.tensor_copy(wv[0][:].rearrange("p (h d) -> p h d", h=H), fc[:, 2])
                    nc.vector.tensor_scalar(wqk[1][:, 0, :], ps[:, 1, 128:256], scale, None, ALU.mult)
                    nc.vector.tensor_copy(wqk[1][:, 1, :], ps[:, 1, 256:384])
                    nc.vector.tensor_scalar(wide_bias[:, 0:128].rearrange("p (h d) -> p h d", h=H), bias[:, 0], scale,
                                            None, ALU.mult)
                    nc.vector.tensor_copy(wide_bias[:, 128:256].rearrange("p (h d) -> p h d", h=H), bias[:, 1])\
                        .then_inc(biased, 1)
                    dve.wait_ge(turned, 2)
                    nc.vector.tensor_copy(q_bias[:], ps[:, 4, 0:2])
                    nc.vector.tensor_copy(v_bias[:], ps[:, 5, 0:128])

        ident = consts["ident"]
        masks = {"ident": ident16, "rows": window[:, 0], "columns": window[:, 1], "keep": consts["causal"]}
        weights = [{"qk": wqk[i], "v": wv[i], "o": wo[i]} for i in range(3)]

        spatial_gate(nc, x, x_in, w, xf, tokens, consts, ps)
        first_input.close()
        attention(nc, "softmax", xf, tokens, weights[0], ident, q_bias, v_bias, o_bias[:, 0, :], spread_rows, pick,
                  masks, ps)
        layer_norm(nc, "norm0", tokens, normed, xf, ident, ps)
        attention(nc, "window", xf, tokens, weights[1], ident, None, None, None, spread_rows, pick, masks, ps)
        layer_norm(nc, "norm1", tokens, normed, None, ident, ps, gate2)
        with ExitStack() as turning:
            w1T = sb("w1T", [128, E2, F], into=turning)
            route(nc, "route2", E2, K2, S2, None, consts, normed, slots, position, tile_expert, weight2, inverse,
                  tile_choice, ps, beside=turn_experts(nc, w1_raw, w1T, experts_in, ident, ps))
            expert_sums(nc, slots, tile_expert, w1T, partial, consts, ps)
            mix_means(nc, partial, tile_choice, w2, inverse, weight2, tokens, consts, ps)
        experts2.close()

        experts3 = sb("experts3", [128, E3, F + FC * C + FC + C])
        b1_rows = sb("b1_rows", [E3 * FC, 128])
        with nc.Block() as block:
            @block.sync
            def _(sp):
                sp.dma_start(experts3[:, :, 0:F], a["L3_ffn_W1"].rearrange("e d f -> d e f")).then_inc(last_in, 16)
                for k in range(FC):
                    at = F + k * C
                    sp.dma_start(experts3[:, :, at:at + C],
                                 a["L3_ffn_W2"][:, k * 128:(k + 1) * 128, :].rearrange("e p d -> p e d"))\
                        .then_inc(last_in, 16)
                sp.dma_start(b1_rows[:], a["L3_ffn_b1"].rearrange("e (k p) -> (e k) p", p=128)).then_inc(last_in, 16)
                sp.dma_start(experts3[:, :, F + FC * C + FC:],
                             a["L3_ffn_b2"].rearrange("(o e) n -> o e n", o=1).to_broadcast([128, E3, C]))\
                    .then_inc(last_in, 16)
        layer_norm(nc, "norm2", tokens, normed, xf, ident, ps)
        attention(nc, "linear", xf, tokens, weights[2], ident, None, None, o_bias[:, 1, :], spread_rows, pick,
                  masks, ps)
        layer_norm(nc, "norm3", tokens, normed, None, ident, ps, gate3)
        route(nc, "route3", E3, K3, S3, gate3_bias, consts, rows, slots3, position, tile_expert[:, 0:S3], weight3, None,
              None, ps)
        with nc.Block() as block:
            @block.sync
            def _(sp):
                sp.wait_ge(last_in, 16 * (FC + 3))
        expert_outputs(nc, slots3, outputs, tile_expert, experts3, b1_rows, consts, ps)
        add_outputs(nc, outputs, weight3, tokens, normed, out, consts, ps)


def constants():
    import numpy as np

    p = np.arange(128)[:, None]
    row, column = np.arange(128)[:, None], np.arange(N)[None]
    by_query = [row + 128 * i - column for i in range(2)]
    by_key = [column - (row + 128 * i) for i in range(2)]

    def blocks(first, second):
        return np.concatenate([first, second], 1)

    def seen(d):
        return np.where((d >= 0) & (d < WINDOW), 0, MASKED)

    p3, column3 = np.arange(128)[:, None, None], np.arange(128)[None, None]
    pair = np.arange(4)[None, :, None]
    same = (p3 // 16 == 2 * pair + column3 // 64) & (p3 % 16 == column3 % 16)
    time = column3 % 64 // 16
    spread = np.stack([same & (time % 2 == 0), same & (time % 2 == 1),
                       same & (time // 2 == 0), same & (time // 2 == 1)], 1)
    arrays = {
        "ident": np.eye(128, dtype=np.float32),
        "group": (p // GROUP == p.T // GROUP).astype(np.float32) / GROUP,
        "before": (p < p.T).astype(np.float32),
        "ones": np.ones((128, 128), np.float32),
        "window": blocks(blocks(seen(by_query[0])[:, 0:128], seen(by_query[1])),
                         blocks(seen(by_key[0]), seen(by_key[1])[:, 128:])).astype(np.float32),
        "causal": blocks(by_key[0] >= 0, by_key[1][:, 128:] >= 0).astype(np.float32),
        "spread": spread.reshape(128, 16 * 128).astype(np.float32),
        "pick": ((p % 64 < 8) & (p % 4 == np.arange(4)[None])).astype(np.float32),
        "index": np.tile(np.arange(E2, dtype=np.float32) - E2, (128, 1)),
        "row": p.astype(np.float32),
        "token": (p + 128 * np.arange(TILES)[None]).astype(np.float32),
        "tile": np.tile(np.arange(S2, dtype=np.float32), (128, 1)),
        "part": (p // E2 == np.arange(128 // E2)[None]).astype(np.float32),
    }
    prep = [arrays.pop(k) for k in ("window", "spread", "pick")]
    return {"all": np.concatenate([arrays[k] for k in CONSTS], 1), "prep": np.concatenate(prep, 1)}


def kernel(**inputs):
    import numpy as np
    import concourse.bacc as bacc
    from concourse.bass_utils import run_bass_kernel_spmd

    nc = bacc.Bacc("TRN2", target_bir_lowering=False, num_devices=1)
    given = {k: np.ascontiguousarray(v) for k, v in inputs.items()}
    given.update({f"const_{k}": v for k, v in constants().items()})
    arrays, tensors = {}, {}
    for name, value in given.items():
        arrays[f"in_{name}"] = value
        tensors[name] = nc.dram_tensor(f"in_{name}", value.shape, mybir.dt.from_np(value.dtype),
                                       kind="ExternalInput").ap()
    out = nc.dram_tensor("out", (IMAGES, C, 16, 16), FP32, kind="ExternalOutput").ap()
    build(nc, tensors, out)
    result = run_bass_kernel_spmd(nc, [arrays], core_ids=[0])
    return result.results[0]["out"]
```
